# Optimizing a Trainium2 kernel written in Bass

```python
import numpy as np
import jax
import jax.numpy as jnp

def _softmax(x, axis=-1):
    return jax.nn.softmax(x, axis=axis)

def _gelu(x):
    return jax.nn.gelu(x, approximate=True)

def _silu(x):
    return jax.nn.silu(x)

def _sigmoid(x):
    return jax.nn.sigmoid(x)

def _layernorm(x, axis=-1, eps=1e-05):
    m = jnp.mean(x, axis=axis, keepdims=True)
    v = jnp.var(x, axis=axis, keepdims=True)
    return (x - m) / jnp.sqrt(v + eps)

def _scatter_add(tgt, idx, src, axis=0):
    return tgt.at[idx].add(src)

def _segment_sum(src, seg, n):
    return jax.ops.segment_sum(src, seg, n)
kernel_name = 'mk_perceiver_d1_seqx_r2_905a87'

def setup_inputs(seed: int=0):
    np.random.seed(seed)
    _w = jnp.asarray

    def _rec_inputs():
        import jax
        import jax.numpy as jnp
        _rk = jax.random.key(seed)
        x = -0.0003929 + 0.9999 * jax.random.normal(jax.random.fold_in(_rk, 1), (16, 128, 512), jnp.float32)
        _lenS = 128 - jax.random.randint(jax.random.fold_in(_rk, 7), (16,), 0, max(1, 128 // 4) + 1, jnp.int32)
        _lenS2 = 2048 - jax.random.randint(jax.random.fold_in(_rk, 8), (16,), 0, max(1, 2048 // 4) + 1, jnp.int32)
        _ctx_1024P = jax.random.normal(jax.random.fold_in(_rk, 11), (16, 16, 512), jnp.float32)
        _ctx_1024c = jax.random.dirichlet(jax.random.fold_in(_rk, 511), 0.3 * jnp.ones((16,), jnp.float32), (16, 2048))
        _ctx_1024t = jnp.einsum('bsk,bkd->bsd', _ctx_1024c, _ctx_1024P)
        _ctx_1024t = _ctx_1024t * jax.lax.rsqrt(jnp.mean(jnp.square(_ctx_1024t)) + 1e-12) * 0.953939
        ctx_1024 = -1.39393e-06 + 0.999914 * (_ctx_1024t + 0.3 * jax.random.normal(jax.random.fold_in(_rk, 611), (16, 2048, 512), jnp.float32))
        return (x, ctx_1024)
    x, ctx_1024 = _rec_inputs()

    def _L0_xattn_setup():
        import jax, jax.numpy as jnp
        import numpy as np
        B, C_LEN, Q_LEN, D = (8, 1024, 256, 512)
        key = jax.random.key(seed)
        ks = jax.random.split(key, 10)
        scale = 1.0 / np.sqrt(D)
        return {'c': jax.random.normal(ks[0], (B, C_LEN, D), dtype=jnp.float32), 'q': jax.random.normal(ks[1], (B, Q_LEN, D), dtype=jnp.float32), 'w_cq': jax.random.normal(ks[2], (D,), dtype=jnp.float32) * scale, 'b_cq': jax.random.normal(ks[3], (), dtype=jnp.float32) * scale, 'w_c': jax.random.normal(ks[4], (D,), dtype=jnp.float32) * scale, 'b_c': jax.random.normal(ks[5], (), dtype=jnp.float32) * scale, 'w_q': jax.random.normal(ks[6], (D,), dtype=jnp.float32) * scale, 'b_q': jax.random.normal(ks[7], (), dtype=jnp.float32) * scale, 'W_l': jax.random.normal(ks[8], (D, 4 * D), dtype=jnp.float32) * (1.0 / np.sqrt(4 * D)), 'b_l': jax.random.normal(ks[9], (D,), dtype=jnp.float32) * (1.0 / np.sqrt(4 * D))}
    _L0_xattn_all = _L0_xattn_setup()
    _L0_xattn_in = {k: v for k, v in _L0_xattn_all.items() if k in ('w_cq', 'b_cq', 'w_c', 'b_c', 'w_q', 'b_q', 'W_l', 'b_l')}
    del _L0_xattn_all

    def _L0_attn_setup():
        import jax, jax.numpy as jnp
        import numpy as np
        N_HEADS = 16
        EMBED_DIM = 512
        HEAD_DIM = EMBED_DIM // N_HEADS
        B, S = (4, 1024)
        key = jax.random.key(seed)
        k1, k2, k3, k4 = jax.random.split(key, 4)
        scale = 1.0 / np.sqrt(EMBED_DIM)
        x = jax.random.normal(k1, (B, S, EMBED_DIM), dtype=jnp.float32)
        Wq = jax.random.normal(k2, (EMBED_DIM, EMBED_DIM), dtype=jnp.float32) * scale
        Wk = jax.random.normal(k3, (EMBED_DIM, EMBED_DIM), dtype=jnp.float32) * scale
        Wv = jax.random.normal(k4, (EMBED_DIM, EMBED_DIM), dtype=jnp.float32) * scale
        return {'x': x, 'Wq': Wq, 'Wk': Wk, 'Wv': Wv}
    _L0_attn_all = _L0_attn_setup()
    _L0_attn_in = {k: v for k, v in _L0_attn_all.items() if k in ('Wq', 'Wk', 'Wv')}
    del _L0_attn_all

    def _L0_ffn_setup():
        import jax, jax.numpy as jnp
        import numpy as np
        TOP_K = 4
        CAP_FACTOR = 4

        def swiglu(x, w1, w2, w3):
            return jax.nn.silu(x @ w1) * (x @ w3) @ w2
        key = jax.random.key(seed)
        ks = jax.random.split(key, 8)
        B, S, D, H, E = (2, 1024, 512, 256, 32)
        Hs = 2 * H
        sd = lambda *sh: 1.0 / np.sqrt(sh[-2])
        x = jax.random.normal(ks[0], (B, S, D), dtype=jnp.float32)
        Wg = jax.random.normal(ks[1], (D, E), dtype=jnp.float32) * (1.0 / np.sqrt(D))
        W1 = jax.random.normal(ks[2], (E, D, H), dtype=jnp.float32) * (1.0 / np.sqrt(D))
        W3 = jax.random.normal(ks[3], (E, D, H), dtype=jnp.float32) * (1.0 / np.sqrt(D))
        W2 = jax.random.normal(ks[4], (E, H, D), dtype=jnp.float32) * (1.0 / np.sqrt(H))
        Ws1 = jax.random.normal(ks[5], (D, Hs), dtype=jnp.float32) * (1.0 / np.sqrt(D))
        Ws3 = jax.random.normal(ks[6], (D, Hs), dtype=jnp.float32) * (1.0 / np.sqrt(D))
        Ws2 = jax.random.normal(ks[7], (Hs, D), dtype=jnp.float32) * (1.0 / np.sqrt(Hs))
        return {'x': x, 'Wg': Wg, 'W1': W1, 'W2': W2, 'W3': W3, 'Ws1': Ws1, 'Ws2': Ws2, 'Ws3': Ws3}
    _L0_ffn_all = _L0_ffn_setup()
    _L0_ffn_in = {k: v for k, v in _L0_ffn_all.items() if k in ('Wg', 'W1', 'W2', 'W3', 'Ws1', 'Ws2', 'Ws3')}
    del _L0_ffn_all
    return {'x': x, 'ctx_1024': ctx_1024, 'L0_xattn_w_cq': _L0_xattn_in['w_cq'], 'L0_xattn_b_cq': _L0_xattn_in['b_cq'], 'L0_xattn_w_c': _L0_xattn_in['w_c'], 'L0_xattn_b_c': _L0_xattn_in['b_c'], 'L0_xattn_w_q': _L0_xattn_in['w_q'], 'L0_xattn_b_q': _L0_xattn_in['b_q'], 'L0_xattn_W_l': _L0_xattn_in['W_l'], 'L0_xattn_b_l': _L0_xattn_in['b_l'], 'L0_attn_Wq': _L0_attn_in['Wq'], 'L0_attn_Wk': _L0_attn_in['Wk'], 'L0_attn_Wv': _L0_attn_in['Wv'], 'L0_ffn_Wg': _L0_ffn_in['Wg'], 'L0_ffn_W1': _L0_ffn_in['W1'], 'L0_ffn_W2': _L0_ffn_in['W2'], 'L0_ffn_W3': _L0_ffn_in['W3'], 'L0_ffn_Ws1': _L0_ffn_in['Ws1'], 'L0_ffn_Ws2': _L0_ffn_in['Ws2'], 'L0_ffn_Ws3': _L0_ffn_in['Ws3']}

def reference(x, ctx_1024, L0_xattn_w_cq, L0_xattn_b_cq, L0_xattn_w_c, L0_xattn_b_c, L0_xattn_w_q, L0_xattn_b_q, L0_xattn_W_l, L0_xattn_b_l, L0_attn_Wq, L0_attn_Wk, L0_attn_Wv, L0_ffn_Wg, L0_ffn_W1, L0_ffn_W2, L0_ffn_W3, L0_ffn_Ws1, L0_ffn_Ws2, L0_ffn_Ws3):
    import jax
    import jax.numpy as jnp

    def _L0_xattn_ref(c, q, w_cq, b_cq, w_c, b_c, w_q, b_q, W_l, b_l):
        import jax, jax.numpy as jnp
        import numpy as np
        B, C_LEN, Q_LEN, D = (8, 1024, 256, 512)
        cq = jnp.einsum('bcd,bqd,d->bcq', c, q, w_cq) + b_cq
        s = (c @ w_c + b_c)[:, :, None] + (q @ w_q + b_q)[:, None, :] + cq
        a = jax.nn.softmax(s, axis=2)
        c2q_att = jnp.einsum('bcq,bqd->bcd', a, q)
        b_att = jax.nn.softmax(jnp.max(s, axis=2), axis=1)
        q2c_att = jnp.einsum('bc,bcd->bd', b_att, c)[:, None, :]
        x = jnp.concatenate([c, c2q_att, c * c2q_att, c * q2c_att], axis=-1)
        z = x @ W_l.T + b_l
        return z

    def _L0_attn_ref(x, Wq, Wk, Wv):
        import jax, jax.numpy as jnp
        import numpy as np
        N_HEADS = 16
        EMBED_DIM = 512
        HEAD_DIM = EMBED_DIM // N_HEADS
        B, S = (4, 1024)
        b, s, d = x.shape

        def proj(W):
            return (x @ W.T).reshape(b, s, N_HEADS, HEAD_DIM).transpose(0, 2, 1, 3)
        q, k, v = (proj(Wq), proj(Wk), proj(Wv))
        scores = jnp.einsum('bhqd,bhkd->bhqk', q, k) / jnp.sqrt(jnp.float32(d))
        attn = jax.nn.softmax(scores, axis=-1)
        out = jnp.einsum('bhqk,bhkd->bhqd', attn, v)
        return out.transpose(0, 2, 1, 3).reshape(b, s, d)

    def _L0_ffn_ref(x, Wg, W1, W2, W3, Ws1, Ws2, Ws3):
        import jax, jax.numpy as jnp
        import numpy as np
        TOP_K = 4
        CAP_FACTOR = 4

        def swiglu(x, w1, w2, w3):
            return jax.nn.silu(x @ w1) * (x @ w3) @ w2
        B, S, D = x.shape
        E = Wg.shape[1]
        T = B * S
        xf = x.reshape(T, D)
        scores = jax.nn.softmax(xf @ Wg, axis=-1)
        weights, indices = jax.lax.top_k(scores, TOP_K)
        P = T * TOP_K
        pair_expert = indices.reshape(-1)
        pair_token = jnp.repeat(jnp.arange(T), TOP_K)
        pair_weight = weights.reshape(-1).astype(xf.dtype)
        C = CAP_FACTOR * P // E
        y = jnp.zeros_like(xf)
        for e in range(E):
            pos = jnp.nonzero(pair_expert == e, size=C, fill_value=P)[0]
            valid = pos < P
            safe = jnp.minimum(pos, P - 1)
            tok = jnp.where(valid, pair_token[safe], 0)
            w = jnp.where(valid, pair_weight[safe], 0.0)
            xg = xf[tok]
            out = swiglu(xg, W1[e], W2[e], W3[e]) * w[:, None]
            y = y.at[tok].add(out)
        z = swiglu(xf, Ws1, Ws2, Ws3)
        return (y + z).reshape(B, S, D)
    x = x + _L0_xattn_ref(_layernorm(x, axis=-1), ctx_1024, L0_xattn_w_cq, L0_xattn_b_cq, L0_xattn_w_c, L0_xattn_b_c, L0_xattn_w_q, L0_xattn_b_q, L0_xattn_W_l, L0_xattn_b_l)
    x = x + _L0_attn_ref(_layernorm(x, axis=-1), L0_attn_Wq, L0_attn_Wk, L0_attn_Wv)
    x = x + _L0_ffn_ref(_layernorm(x, axis=-1), L0_ffn_Wg, L0_ffn_W1, L0_ffn_W2, L0_ffn_W3, L0_ffn_Ws1, L0_ffn_Ws2, L0_ffn_Ws3)
    return x

_drawn_inputs = setup_inputs


def setup_inputs(seed=0):
    import zlib

    import numpy as np

    out = dict(_drawn_inputs(seed))
    spreads = {}
    factors = {}
    for name, (base, spread) in spreads.items():
        noise = np.random.default_rng([zlib.crc32(name.encode()), seed]).standard_normal(out[name].shape)
        drawn = base * np.exp(spread * noise) if base else spread * noise
        out[name] = jnp.asarray(drawn.astype(out[name].dtype))
    for name, factor in factors.items():
        out[name] = (out[name] * factor).astype(out[name].dtype)
    return out
```

```python
from contextlib import ExitStack

import concourse.bass as bass
from concourse import mybir

ALU = mybir.AluOpType
ACT = mybir.ActivationFunctionType
AX = mybir.AxisListType
F32 = mybir.dt.float32
F32R = mybir.dt.float32r
I32 = mybir.dt.int32
U32 = mybir.dt.uint32
MAX_OVER_PARTITIONS = bass.bass_isa.ReduceOp.max

P = 128
B = 16
D = 512
KD = D // P
CTX = 2048
BANK = 512
EPS = 1e-5


class Tally:

    def __init__(self, sem, per, credit=0):
        self.sem, self.per, self.credit = sem, per, credit

    def value(self, batch, k):
        return batch * self.per + (self.credit + k)


def grant(eng, *tallies):
    for t in tallies:
        if t.credit:
            eng.sem_inc(t.sem, t.credit)


class Memory:

    def __init__(self, nc, stack, phase):
        self.nc, self.stack, self.phase = nc, stack, phase

    def sb(self, name, shape, dt=F32):
        return self.stack.enter_context(self.nc.sbuf_tensor(f"{self.phase}_{name}", shape, dt))

    def ps(self, name, shape):
        return self.stack.enter_context(self.nc.psum_tensor(f"{self.phase}_{name}", shape, F32))

    def sem(self, name):
        return self.stack.enter_context(self.nc.semaphore(f"{self.phase}_{name}"))

    def tally(self, name, per, credit=0):
        return Tally(self.sem(name), per, credit)


def product(nc, out, stationary, moving, first, last):
    (sh, sl), (mh, ml) = stationary, moving
    nc.tensor.matmul(out, sh, mh, start=first, stop=False)
    nc.tensor.matmul(out, sh, ml, start=False, stop=False)
    return nc.tensor.matmul(out, sl, mh, start=False, stop=last)


def cross_attention(nc, x, ctx_rows, ctx_cols, w_cq, w_c, w_q, b_cq, b_c, b_q, W_lT, b_l, ident_in, x1_out):
    QC = CTX // BANK
    RC = 8
    NJ = CTX // RC // P
    RING = 4
    KZ = 4 * KD

    with ExitStack() as stack:
        m = Memory(nc, stack, "xa")
        wl_hi = m.sb("wl_hi", [P, KZ, D], F32R)
        wl_lo = m.sb("wl_lo", [P, KZ, D], F32R)
        ident = m.sb("ident", [P, P])
        ones = m.sb("ones", [P, P])
        w_c_rows = m.sb("w_c_rows", [P, D])
        b_l_rows = m.sb("b_l_rows", [P, D])
        w_cq_col = m.sb("w_cq_col", [P, KD])
        w_q_col = m.sb("w_q_col", [P, KD])
        biases = m.sb("biases", [P, 3])
        bias_sum = m.sb("bias_sum", [P, 1])
        cols_raw = m.sb("cols_raw", [P, 2, KD * BANK])
        cols_hi = m.sb("cols_hi", [P, 2, KD, BANK], F32R)
        cols_lo = m.sb("cols_lo", [P, 2, KD, BANK], F32R)
        rows_raw = m.sb("rows_raw", [P, 2, NJ * D])
        rows_hi = m.sb("rows_hi", [P, RING, NJ, D], F32R)
        rows_lo = m.sb("rows_lo", [P, RING, NJ, D], F32R)
        x_in = m.sb("x_in", [P, D])
        x_bias = m.sb("x_bias", [P, D])
        c = m.sb("c", [P, D])
        stats = m.sb("stats", [P, 6])
        mean_var = m.sb("mean_var", [P, 2])
        eps_pow = m.sb("eps_pow", [P, 2])
        var_eps = m.sb("var_eps", [P, 1])
        rstd = m.sb("rstd", [P, 1])
        row_dot = m.sb("row_dot", [P, 1])
        cT = m.sb("cT", [P, D])
        cT_held = m.sb("cT_held", [P, D])
        cT_hi = m.sb("cT_hi", [P, D], F32R)
        cT_lo = m.sb("cT_lo", [P, D], F32R)
        cw = m.sb("cw", [P, D])
        cw_hi = m.sb("cw_hi", [P, D], F32R)
        cw_lo = m.sb("cw_lo", [P, D], F32R)
        chunk_max = m.sb("chunk_max", [P, QC])
        neg_max = m.sb("neg_max", [P, 1])
        probs = m.sb("probs", [P, CTX])
        chunk_sum = m.sb("chunk_sum", [P, QC])
        row_sum = m.sb("row_sum", [P, 1])
        row_inv = m.sb("row_inv", [P, 1])
        tok_max = m.sb("tok_max", [P, 1])
        all_max = m.sb("all_max", [P, 1])
        tok_exp = m.sb("tok_exp", [P, 1])
        tok_inv = m.sb("tok_inv", [P, 1])
        q2c = m.sb("q2c", [P, KD])
        probsT_hi = m.sb("probsT_hi", [P, 2, BANK], F32R)
        probsT_lo = m.sb("probsT_lo", [P, 2, BANK], F32R)
        cq2c = m.sb("cq2c", [P, D])
        cq2c_hi = m.sb("cq2c_hi", [P, D], F32R)
        cq2c_lo = m.sb("cq2c_lo", [P, D], F32R)
        c2q = m.sb("c2q", [P, D])
        c2qT_hi = m.sb("c2qT_hi", [P, D], F32R)
        c2qT_lo = m.sb("c2qT_lo", [P, D], F32R)
        cc2q, cc2q_hi, cc2q_lo = cq2c, cq2c_hi, cq2c_lo
        x1 = m.sb("x1", [P, D])

        scores = m.ps("scores", [P, QC, BANK])
        turn = [m.ps("turn0", [P, BANK]), m.ps("turn1", [P, BANK])]
        summed = m.ps("summed", [P, BANK])
        projected = m.ps("projected", [P, BANK])
        tok_sum_ps = scores[:, 0, 8:9]
        q2c_ps = scores[:, 0, 0:KD]

        const_landed = m.sem("const_landed")
        ones_done = m.sem("ones_done")
        bias_done = m.sem("bias_done")
        weight_landed = [m.sem(f"weight_landed{s}") for s in range(2)]
        weight_hi = m.sem("weight_hi")
        weight_lo = m.sem("weight_lo")
        x_landed = m.tally("x_landed", 16)
        cols_landed = [m.tally(f"cols_landed{s}", 16 * QC // 2) for s in range(2)]
        rows_landed = [m.tally(f"rows_landed{s}", 16 * RC // 2) for s in range(2)]
        cols_hi_done = m.tally("cols_hi_done", QC)
        cols_lo_done = m.tally("cols_lo_done", QC, QC)
        rows_hi_done = m.tally("rows_hi_done", RC)
        rows_lo_done = m.tally("rows_lo_done", RC, RC)
        norm_steps = m.tally("norm_steps", 4)
        rstd_steps = m.tally("rstd_steps", 2)
        c_turned = m.tally("c_turned", 1)
        cT_steps = m.tally("cT_steps", 1 + KD)
        cT_hi_done = m.tally("cT_hi_done", 1)
        cT_lo_done = m.tally("cT_lo_done", 1)
        cw_hi_done = m.tally("cw_hi_done", 1)
        cw_lo_done = m.tally("cw_lo_done", 1)
        scored = m.tally("scored", QC, QC)
        max_done = m.tally("max_done", QC + 1)
        tok_max_done = m.tally("tok_max_done", 1)
        all_max_done = m.tally("all_max_done", 1)
        exp_done = m.tally("exp_done", QC)
        tok_exp_done = m.tally("tok_exp_done", 1)
        sum_steps = m.tally("sum_steps", 2, 1)
        probs_turned = m.tally("probs_turned", QC, 1)
        probsT_hi_done = m.tally("probsT_hi_done", QC)
        probsT_lo_done = m.tally("probsT_lo_done", QC, QC)
        q2c_summed = m.tally("q2c_summed", 1, 1)
        q2c_steps = m.tally("q2c_steps", 2 + KD)
        cq2c_hi_done = m.tally("cq2c_hi_done", 1)
        cq2c_lo_done = m.tally("cq2c_lo_done", 1)
        held = m.tally("held", 1)
        gathered = m.tally("gathered", QC, QC)
        c_projected = m.tally("c_projected", 2, 2)
        c2q_done = m.tally("c2q_done", 1, 1)
        c2q_turned = m.tally("c2q_turned", 1)
        c2qT_hi_done = m.tally("c2qT_hi_done", 1)
        c2qT_lo_done = m.tally("c2qT_lo_done", 1, 1)
        cc2q_done = m.tally("cc2q_done", 1, 1)
        cc2q_hi_done = m.tally("cc2q_hi_done", 1)
        cc2q_lo_done = m.tally("cc2q_lo_done", 1)
        z_done = m.tally("z_done", 1, 1)
        x1_done = m.tally("x1_done", 1, 1)
        x_bias_done = m.tally("x_bias_done", 1, 1)
        x1_stored = m.tally("x1_stored", 16, 1)
        block = stack.enter_context(nc.Block())

        @block.sync
        def _(sp):
            grant(sp, x1_stored)
            consts = [(ident[:], ident_in), (w_c_rows[:], w_c[None, :].to_broadcast([P, D])),
                      (b_l_rows[:], b_l[None, :].to_broadcast([P, D])),
                      (biases[:, 0:1], b_cq[None, :].to_broadcast([P, 1])),
                      (biases[:, 1:2], b_c[None, :].to_broadcast([P, 1])),
                      (biases[:, 2:3], b_q[None, :].to_broadcast([P, 1]))]
            sp.dma_start(x_in[:], x[0]).then_inc(x_landed.sem, 16)
            for dst, src in consts:
                sp.dma_start(dst, src).then_inc(const_landed, 16)
            sp.dma_start(w_cq_col[:], w_cq).then_inc(const_landed, 16)
            sp.dma_start(w_q_col[:], w_q).then_inc(const_landed, 16)

            def load_x(b):
                sp.wait_ge(x_bias_done.sem, x_bias_done.value(b, 0))
                sp.dma_start(x_in[:], x[b]).then_inc(x_landed.sem, 16)

            def load_cols(b, q):
                sp.wait_ge(cols_lo_done.sem, cols_lo_done.value(b, q - 1))
                sp.dma_start(cols_raw[:, q % 2, :], ctx_cols[b, q]).then_inc(cols_landed[q % 2].sem, 16)

            def load_rows(b, h):
                sp.wait_ge(rows_lo_done.sem, rows_lo_done.value(b, h - 1))
                sp.dma_start(rows_raw[:, h % 2, :], ctx_rows[b, h]).then_inc(rows_landed[h % 2].sem, 16)

            def load_scores(b):
                for q in range(QC):
                    load_cols(b, q)

            load_cols(0, 0)
            for w in range(KZ // NJ):
                if w >= 2:
                    sp.wait_ge(weight_lo, w - 1)
                sp.dma_start(rows_raw[:, w % 2, :].rearrange("p (j d) -> p j d", j=NJ),
                             W_lT[:, w * NJ:(w + 1) * NJ, :]).then_inc(weight_landed[w % 2], 16)
                if w % 2 and w // 2 + 1 < QC:
                    load_cols(0, w // 2 + 1)
            sp.wait_ge(weight_lo, KZ // NJ)
            for h in range(RING):
                load_rows(0, h)

            def step(b, more):
                for h in range(RING, RC):
                    load_rows(b, h)
                if more:
                    load_x(b + 1)
                    load_scores(b + 1)
                    for h in range(RING):
                        load_rows(b + 1, h)
                sp.wait_ge(x1_done.sem, x1_done.value(b, 1))
                sp.dma_start(x1_out[b], x1[:]).then_inc(x1_stored.sem, 16)

            with sp.Fori(0, B - 1) as i:
                step(i, True)
            step(B - 1, False)
            sp.wait_ge(x1_stored.sem, x1_stored.value(B - 1, 16))

        @block.gpsimd
        def _(pool):
            nc.gpsimd.memset(eps_pow[:, 0:1], EPS)
            nc.gpsimd.memset(eps_pow[:, 1:2], -0.5)
            nc.gpsimd.memset(ones[:], 1.0).then_inc(ones_done, 1)
            pool.wait_ge(ones_done, 1)

            def inverse_spread(b):
                pool.wait_ge(norm_steps.sem, norm_steps.value(b, 2))
                pool.nop(nofuse=True)
                nc.gpsimd.tensor_tensor(var_eps[:], mean_var[:, 1:2], eps_pow[:, 0:1], ALU.add).then_inc(rstd_steps.sem, 1)
                pool.wait_ge(rstd_steps.sem, rstd_steps.value(b, 1))
                pool.nop(nofuse=True)
                nc.gpsimd.tensor_tensor(rstd[:], var_eps[:], eps_pow[:, 1:2], ALU.pow).then_inc(rstd_steps.sem, 1)

            def token_maximum(b):
                pool.wait_ge(tok_max_done.sem, tok_max_done.value(b, 1))
                pool.nop(nofuse=True)
                nc.gpsimd.partition_all_reduce(all_max[:], tok_max[:], P, MAX_OVER_PARTITIONS).then_inc(all_max_done.sem, 1)

            inverse_spread(0)
            with pool.Fori(0, B - 1) as i:
                token_maximum(i)
                inverse_spread(i + 1)
            token_maximum(B - 1)

        @block.scalar
        def _(act):
            def high(out, src):
                return nc.scalar.activation(out, src, ACT.Copy)

            def cols_high(b, q):
                s = cols_landed[q % 2]
                act.wait_ge(s.sem, s.value(b, 16 * (q // 2 + 1)))
                act.wait_ge(scored.sem, scored.value(b, q - 1))
                high(cols_hi[:, q % 2].rearrange("p k n -> p (k n)"), cols_raw[:, q % 2, :]).then_inc(cols_hi_done.sem, 1)

            def rows_high(b, h):
                act.wait_ge(rows_landed[h % 2].sem, rows_landed[h % 2].value(b, 16 * (h // 2 + 1)))
                act.wait_ge(gathered.sem, gathered.value(b, (h - RING) // 2 + 1))
                high(rows_hi[:, h % RING].rearrange("p j d -> p (j d)"), rows_raw[:, h % 2, :]).then_inc(rows_hi_done.sem, 1)

            def exps(b):
                act.wait_ge(max_done.sem, max_done.value(b, QC + 1))
                act.wait_ge(sum_steps.sem, sum_steps.value(b, 0))
                act.wait_ge(probs_turned.sem, probs_turned.value(b, 0))
                for q in range(QC):
                    nc.scalar.activation(probs[:, q * BANK:(q + 1) * BANK], scores[:, q, :], ACT.Exp,
                                         bias=neg_max[:], accum_out=chunk_sum[:, q:q + 1]).then_inc(exp_done.sem, 1)

            def probsT_high(b, g):
                act.wait_ge(probs_turned.sem, probs_turned.value(b, g + 1))
                act.wait_ge(gathered.sem, gathered.value(b, g - 1))
                high(probsT_hi[:, g % 2, :], turn[g % 2][:] if g < 3 else turn[0][:]).then_inc(probsT_hi_done.sem, 1)

            def token_exp(b):
                act.wait_ge(all_max_done.sem, all_max_done.value(b, 1))
                act.wait_ge(q2c_summed.sem, q2c_summed.value(b, 0))
                nc.scalar.activation(tok_exp[:], all_max[:], ACT.Exp, bias=tok_max[:], scale=-1.0).then_inc(tok_exp_done.sem, 1)

            def normed_high(b):
                act.wait_ge(cT_steps.sem, cT_steps.value(b, 1))
                act.wait_ge(c_projected.sem, c_projected.value(b, -1))
                high(cT_hi[:], cT[:]).then_inc(cT_hi_done.sem, 1)
                act.wait_ge(cT_steps.sem, cT_steps.value(b, 1 + KD))
                act.wait_ge(scored.sem, scored.value(b, 0))
                high(cw_hi[:], cw[:]).then_inc(cw_hi_done.sem, 1)

            def weighted_out(b):
                act.wait_ge(gathered.sem, gathered.value(b, QC))
                act.wait_ge(sum_steps.sem, sum_steps.value(b, 2))
                nc.scalar.activation(c2q[:], summed[:], ACT.Copy, scale=row_inv[:]).then_inc(c2q_done.sem, 1)

            def weighted_high(b):
                act.wait_ge(c2q_turned.sem, c2q_turned.value(b, 1))
                act.wait_ge(z_done.sem, z_done.value(b, 0))
                high(c2qT_hi[:], turn[1][:]).then_inc(c2qT_hi_done.sem, 1)

            def weighted_product_high(b):
                act.wait_ge(cc2q_done.sem, cc2q_done.value(b, 1))
                high(cc2q_hi[:], cc2q[:]).then_inc(cc2q_hi_done.sem, 1)

            def weight_high_part(w):
                act.wait_ge(weight_landed[w % 2], 16 * (w // 2 + 1))
                nc.scalar.activation(wl_hi[:, w * NJ:(w + 1) * NJ, :].rearrange("p j d -> p (j d)"),
                                     rows_raw[:, w % 2, :], ACT.Copy).then_inc(weight_hi, 1)

            grant(act, c2q_done)
            normed_high(0)
            for q in range(QC):
                cols_high(0, q)
                weight_high_part(2 * q)
                weight_high_part(2 * q + 1)
            for h in range(RING):
                rows_high(0, h)

            def step(b, more):
                exps(b)
                probsT_high(b, 0)
                probsT_high(b, 1)
                token_exp(b)
                rows_high(b, 4)
                rows_high(b, 5)
                act.wait_ge(q2c_steps.sem, q2c_steps.value(b, 2 + KD))
                act.wait_ge(c_projected.sem, c_projected.value(b, 0))
                high(cq2c_hi[:], cq2c[:]).then_inc(cq2c_hi_done.sem, 1)
                probsT_high(b, 2)
                rows_high(b, 6)
                rows_high(b, 7)
                if more:
                    normed_high(b + 1)
                probsT_high(b, 3)
                if more:
                    cols_high(b + 1, 0)
                    cols_high(b + 1, 1)
                weighted_out(b)
                if more:
                    cols_high(b + 1, 2)
                weighted_high(b)
                if more:
                    cols_high(b + 1, 3)
                weighted_product_high(b)
                if more:
                    for h in range(RING):
                        rows_high(b + 1, h)

            with act.Fori(0, B - 1) as i:
                step(i, True)
            step(B - 1, False)

        @block.vector
        def _(dve):
            V = nc.vector

            def low(out, raw, hi):
                return V.tensor_tensor(out, raw, hi.bitcast(F32), ALU.subtract)

            def cols_low(b, q):
                dve.wait_ge(cols_hi_done.sem, cols_hi_done.value(b, q + 1))
                low(cols_lo[:, q % 2].rearrange("p k n -> p (k n)"), cols_raw[:, q % 2, :],
                    cols_hi[:, q % 2].rearrange("p k n -> p (k n)")).then_inc(cols_lo_done.sem, 1)

            def rows_low(b, h):
                dve.wait_ge(rows_hi_done.sem, rows_hi_done.value(b, h + 1))
                low(rows_lo[:, h % RING].rearrange("p j d -> p (j d)"), rows_raw[:, h % 2, :],
                    rows_hi[:, h % RING].rearrange("p j d -> p (j d)")).then_inc(rows_lo_done.sem, 1)

            def norm(b):
                dve.wait_ge(x_landed.sem, x_landed.value(b, 16))
                V.bn_stats(stats[:], x_in[:]).then_inc(norm_steps.sem, 1)
                dve.wait_ge(norm_steps.sem, norm_steps.value(b, 1))
                dve.nop(nofuse=True)
                V.bn_aggr(mean_var[:], stats[:]).then_inc(norm_steps.sem, 1)
                dve.wait_ge(rstd_steps.sem, rstd_steps.value(b, 2))
                V.tensor_scalar(c[:], x_in[:], mean_var[:, 0:1], rstd[:], ALU.subtract, ALU.mult).then_inc(norm_steps.sem, 1)
                dve.wait_ge(norm_steps.sem, norm_steps.value(b, 3))
                V.tensor_tensor_reduce(out=cw[:], in0=c[:], in1=w_c_rows[:], scale=1.0, scalar=0.0,
                                       op0=ALU.mult, op1=ALU.add, accum_out=row_dot[:]).then_inc(norm_steps.sem, 1)

            def normed_low(b):
                dve.wait_ge(c_turned.sem, c_turned.value(b, 1))
                V.tensor_copy(cT[:], turn[1][:]).then_inc(cT_steps.sem, 1)
                dve.wait_ge(cT_steps.sem, cT_steps.value(b, 1))
                for k in range(KD):
                    V.tensor_scalar(cw[:, k * P:(k + 1) * P], cT[:, k * P:(k + 1) * P], w_cq_col[:, k:k + 1],
                                    w_q_col[:, k:k + 1], ALU.mult, ALU.add).then_inc(cT_steps.sem, 1)
                dve.wait_ge(cT_hi_done.sem, cT_hi_done.value(b, 1))
                low(cT_lo[:], cT[:], cT_hi[:]).then_inc(cT_lo_done.sem, 1)
                dve.wait_ge(cw_hi_done.sem, cw_hi_done.value(b, 1))
                low(cw_lo[:], cw[:], cw_hi[:]).then_inc(cw_lo_done.sem, 1)

            def chunk_maximum(b, q):
                dve.wait_ge(scored.sem, scored.value(b, q + 1))
                V.reduce_max(chunk_max[:, q:q + 1], scores[:, q, :], AX.X).then_inc(max_done.sem, 1)

            def row_maximum(b):
                dve.wait_ge(max_done.sem, max_done.value(b, QC))
                V.tensor_reduce(neg_max[:], chunk_max[:], AX.X, ALU.max, negate=True).then_inc(max_done.sem, 1)
                dve.wait_ge(max_done.sem, max_done.value(b, QC + 1))
                V.tensor_scalar(tok_max[:], row_dot[:], neg_max[:], bias_sum[:], ALU.subtract, ALU.add).then_inc(tok_max_done.sem, 1)

            def probsT_low(b, g):
                dve.wait_ge(probsT_hi_done.sem, probsT_hi_done.value(b, g + 1))
                low(probsT_lo[:, g % 2, :], turn[g % 2][:] if g < 3 else turn[0][:], probsT_hi[:, g % 2, :]).then_inc(probsT_lo_done.sem, 1)

            def sums(b):
                dve.wait_ge(exp_done.sem, exp_done.value(b, QC))
                V.reduce_sum(row_sum[:], chunk_sum[:], AX.X).then_inc(sum_steps.sem, 1)
                dve.wait_ge(sum_steps.sem, sum_steps.value(b, 1))
                dve.wait_ge(c2q_done.sem, c2q_done.value(b, 0))
                V.reciprocal(row_inv[:], row_sum[:]).then_inc(sum_steps.sem, 1)

            def token_part(b):
                dve.wait_ge(q2c_summed.sem, q2c_summed.value(b, 1))
                V.reciprocal(tok_inv[:], tok_sum_ps).then_inc(q2c_steps.sem, 1)
                dve.wait_ge(q2c_steps.sem, q2c_steps.value(b, 1))
                V.tensor_scalar(q2c[:], q2c_ps, tok_inv[:], None, ALU.mult).then_inc(q2c_steps.sem, 1)
                dve.wait_ge(q2c_steps.sem, q2c_steps.value(b, 2))
                for k in range(KD):
                    V.tensor_scalar(cq2c[:, k * P:(k + 1) * P], cT[:, k * P:(k + 1) * P], q2c[:, k:k + 1],
                                    None, ALU.mult).then_inc(q2c_steps.sem, 1)

            def token_part_low(b):
                dve.wait_ge(cq2c_hi_done.sem, cq2c_hi_done.value(b, 1))
                low(cq2c_lo[:], cq2c[:], cq2c_hi[:]).then_inc(cq2c_lo_done.sem, 1)

            def x_plus_bias(b):
                dve.wait_ge(x1_done.sem, x1_done.value(b, 0))
                V.tensor_tensor(x_bias[:], x_in[:], b_l_rows[:], ALU.add).then_inc(x_bias_done.sem, 1)

            grant(dve, sum_steps, c2qT_lo_done, cols_lo_done, rows_lo_done, probsT_lo_done, cc2q_done, x1_done, x_bias_done)
            dve.wait_ge(const_landed, 16 * 8)
            V.reduce_sum(bias_sum[:], biases[:], AX.X).then_inc(bias_done, 1)
            dve.wait_ge(bias_done, 1)
            norm(0)
            normed_low(0)
            def weight_low_part(w):
                dve.wait_ge(weight_hi, w + 1)
                V.tensor_tensor(wl_lo[:, w * NJ:(w + 1) * NJ, :].rearrange("p j d -> p (j d)"), rows_raw[:, w % 2, :],
                                wl_hi[:, w * NJ:(w + 1) * NJ, :].rearrange("p j d -> p (j d)").bitcast(F32),
                                ALU.subtract).then_inc(weight_lo, 1)

            for q in range(QC):
                cols_low(0, q)
                weight_low_part(2 * q)
                weight_low_part(2 * q + 1)
                chunk_maximum(0, q)
            row_maximum(0)
            for h in range(RING):
                rows_low(0, h)
            x_plus_bias(0)

            def step(b, more):
                probsT_low(b, 0)
                probsT_low(b, 1)
                sums(b)
                rows_low(b, 4)
                rows_low(b, 5)
                token_part(b)
                token_part_low(b)
                probsT_low(b, 2)
                V.tensor_copy(cT_held[:], cT[:]).then_inc(held.sem, 1)
                if more:
                    norm(b + 1)
                rows_low(b, 6)
                rows_low(b, 7)
                dve.wait_ge(held.sem, held.value(b, 1))
                if more:
                    normed_low(b + 1)
                probsT_low(b, 3)
                if more:
                    cols_low(b + 1, 0)
                    cols_low(b + 1, 1)
                    chunk_maximum(b + 1, 0)
                    cols_low(b + 1, 2)
                dve.wait_ge(c2qT_hi_done.sem, c2qT_hi_done.value(b, 1))
                V.tensor_tensor(cc2q[:], turn[1][:], cT_held[:], ALU.mult).then_inc(cc2q_done.sem, 1)
                low(c2qT_lo[:], turn[1][:], c2qT_hi[:]).then_inc(c2qT_lo_done.sem, 1)
                if more:
                    chunk_maximum(b + 1, 1)
                    cols_low(b + 1, 3)
                dve.wait_ge(cc2q_hi_done.sem, cc2q_hi_done.value(b, 1))
                low(cc2q_lo[:], cc2q[:], cc2q_hi[:]).then_inc(cc2q_lo_done.sem, 1)
                if more:
                    chunk_maximum(b + 1, 2)
                    rows_low(b + 1, 0)
                    chunk_maximum(b + 1, 3)
                    row_maximum(b + 1)
                    for h in range(1, RING):
                        rows_low(b + 1, h)
                dve.wait_ge(z_done.sem, z_done.value(b, 1))
                dve.wait_ge(x_bias_done.sem, x_bias_done.value(b, 1))
                dve.wait_ge(x1_stored.sem, x1_stored.value(b, 0))
                V.tensor_tensor(x1[:], projected[:], x_bias[:], ALU.add).then_inc(x1_done.sem, 1)
                if more:
                    x_plus_bias(b + 1)

            with dve.Fori(0, B - 1) as i:
                step(i, True)
            step(B - 1, False)

        @block.tensor
        def _(pe):
            def turn_normed(b):
                pe.wait_ge(norm_steps.sem, norm_steps.value(b, 3))
                pe.wait_ge(probsT_lo_done.sem, probsT_lo_done.value(b, -2))
                for k in range(KD):
                    last = nc.tensor.transpose(turn[1][:, k * P:(k + 1) * P], c[:, k * P:(k + 1) * P], ident[:])
                last.then_inc(c_turned.sem, 1)

            def score(b, q):
                pe.wait_ge(cols_lo_done.sem, cols_lo_done.value(b, q + 1))
                for k in range(KD):
                    ks = slice(k * P, (k + 1) * P)
                    last = product(nc, scores[:, q, :], (cw_hi[:, ks], cw_lo[:, ks]),
                                   (cols_hi[:, q % 2, k, :], cols_lo[:, q % 2, k, :]), k == 0, k == KD - 1)
                last.then_inc(scored.sem, 1)

            def turn_probs(b, g):
                pe.wait_ge(exp_done.sem, exp_done.value(b, g + 1))
                if g == 0:
                    pe.wait_ge(probsT_lo_done.sem, probsT_lo_done.value(b, 0))
                elif g == 1:
                    pe.wait_ge(cc2q_done.sem, cc2q_done.value(b, 0))
                    pe.wait_ge(c2qT_lo_done.sem, c2qT_lo_done.value(b, 0))
                    if True:
                        pe.wait_ge(cT_lo_done.sem, cT_lo_done.value(b, 1))
                else:
                    pe.wait_ge(probsT_lo_done.sem, probsT_lo_done.value(b, g - 1 if g == 2 else 3))
                to = turn[g % 2] if g < 3 else turn[0]
                for t in range(4):
                    h, j = 2 * g + t // NJ, t % NJ
                    last = nc.tensor.transpose(to[:, t * P:(t + 1) * P],
                                               probs[:, h * NJ * P + j:(h + 1) * NJ * P:NJ], ident[:])
                last.then_inc(probs_turned.sem, 1)

            def gather(b, g):
                pe.wait_ge(probsT_lo_done.sem, probsT_lo_done.value(b, g + 1))
                pe.wait_ge(rows_lo_done.sem, rows_lo_done.value(b, 2 * g + 2))
                if g == 0:
                    pe.wait_ge(c2q_done.sem, c2q_done.value(b, 0))
                for t in range(4):
                    h, j = 2 * g + t // NJ, t % NJ
                    last = product(nc, summed[:], (probsT_hi[:, g % 2, t * P:(t + 1) * P], probsT_lo[:, g % 2, t * P:(t + 1) * P]),
                                   (rows_hi[:, h % RING, j, :], rows_lo[:, h % RING, j, :]), g == 0 and t == 0, g == QC - 1 and t == 3)
                last.then_inc(gathered.sem, 1)

            def project(part, hi, lo, first, last):
                for k in range(KD):
                    ks = slice(k * P, (k + 1) * P)
                    z = part * KD + k
                    made = product(nc, projected[:], (hi[:, ks], lo[:, ks]), (wl_hi[:, z, :], wl_lo[:, z, :]),
                                   first and k == 0, last and k == KD - 1)
                return made

            def sum_tokens(b):
                pe.wait_ge(tok_exp_done.sem, tok_exp_done.value(b, 1))
                pe.wait_ge(exp_done.sem, exp_done.value(b, QC))
                nc.tensor.matmul(tok_sum_ps, ones[:], tok_exp[:], start=True, stop=True)
                for k in range(KD):
                    last = nc.tensor.matmul(q2c_ps[:, k:k + 1], c[:, k * P:(k + 1) * P], tok_exp[:], start=True, stop=True)
                last.then_inc(q2c_summed.sem, 1)

            grant(pe, probs_turned, q2c_summed, scored, gathered, c_projected, z_done)
            pe.wait_ge(const_landed, 16 * 8)
            pe.wait_ge(ones_done, 1)
            turn_normed(0)
            pe.wait_ge(cw_lo_done.sem, cw_lo_done.value(0, 1))
            for q in range(QC):
                score(0, q)

            def step(b, more):
                turn_probs(b, 0)
                turn_probs(b, 1)
                gather(b, 0)
                sum_tokens(b)
                turn_probs(b, 2)
                pe.wait_ge(x1_done.sem, x1_done.value(b, 0))
                pe.wait_ge(cT_lo_done.sem, cT_lo_done.value(b, 1))
                if b is not None:
                    pe.wait_ge(weight_lo, KZ // NJ)
                project(0, cT_hi, cT_lo, True, False).then_inc(c_projected.sem, 1)
                gather(b, 1)
                if more:
                    turn_normed(b + 1)
                turn_probs(b, 3)
                pe.wait_ge(cq2c_lo_done.sem, cq2c_lo_done.value(b, 1))
                project(3, cq2c_hi, cq2c_lo, False, False).then_inc(c_projected.sem, 1)
                gather(b, 2)
                gather(b, 3)
                if more:
                    pe.wait_ge(cw_lo_done.sem, cw_lo_done.value(b + 1, 1))
                    pe.wait_ge(q2c_steps.sem, q2c_steps.value(b, 2))
                    score(b + 1, 0)
                    score(b + 1, 1)
                pe.wait_ge(c2q_done.sem, c2q_done.value(b, 1))
                if more:
                    pe.wait_ge(cT_lo_done.sem, cT_lo_done.value(b + 1, 1))
                for k in range(KD):
                    last = nc.tensor.transpose(turn[1][:, k * P:(k + 1) * P], c2q[:, k * P:(k + 1) * P], ident[:])
                last.then_inc(c2q_turned.sem, 1)
                if more:
                    score(b + 1, 2)
                    score(b + 1, 3)
                pe.wait_ge(c2qT_lo_done.sem, c2qT_lo_done.value(b, 1))
                project(1, c2qT_hi, c2qT_lo, False, False)
                pe.wait_ge(cc2q_lo_done.sem, cc2q_lo_done.value(b, 1))
                project(2, cc2q_hi, cc2q_lo, False, True).then_inc(z_done.sem, 1)

            with pe.Fori(0, B - 1) as i:
                step(i, True)
            step(B - 1, False)


H = 16
HD = D // H
E = 32
TOPK = 4
CAP = 1024
G = 4
NG = B // G
NBLOCKS = 96
NONE = E * CAP
ROWS = NONE + NBLOCKS * P


def self_attention_and_routing(nc, x1_in, W_qkT, W_vT, W_g, W_s13, W_s2, ident_in, before_in, normed_out, acc_out,
                               token_of_slot, pair_rank, pair_expert, pair_weight, expert_count):
    CQ = 2 * D // P
    CF = 512 // P
    QUARTER = H // 4
    VW = HD + 1
    with ExitStack() as stack:
        m = Memory(nc, stack, "sa")
        wqk = [m.sb("wqk_hi", [P, KD, 2 * D], F32R), m.sb("wqk_lo", [P, KD, 2 * D], F32R)]
        wv = [m.sb("wv_hi", [P, KD, D], F32R), m.sb("wv_lo", [P, KD, D], F32R)]
        ws13 = [m.sb("ws13_hi", [P, KD, 2 * D], F32R), m.sb("ws13_lo", [P, KD, 2 * D], F32R)]
        ws2 = [m.sb("ws2_hi", [P, CF, D], F32R), m.sb("ws2_lo", [P, CF, D], F32R)]
        wg = [m.sb("wg_hi", [P, KD, E], F32R), m.sb("wg_lo", [P, KD, E], F32R)]
        wg_raw = m.sb("wg_raw", [P, KD, E])
        ident = m.sb("ident", [P, P])
        before = m.sb("before", [P, P])
        ones = m.sb("ones", [P, P])
        eps_pow = m.sb("eps_pow", [P, 2])
        x = m.sb("x", [P, G, D])
        xn = m.sb("xn", [P, 4, D])
        xnT_hi = m.sb("xnT_hi", [P, KD, G * P], F32R)
        xnT_lo = m.sb("xnT_lo", [P, KD, G * P], F32R)
        stats = m.sb("stats", [P, 6])
        mean_var = m.sb("mean_var", [P, 2])
        var_eps = m.sb("var_eps", [P, 1])
        rstd = m.sb("rstd", [P, 1])
        qkT = m.sb("qkT", [P, CQ, G * P])
        v = m.sb("v", [P, G, H, VW])
        probs = m.sb("probs", [P, H, P])
        probsT = m.sb("probsT", [P, H, P])
        head_max = m.sb("head_max", [P, H])
        head_inv = m.sb("head_inv", [P, H])
        mixed = m.sb("mixed", [P, D])
        gate = m.sb("gate", [P, G * P])
        hT = m.sb("hT", [P, G * P])
        hT_hi = m.sb("hT_hi", [P, CF, G * P], F32R)
        hT_lo = m.sb("hT_lo", [P, CF, G * P], F32R)
        acc = m.sb("acc", [P, 2, D])
        logits = m.sb("logits", [P, G, E])
        top = m.sb("top", [P, G, 8])
        top_at = m.sb("top_at", [P, G, 8], U32)
        expert = m.sb("expert", [P, G, TOPK])
        shifted = m.sb("shifted", [P, G, E])
        top_shifted = m.sb("top_shifted", [P, G, TOPK])
        exp_sum = m.sb("exp_sum", [P, G])
        exp_inv = m.sb("exp_inv", [P, G])
        iota_e = m.sb("iota_e", [P, E])
        one_hot = m.sb("one_hot", [P, G, TOPK, E])
        taken = m.sb("taken", [P, G, E])
        counted = expert_count
        group_taken = m.sb("group_taken", [P, E])
        ranked = m.sb("ranked", [P, G, TOPK, E])
        rank = m.sb("rank", [P, G * TOPK])
        kept = m.sb("kept", [P, G * TOPK])
        base = m.sb("base", [P, G * TOPK])
        slot = m.sb("slot", [P, G * TOPK])
        scatter_to = m.sb("scatter_to", [P, G * TOPK], I32)
        tokens_f = m.sb("tokens_f", [P, G])
        tokens = m.sb("tokens", [P, G], I32)
        zeros = m.sb("zeros", [P, ROWS // P], I32)

        S = m.ps("scores", [P, 4, BANK])
        turn = [m.ps("turn0", [P, BANK]), m.ps("turn1", [P, BANK])]
        work = [m.ps("work0", [P, BANK]), m.ps("work1", [P, BANK])]

        const_landed = m.sem("const_landed")
        setup = m.sem("setup")
        NW = 6
        w_landed = [m.sem("w_landed0"), m.sem("w_landed1")]
        w_hi = m.sem("w_hi")
        w_lo = m.sem("w_lo")
        x_landed = m.tally("x_landed", 16)
        norm_steps = m.tally("norm_steps", 3 * 2 * G)
        rstd_steps = m.tally("rstd_steps", 2 * 2 * G)
        turned = m.tally("turned", 2 * G, 1)
        xnT_hi_done = m.tally("xnT_hi_done", 2 * G)
        xnT_lo_done = m.tally("xnT_lo_done", 2 * G, 2 * G)
        normed_stored = [m.tally("normed_stored0", 16 * G // 2, 1), m.tally("normed_stored1", 16 * G // 2, 1)]
        qk_done = m.tally("qk_done", CQ)
        qk_read = m.tally("qk_read", CQ)
        v_done = m.tally("v_done", G)
        v_read = m.tally("v_read", G)
        scored = m.tally("scored", G, 1)
        max_done = m.tally("max_done", G)
        shift_done = m.tally("shift_done", G)
        exp_done = m.tally("exp_done", G)
        probs_turned = m.tally("probs_turned", 4 * G, 1)
        probsT_read = m.tally("probsT_read", 4 * G, 4 * G)
        mixed_done = m.tally("mixed_done", G, 1)
        mix_steps = m.tally("mix_steps", 6 * G, 1)
        logits_done = m.tally("logits_done", 1)
        logits_steps = m.tally("logits_steps", 1)
        up_done = m.tally("up_done", CF, 1)
        gate_done = m.tally("gate_done", CF)
        h_steps = m.tally("h_steps", 2 * CF, 2 * CF)
        hT_hi_done = m.tally("hT_hi_done", CF, 1)
        hT_lo_done = m.tally("hT_lo_done", CF, 1)
        down_done = m.tally("down_done", G, 1)
        acc_done = m.tally("acc_done", G, 1)
        acc_stored = [m.tally("acc_stored0", 16 * G // 2, 1), m.tally("acc_stored1", 16 * G // 2, 1)]
        R_SHIFTED, R_TAKEN, R_RANKED, ROUTE_STEPS = 11, 13, 16, 30
        route_steps = m.tally("route_steps", ROUTE_STEPS, 1)
        route_exp_done = m.tally("route_exp_done", 2)
        ranks_done = m.tally("ranks_done", 1)
        scattered = m.tally("scattered", 16 * G * TOPK)
        scatter_over = m.tally("scatter_over", 1, 1)
        zeroed = m.sem("zeroed")
        block = stack.enter_context(nc.Block())

        stage = [probs[:].rearrange("p h n -> p (h n)"), probsT[:].rearrange("p h n -> p (h n)")]
        half = KD // 2

        def flat(ap):
            return ap.rearrange("p k n -> p (k n)")

        pieces = [(flat(W_qkT[:, :half, :]), wqk, slice(0, half)), (flat(W_qkT[:, half:, :]), wqk, slice(half, KD)),
                  (flat(W_vT), wv, slice(0, KD)),
                  (flat(W_s13[:, :half, :]), ws13, slice(0, half)), (flat(W_s13[:, half:, :]), ws13, slice(half, KD)),
                  (flat(W_s2), ws2, slice(0, CF))]

        @block.sync
        def _(sp):
            grant(sp, normed_stored[0], normed_stored[1], acc_stored[0], acc_stored[1])
            sp.dma_start(x[:], x1_in[0:G].rearrange("b p d -> p b d")).then_inc(x_landed.sem, 16)
            for dst, src in ((ident[:], ident_in), (before[:], before_in), (wg_raw[:], W_g)):
                sp.dma_start(dst, src).then_inc(const_landed, 16)
            for n, (src, _, _) in enumerate(pieces):
                if n >= 2:
                    sp.wait_ge(w_lo, n)
                sp.dma_start(stage[n % 2], src).then_inc(w_landed[n % 2], 16)
            sp.wait_ge(setup, 1)
            sp.dma_start(token_of_slot.rearrange("(p n) one -> p (n one)", p=P), zeros[:]).then_inc(zeroed, 16)

            def step(g, more):
                for j in range(G):
                    sp.wait_ge(norm_steps.sem, norm_steps.value(g, 3 * (G + j) + 3))
                    sp.dma_start(normed_out[g * G + j], xn[:, 2 + j % 2, :]).then_inc(normed_stored[j % 2].sem, 16)
                for j in range(G):
                    sp.wait_ge(acc_done.sem, acc_done.value(g, j + 1))
                    sp.dma_start(acc_out[g * G + j], acc[:, j % 2, :]).then_inc(acc_stored[j % 2].sem, 16)
                if more:
                    sp.dma_start(x[:], x1_in[bass.ds(g * G + G, G)].rearrange("b p d -> p b d")).then_inc(x_landed.sem, 16)

            with sp.Fori(0, NG - 1) as i:
                step(i, True)
            step(NG - 1, False)
            for j in range(2):
                sp.wait_ge(normed_stored[j].sem, normed_stored[j].value(NG - 1, 16 * G // 2))
                sp.wait_ge(acc_stored[j].sem, acc_stored[j].value(NG - 1, 16 * G // 2))

        @block.gpsimd
        def _(pool):
            nc.gpsimd.memset(eps_pow[:, 0:1], EPS)
            nc.gpsimd.memset(eps_pow[:, 1:2], -0.5)
            nc.gpsimd.memset(ones[:], 1.0)
            nc.gpsimd.memset(zeros[:], 0)
            nc.gpsimd.memset(counted[:], 0.0)
            for j in range(G):
                nc.gpsimd.memset(v[:, j, :, HD:VW], 1.0)
            nc.gpsimd.iota(iota_e[:], pattern=[[1, E]], base=0, channel_multiplier=0, allow_small_or_imprecise_dtypes=True)
            nc.gpsimd.iota(tokens_f[:], pattern=[[P, G]], base=0, channel_multiplier=1, allow_small_or_imprecise_dtypes=True).then_inc(setup, 1)
            grant(pool, scatter_over)
            pool.wait_ge(setup, 1)
            pool.wait_ge(zeroed, 16)

            def inverse_spread(g, n):
                pool.wait_ge(norm_steps.sem, norm_steps.value(g, 3 * n + 2))
                pool.nop(nofuse=True)
                nc.gpsimd.tensor_tensor(var_eps[:], mean_var[:, 1:2], eps_pow[:, 0:1], ALU.add).then_inc(rstd_steps.sem, 1)
                pool.wait_ge(rstd_steps.sem, rstd_steps.value(g, 2 * n + 1))
                pool.nop(nofuse=True)
                nc.gpsimd.tensor_tensor(rstd[:], var_eps[:], eps_pow[:, 1:2], ALU.pow).then_inc(rstd_steps.sem, 1)

            def step(g):
                for n in range(2 * G):
                    inverse_spread(g, n)
                pool.wait_ge(route_steps.sem, route_steps.value(g, ROUTE_STEPS))
                pool.nop(nofuse=True)
                for j in range(G):
                    for k in range(TOPK):
                        n = j * TOPK + k
                        pool.indirect_dma_start(token_of_slot, bass.IndirectOffsetOnAxis(ap=scatter_to[:, n:n + 1], axis=0),
                                                tokens[:, j:j + 1], None, bounds_check=NONE - 1, oob_is_err=False)\
                            .then_inc(scattered.sem, 16)
                pool.wait_ge(scattered.sem, scattered.value(g, 16 * G * TOPK))
                pool.nop(nofuse=True)
                pool.sem_inc(scatter_over.sem, 1)

            with pool.Fori(0, NG) as i:
                step(i)

        @block.scalar
        def _(act):
            def copy(out, src):
                return nc.scalar.activation(out, src, ACT.Copy)

            grant(act, probsT_read, hT_hi_done)

            def normed_high(g, n):
                j = n % G
                act.wait_ge(turned.sem, turned.value(g, n + 1))
                if n < G:
                    act.wait_ge(up_done.sem, up_done.value(g, 0))
                else:
                    act.wait_ge(v_done.sem, v_done.value(g, G))
                copy(xnT_hi[:, :, j * P:(j + 1) * P], turn[n % 2][:].rearrange("p (k t) -> p k t", k=KD)).then_inc(xnT_hi_done.sem, 1)

            def project_out(g, c):
                act.wait_ge(qk_done.sem, qk_done.value(g, c + 1))
                if c == 0:
                    act.wait_ge(scored.sem, scored.value(g, 0))
                copy(qkT[:, c, :], S[:, c % 4, :]).then_inc(qk_read.sem, 1)

            def attend(g, j):
                act.wait_ge(shift_done.sem, shift_done.value(g, j + 1))
                nc.scalar.activation(probs[:], probs[:], ACT.Exp, scale=float(D) ** -0.5).then_inc(exp_done.sem, 1)

            def probsT_out(g, j):
                for q in range(4):
                    act.wait_ge(probs_turned.sem, probs_turned.value(g, 4 * j + q + 1))
                    act.wait_ge(mixed_done.sem, mixed_done.value(g, j))
                    copy(probsT[:, q * 4:q * 4 + 4, :], turn[q % 2][:].rearrange("p (h t) -> p h t", h=4)).then_inc(probsT_read.sem, 1)

            act.wait_ge(const_landed, 16 * 3)
            copy(flat(wg[0][:]), flat(wg_raw[:])).then_inc(w_hi, 1)
            for n in range(NW):
                _, (hi, _), ks = pieces[n]
                act.wait_ge(w_landed[n % 2], 16 * (n // 2 + 1))
                copy(flat(hi[:, ks, :]), stage[n % 2]).then_inc(w_hi, 1)

            def step(g):
                for n in range(G):
                    normed_high(g, n)
                for c in range(CQ):
                    project_out(g, c)
                attend(g, 0)
                for j in range(G):
                    probsT_out(g, j)
                    if j + 1 < G:
                        attend(g, j + 1)
                    if j:
                        normed_high(g, G + j - 1)
                normed_high(g, 2 * G - 1)
                act.wait_ge(route_steps.sem, route_steps.value(g, R_SHIFTED))
                nc.scalar.activation(shifted[:], shifted[:], ACT.Exp).then_inc(route_exp_done.sem, 1)
                nc.scalar.activation(top_shifted[:], top_shifted[:], ACT.Exp).then_inc(route_exp_done.sem, 1)
                for c in range(CF):
                    act.wait_ge(up_done.sem, up_done.value(g, c + 1))
                    act.wait_ge(h_steps.sem, h_steps.value(g, 2 * c - 1))
                    nc.scalar.activation(gate[:], S[:, 2 * (c % 2), :], ACT.Tanh, scale=0.5).then_inc(gate_done.sem, 1)
                    act.wait_ge(h_steps.sem, h_steps.value(g, 2 * c + 2))
                    act.wait_ge(down_done.sem, down_done.value(g, 0))
                    copy(hT_hi[:, c, :], hT[:]).then_inc(hT_hi_done.sem, 1)

            with act.Fori(0, NG) as i:
                step(i)

        @block.vector
        def _(dve):
            V = nc.vector
            grant(dve, xnT_lo_done, h_steps, route_steps, hT_lo_done, acc_done, mix_steps)

            def low(out, raw, hi):
                return V.tensor_tensor(out, raw, hi.bitcast(F32), ALU.subtract)

            def norm(g, n):
                j = n % G
                if n == 0:
                    dve.wait_ge(x_landed.sem, x_landed.value(g, 16))
                if n >= G:
                    dve.wait_ge(mix_steps.sem, mix_steps.value(g, 6 * j + 6))
                V.bn_stats(stats[:], x[:, j, :]).then_inc(norm_steps.sem, 1)
                dve.wait_ge(norm_steps.sem, norm_steps.value(g, 3 * n + 1))
                dve.nop(nofuse=True)
                V.bn_aggr(mean_var[:], stats[:]).then_inc(norm_steps.sem, 1)
                dve.wait_ge(rstd_steps.sem, rstd_steps.value(g, 2 * n + 2))
                dve.wait_ge(turned.sem, turned.value(g, n - 1 if j >= 2 else 0))
                if n >= G:
                    dve.wait_ge(normed_stored[j % 2].sem, normed_stored[j % 2].value(g, 16 * (j // 2)))
                V.tensor_scalar(xn[:, 2 * (n // G) + j % 2, :], x[:, j, :], mean_var[:, 0:1], rstd[:], ALU.subtract, ALU.mult)\
                    .then_inc(norm_steps.sem, 1)

            def normed_low(g, n):
                j = n % G
                dve.wait_ge(xnT_hi_done.sem, xnT_hi_done.value(g, n + 1))
                low(xnT_lo[:, :, j * P:(j + 1) * P], turn[n % 2][:].rearrange("p (k t) -> p k t", k=KD),
                    xnT_hi[:, :, j * P:(j + 1) * P]).then_inc(xnT_lo_done.sem, 1)

            def maximum_and_shift(g, j):
                dve.wait_ge(scored.sem, scored.value(g, j + 1))
                V.reduce_max(head_max[:].rearrange("p (c r) -> p r c", r=4), S[:].rearrange("p r (c n) -> p r c n", n=P), AX.X).then_inc(max_done.sem, 1)
                dve.wait_ge(max_done.sem, max_done.value(g, j + 1))
                dve.wait_ge(probs_turned.sem, probs_turned.value(g, 4 * j))
                for r in range(4):
                    last = V.tensor_tensor(probs[:].rearrange("p (c r) n -> p r c n", r=4)[:, r],
                                           S[:, r, :].rearrange("p (c n) -> p c n", n=P),
                                           head_max[:].rearrange("p (c r) -> p r c", r=4)[:, r].unsqueeze(2).to_broadcast([P, QUARTER, P]),
                                           ALU.subtract)
                last.then_inc(shift_done.sem, 1)

            def mix_out(g, j):
                dve.wait_ge(mixed_done.sem, mixed_done.value(g, j + 1))
                k0 = 6 * j
                for w in range(2):
                    hs = slice(w * 8, w * 8 + 8)
                    o = work[w][:, 0:8 * VW].rearrange("p (h n) -> p h n", n=VW)
                    mw = mixed[:, w * 256:(w + 1) * 256].rearrange("p (h n) -> p h n", n=HD)
                    V.reciprocal(head_inv[:, hs], o[:, :, HD:VW].rearrange("p h n -> p (h n)")).then_inc(mix_steps.sem, 1)
                    dve.wait_ge(mix_steps.sem, mix_steps.value(g, k0 + 3 * w + 1))
                    V.tensor_tensor(mw, o[:, :, 0:HD], head_inv[:, hs].unsqueeze(2).to_broadcast([P, 8, HD]), ALU.mult).then_inc(mix_steps.sem, 1)
                    dve.wait_ge(mix_steps.sem, mix_steps.value(g, k0 + 3 * w + 2))
                    xw = x[:, j, w * 256:(w + 1) * 256]
                    V.tensor_tensor(xw, xw, mixed[:, w * 256:(w + 1) * 256], ALU.add).then_inc(mix_steps.sem, 1)

            dve.wait_ge(const_landed, 16 * 3)
            dve.wait_ge(setup, 1)
            dve.wait_ge(w_hi, 1)
            low(flat(wg[1][:]), flat(wg_raw[:]), flat(wg[0][:])).then_inc(w_lo, 1)
            for n in range(NW):
                _, (hi, lo), ks = pieces[n]
                dve.wait_ge(w_hi, n + 2)
                low(flat(lo[:, ks, :]), stage[n % 2], flat(hi[:, ks, :])).then_inc(w_lo, 1)

            def choose(g):
                dve.wait_ge(logits_done.sem, logits_done.value(g, 1))
                dve.wait_ge(route_steps.sem, route_steps.value(g, 0))
                V.tensor_copy(logits[:], work[0][:, 0:G * E].rearrange("p (j e) -> p j e", e=E)).then_inc(logits_steps.sem, 1)
                dve.wait_ge(logits_steps.sem, logits_steps.value(g, 1))
                dve.nop(nofuse=True)
                for j in range(G):
                    V.max(top[:, j, :], logits[:, j, :]).then_inc(route_steps.sem, 1)
                dve.wait_ge(route_steps.sem, route_steps.value(g, 4))
                dve.nop(nofuse=True)
                for j in range(G):
                    V.max_index(top_at[:, j, :], top[:, j, :], logits[:, j, :]).then_inc(route_steps.sem, 1)
                dve.wait_ge(route_steps.sem, route_steps.value(g, 8))
                V.tensor_copy(expert[:], top_at[:, :, 0:TOPK]).then_inc(route_steps.sem, 1)
                V.tensor_tensor(shifted[:], logits[:], top[:, :, 0:1].to_broadcast([P, G, E]), ALU.subtract).then_inc(route_steps.sem, 1)
                V.tensor_tensor(top_shifted[:], top[:, :, 0:TOPK], top[:, :, 0:1].to_broadcast([P, G, TOPK]), ALU.subtract).then_inc(route_steps.sem, 1)
                dve.wait_ge(route_steps.sem, route_steps.value(g, 11))
                V.tensor_tensor(one_hot[:], iota_e[:].unsqueeze(1).unsqueeze(1).to_broadcast([P, G, TOPK, E]),
                                     expert[:].unsqueeze(3).to_broadcast([P, G, TOPK, E]), ALU.is_equal).then_inc(route_steps.sem, 1)
                dve.wait_ge(route_steps.sem, route_steps.value(g, 12))
                V.tensor_reduce(taken[:], one_hot[:].rearrange("p j k e -> p j e k"), AX.X, ALU.add).then_inc(route_steps.sem, 1)

            def place(g):
                pairs = slice(0, G * TOPK)
                dve.wait_ge(route_exp_done.sem, route_exp_done.value(g, 2))
                V.reduce_sum(exp_sum[:], shifted[:], AX.X).then_inc(route_steps.sem, 1)
                dve.wait_ge(route_steps.sem, route_steps.value(g, 14))
                V.reciprocal(exp_inv[:], exp_sum[:]).then_inc(route_steps.sem, 1)
                dve.wait_ge(ranks_done.sem, ranks_done.value(g, 1))
                V.tensor_tensor(ranked[:], one_hot[:], work[1][:, 0:G * E].rearrange("p (j e) -> p j e", e=E).unsqueeze(2)
                                     .to_broadcast([P, G, TOPK, E]), ALU.mult).then_inc(route_steps.sem, 1)
                V.tensor_reduce(group_taken[:], taken[:].rearrange("p j e -> p e j"), AX.X, ALU.add).then_inc(route_steps.sem, 1)
                dve.wait_ge(route_steps.sem, route_steps.value(g, 17))
                V.tensor_tensor(counted[:], counted[:], group_taken[:], ALU.add).then_inc(route_steps.sem, 1)
                V.reduce_sum(rank[:], ranked[:].rearrange("p j k e -> p (j k) e"), AX.X).then_inc(route_steps.sem, 1)
                dve.wait_ge(route_steps.sem, route_steps.value(g, 19))
                V.tensor_single_scalar(kept[:], rank[:], float(CAP), ALU.is_lt).then_inc(route_steps.sem, 1)
                V.tensor_single_scalar(base[:], expert[:].rearrange("p j k -> p (j k)"), float(CAP), ALU.mult).then_inc(route_steps.sem, 1)
                V.tensor_tensor(top_shifted[:], top_shifted[:], exp_inv[:].unsqueeze(2).to_broadcast([P, G, TOPK]), ALU.mult).then_inc(route_steps.sem, 1)
                dve.wait_ge(route_steps.sem, route_steps.value(g, 22))
                V.tensor_tensor(pair_weight[:, bass.ds(g * (G * TOPK), G * TOPK)], top_shifted[:].rearrange("p j k -> p (j k)"),
                                     kept[:], ALU.mult).then_inc(route_steps.sem, 1)
                V.tensor_single_scalar(pair_rank[:, bass.ds(g * (G * TOPK), G * TOPK)], rank[:], float(CAP - 1), ALU.min).then_inc(route_steps.sem, 1)
                V.tensor_copy(pair_expert[:, bass.ds(g * (G * TOPK), G * TOPK)], expert[:].rearrange("p j k -> p (j k)")).then_inc(route_steps.sem, 1)
                V.tensor_tensor(slot[:], rank[:], base[:], ALU.add).then_inc(route_steps.sem, 1)
                V.tensor_scalar(kept[:], kept[:], -float(NONE), float(NONE), ALU.mult, ALU.add).then_inc(route_steps.sem, 1)
                dve.wait_ge(route_steps.sem, route_steps.value(g, 27))
                dve.wait_ge(scatter_over.sem, scatter_over.value(g, 0))
                V.tensor_tensor(scatter_to[:], slot[:], kept[:], ALU.add).then_inc(route_steps.sem, 1)
                V.tensor_copy(tokens[:], tokens_f[:]).then_inc(route_steps.sem, 1)
                dve.wait_ge(route_steps.sem, route_steps.value(g, 29))
                V.tensor_single_scalar(tokens_f[:], tokens_f[:], float(G * P), ALU.add).then_inc(route_steps.sem, 1)

            def shared_inner(g, c):
                dve.wait_ge(gate_done.sem, gate_done.value(g, c + 1))
                dve.wait_ge(hT_hi_done.sem, hT_hi_done.value(g, c))
                dve.wait_ge(hT_lo_done.sem, hT_lo_done.value(g, c))
                V.scalar_tensor_tensor(hT[:], gate[:], 1.0, S[:, 2 * (c % 2), :], ALU.add, ALU.mult).then_inc(h_steps.sem, 1)
                dve.wait_ge(h_steps.sem, h_steps.value(g, 2 * c + 1))
                V.scalar_tensor_tensor(hT[:], hT[:], 0.5, S[:, 2 * (c % 2) + 1, :], ALU.mult, ALU.mult).then_inc(h_steps.sem, 1)
                dve.wait_ge(hT_hi_done.sem, hT_hi_done.value(g, c + 1))
                low(hT_lo[:, c, :], hT[:], hT_hi[:, c, :]).then_inc(hT_lo_done.sem, 1)

            def shared_out(g, j):
                dve.wait_ge(down_done.sem, down_done.value(g, j + 1))
                dve.wait_ge(acc_stored[j % 2].sem, acc_stored[j % 2].value(g, 16 * (j // 2)))
                V.tensor_tensor(acc[:, j % 2, :], work[j % 2][:], x[:, j, :], ALU.add).then_inc(acc_done.sem, 1)

            def step(g):
                for n in range(G):
                    norm(g, n)
                    if n:
                        normed_low(g, n - 1)
                normed_low(g, G - 1)
                for j in range(G):
                    dve.wait_ge(v_done.sem, v_done.value(g, j + 1))
                    dve.wait_ge(mixed_done.sem, mixed_done.value(g, 0))
                    V.tensor_copy(v[:, j, :, 0:HD], work[j % 2][:].rearrange("p (h n) -> p h n", n=HD)).then_inc(v_read.sem, 1)
                maximum_and_shift(g, 0)
                for j in range(G):
                    if j + 1 < G:
                        maximum_and_shift(g, j + 1)
                    mix_out(g, j)
                    norm(g, G + j)
                    if j:
                        normed_low(g, G + j - 1)
                normed_low(g, 2 * G - 1)
                choose(g)
                shared_inner(g, 0)
                place(g)
                for c in range(1, CF):
                    shared_inner(g, c)
                for j in range(G):
                    shared_out(g, j)

            with dve.Fori(0, NG) as i:
                step(i)

        @block.tensor
        def _(pe):
            grant(pe, up_done, scored, mixed_done, down_done, turned, probs_turned)

            def turn_normed(g, n):
                j = n % G
                pe.wait_ge(norm_steps.sem, norm_steps.value(g, 3 * n + 3))
                pe.wait_ge(xnT_lo_done.sem, xnT_lo_done.value(g, n - 1))
                if n >= G:
                    pe.wait_ge(probsT_read.sem, probsT_read.value(g, 4 * (min(j + 1, G - 1) + 1)))
                for k in range(KD):
                    last = nc.tensor.transpose(turn[n % 2][:, k * P:(k + 1) * P], xn[:, 2 * (n // G) + j % 2, k * P:(k + 1) * P], ident[:])
                last.then_inc(turned.sem, 1)

            def tokens_of(j):
                return slice(j * P, (j + 1) * P)

            def project_qk(g, c):
                if c < 4:
                    pe.wait_ge(h_steps.sem, h_steps.value(g, 0))
                else:
                    pe.wait_ge(qk_read.sem, qk_read.value(g, c - 3))
                for k in range(KD):
                    cs = slice(c * P, (c + 1) * P)
                    last = product(nc, S[:, c % 4, :], (wqk[0][:, k, cs], wqk[1][:, k, cs]),
                                   (xnT_hi[:, k, :], xnT_lo[:, k, :]), k == 0, k == KD - 1)
                last.then_inc(qk_done.sem, 1)

            def from_tokens(out, j, a, w, ks, first=True):
                for k in range(ks):
                    last = product(nc, out, (a[0][:, k, tokens_of(j)], a[1][:, k, tokens_of(j)]), (w[0][:, k, :], w[1][:, k, :]), k == 0, k == ks - 1)
                return last

            def project_v(g, j):
                pe.wait_ge(acc_done.sem, acc_done.value(g, 0))
                if j >= 2:
                    pe.wait_ge(v_read.sem, v_read.value(g, j - 1))
                from_tokens(work[j % 2][:], j, (xnT_hi, xnT_lo), wv, KD).then_inc(v_done.sem, 1)

            def score(g, j):
                if j == 0:
                    pe.wait_ge(qk_read.sem, qk_read.value(g, CQ))
                else:
                    pe.wait_ge(shift_done.sem, shift_done.value(g, j))
                for h in range(H):
                    c, r = h // 4, h % 4
                    rows = slice(r * HD, (r + 1) * HD)
                    last = nc.tensor.matmul(S[:, r, c * P:(c + 1) * P], qkT[rows, c, tokens_of(j)], qkT[rows, CQ // 2 + c, tokens_of(j)],
                                            start=True, stop=True)
                last.then_inc(scored.sem, 1)

            def turn_probs(g, j):
                pe.wait_ge(exp_done.sem, exp_done.value(g, j + 1))
                pe.wait_ge(xnT_lo_done.sem, xnT_lo_done.value(g, G if j == 0 else G + max(0, j - 1)))
                for q in range(4):
                    pe.wait_ge(probsT_read.sem, probsT_read.value(g, 4 * j + q - 1))
                    for t in range(4):
                        last = nc.tensor.transpose(turn[q % 2][:, t * P:(t + 1) * P], probs[:, 4 * q + t, :], ident[:])
                    last.then_inc(probs_turned.sem, 1)

            def mix(g, j):
                pe.wait_ge(probsT_read.sem, probsT_read.value(g, 4 * j + 4))
                pe.wait_ge(v_read.sem, v_read.value(g, G))
                pe.wait_ge(mix_steps.sem, mix_steps.value(g, 6 * j))
                for h in range(H):
                    last = nc.tensor.matmul(work[h // 8][:, (h % 8) * VW:(h % 8 + 1) * VW], probsT[:, h, :], v[:, j, h, :], start=True, stop=True)
                last.then_inc(mixed_done.sem, 1)

            def gate_logits(g):
                pe.wait_ge(mix_steps.sem, mix_steps.value(g, 6 * G))
                for j in range(G):
                    last = from_tokens(work[0][:, j * E:(j + 1) * E], j, (xnT_hi, xnT_lo), wg, KD)
                last.then_inc(logits_done.sem, 1)

            def rank_pairs(g):
                pe.wait_ge(route_steps.sem, route_steps.value(g, R_TAKEN))
                for j in range(G):
                    out = work[1][:, j * E:(j + 1) * E]
                    nc.tensor.matmul(out, before[:], taken[:, j, :], start=True, stop=False)
                    for i in range(j):
                        nc.tensor.matmul(out, ones[:], taken[:, i, :], start=False, stop=False)
                    last = nc.tensor.matmul(out, ones[:], counted[:], start=False, stop=True)
                last.then_inc(ranks_done.sem, 1)

            def shared_up(g, c):
                if c < 2:
                    pe.wait_ge(shift_done.sem, shift_done.value(g, G))
                else:
                    pe.wait_ge(h_steps.sem, h_steps.value(g, 2 * (c - 1)))
                for part in range(2):
                    cs = slice((part * CF + c) * P, (part * CF + c + 1) * P)
                    for k in range(KD):
                        last = product(nc, S[:, 2 * (c % 2) + part, :], (ws13[0][:, k, cs], ws13[1][:, k, cs]),
                                       (xnT_hi[:, k, :], xnT_lo[:, k, :]), k == 0, k == KD - 1)
                last.then_inc(up_done.sem, 1)

            def shared_down(g, j):
                pe.wait_ge(hT_lo_done.sem, hT_lo_done.value(g, CF))
                if j == 0:
                    pe.wait_ge(logits_steps.sem, logits_steps.value(g, 1))
                elif j == 1:
                    pe.wait_ge(route_steps.sem, route_steps.value(g, R_RANKED))
                else:
                    pe.wait_ge(acc_done.sem, acc_done.value(g, j - 1))
                from_tokens(work[j % 2][:], j, (hT_hi, hT_lo), ws2, CF).then_inc(down_done.sem, 1)

            def step(g):
                for n in range(G):
                    turn_normed(g, n)
                pe.wait_ge(xnT_lo_done.sem, xnT_lo_done.value(g, G))
                for c in range(CQ):
                    project_qk(g, c)
                for j in range(G):
                    project_v(g, j)
                score(g, 0)
                for j in range(G):
                    if j + 1 < G:
                        score(g, j + 1)
                    turn_probs(g, j)
                    mix(g, j)
                    if j:
                        turn_normed(g, G + j - 1)
                turn_normed(g, 2 * G - 1)
                pe.wait_ge(xnT_lo_done.sem, xnT_lo_done.value(g, 2 * G))
                gate_logits(g)
                shared_up(g, 0)
                rank_pairs(g)
                for c in range(1, CF):
                    shared_up(g, c)
                for j in range(G):
                    shared_down(g, j)

            pe.wait_ge(const_landed, 16 * 3)
            pe.wait_ge(setup, 1)
            pe.wait_ge(w_lo, NW + 1)
            with pe.Fori(0, NG) as i:
                step(i)


HE = 256
KH = HE // P
UNROLL = 4


def experts(nc, normed, token_of_slot, W_expert, expert_count, pair_rank, pair_expert, gather_rows,
            ident_in, before_in, y_rows):
    W13 = KD * 2 * HE
    WE = W13 + KH * D
    PAIRS = 16
    with ExitStack() as stack:
        m = Memory(nc, stack, "ex")
        weights = m.sb("weights", [P, UNROLL, WE])
        pair_token = m.sb("pair_token", [P, UNROLL, 1], I32)
        xg = m.sb("xg", [P, UNROLL, D])
        xgT = m.sb("xgT", [P, 2, D])
        gate = m.sb("gate", [P, 2, HE])
        h = m.sb("h", [P, 2, HE])
        hT = m.sb("hT", [P, 2, HE])
        y = m.sb("y", [P, UNROLL, D])
        ident = m.sb("ident", [P, P])
        before = m.sb("before", [P, P])
        ones = m.sb("ones", [P, 1])
        thresholds = m.sb("thresholds", [E, CAP // P])
        over = m.sb("over", [E, CAP // P])
        count = m.sb("count", [E, 1])
        blocks = m.sb("blocks", [E, 1])
        first_block = m.sb("first_block", [E, 1])
        end_block = m.sb("end_block", [E, 1])
        expert_id = m.sb("expert_id", [E, 1])
        expert_row = m.sb("expert_row", [E, 1])
        first_row = m.sb("first_row", [E, 1])
        block_id = m.sb("block_id", [E, NBLOCKS])
        block_row = m.sb("block_row", [E, NBLOCKS])
        started = m.sb("started", [E, NBLOCKS])
        parts = m.sb("parts", [E, 3, NBLOCKS])
        spare_row = m.sb("spare_row", [1, NBLOCKS])
        unused = m.sb("unused", [1, NBLOCKS])
        blocks_wide = m.sb("blocks_wide", [E, P])
        first_of = m.sb("first_of", [P, E])
        iota_e = m.sb("iota_e", [P, E])
        one_hot = m.sb("one_hot", [P, PAIRS, E])
        pair_first = m.sb("pair_first", [P, PAIRS])
        table = m.sb("table", [1, 2, NBLOCKS], I32)

        turn = [m.ps("turn0", [P, BANK]), m.ps("turn1", [P, BANK])]
        up = [m.ps("up0", [P, BANK]), m.ps("up1", [P, BANK])]
        hturn = [m.ps("hturn0", [P, BANK]), m.ps("hturn1", [P, BANK])]
        down = [m.ps("down0", [P, BANK]), m.ps("down1", [P, BANK])]

        const_landed = m.sem("const_landed")
        setup = m.sem("setup")
        table_pe = m.sem("table_pe")
        table_steps = m.sem("table_steps")
        place_steps = m.sem("place_steps")
        weights_landed = [m.tally(f"weights_landed{u}", 16) for u in range(UNROLL)]
        pairs_landed = [m.tally(f"pairs_landed{u}", 16) for u in range(UNROLL)]
        gathered = [m.tally(f"gathered{u}", 16) for u in range(UNROLL)]
        stored = [m.tally(f"stored{u}", 16, 1) for u in range(UNROLL)]
        turned = m.tally("turned", 1, UNROLL)
        xgT_done = m.tally("xgT_done", 1)
        up_done = m.tally("up_done", 1)
        gate_done = m.tally("gate_done", 1)
        h_steps = m.tally("h_steps", 2, 4)
        h_turned = m.tally("h_turned", 1, 2)
        hT_done = m.tally("hT_done", 1, 2)
        down_done = m.tally("down_done", 1, UNROLL)
        y_done = m.tally("y_done", 1, 2)
        block = stack.enter_context(nc.Block())

        def loop(eng, step, ahead):
            with eng.Fori(0, NBLOCKS // UNROLL - 1) as i:
                for u in range(UNROLL):
                    step(i * UNROLL + u, u, i, 0)
            for u in range(UNROLL):
                j = NBLOCKS - UNROLL + u
                step(j, u, NBLOCKS // UNROLL - 1, max(0, j + ahead - NBLOCKS + 1))

        @block.sync
        def _(sp):
            grant(sp, *stored)
            sp.dma_start(ident[:], ident_in).then_inc(const_landed, 16)
            sp.dma_start(before[:], before_in).then_inc(const_landed, 16)
            sp.wait_ge(table_steps, 15)

            def fetch(j, u, i):
                row = sp.value_load(table[0:1, 0, bass.ds(j, 1)], min_val=0, max_val=ROWS - P)
                expert = sp.value_load(table[0:1, 1, bass.ds(j, 1)], min_val=0, max_val=E - 1)
                sp.wait_ge(turned.sem, turned.value(j, 1 - UNROLL))
                sp.nop(nofuse=True)
                sp.dma_start(pair_token[:, u, :], token_of_slot[bass.ds(row, P), :]).then_inc(pairs_landed[u].sem, 16)
                sp.wait_ge(down_done.sem, down_done.value(j, 1 - UNROLL))
                sp.nop(nofuse=True)
                sp.dma_start(weights[:, u, :], W_expert[bass.ds(expert, 1)].rearrange("one p n -> p (one n)")).then_inc(weights_landed[u].sem, 16)

            def store(j, u):
                sp.wait_ge(y_done.sem, y_done.value(j, 1))
                sp.nop(nofuse=True)
                sp.dma_start(y_rows[bass.ds(j * P, P), :], y[:, u, :]).then_inc(stored[u].sem, 16)

            AHEAD = UNROLL - 1
            for j in range(AHEAD):
                fetch(j, j, 0)

            def step(j, u, i, late):
                if late == 0:
                    v = (u + AHEAD) % UNROLL
                    fetch(j + AHEAD, v, i)
                store(j, u)

            loop(sp, step, AHEAD)
            for u in range(UNROLL):
                sp.wait_ge(stored[u].sem, stored[u].value(NBLOCKS // UNROLL - 1, 16))
                sp.nop(nofuse=True)

        @block.gpsimd
        def _(pool):
            nc.gpsimd.memset(ones[:], 1.0)
            nc.gpsimd.iota(thresholds[:], pattern=[[P, CAP // P]], base=0, channel_multiplier=0, allow_small_or_imprecise_dtypes=True)
            nc.gpsimd.iota(expert_id[:], pattern=[[0, 1]], base=0, channel_multiplier=1, allow_small_or_imprecise_dtypes=True)
            nc.gpsimd.iota(expert_row[:], pattern=[[0, 1]], base=0, channel_multiplier=CAP, allow_small_or_imprecise_dtypes=True)
            nc.gpsimd.iota(iota_e[:], pattern=[[1, E]], base=0, channel_multiplier=0, allow_small_or_imprecise_dtypes=True)
            nc.gpsimd.iota(block_id[:], pattern=[[1, NBLOCKS]], base=0, channel_multiplier=0, allow_small_or_imprecise_dtypes=True)
            nc.gpsimd.iota(block_row[:], pattern=[[P, NBLOCKS]], base=0, channel_multiplier=0, allow_small_or_imprecise_dtypes=True)
            nc.gpsimd.iota(spare_row[:], pattern=[[P, NBLOCKS]], base=NONE, channel_multiplier=0, allow_small_or_imprecise_dtypes=True).then_inc(setup, 1)

            def step(j, u, i, late):
                pool.wait_ge(pairs_landed[u].sem, pairs_landed[u].value(i, 16))
                pool.nop(nofuse=True)
                pool.wait_ge(turned.sem, turned.value(j, 1 - UNROLL))
                pool.nop(nofuse=True)
                pool.indirect_dma_start(xg[:, u, :], None, normed, bass.IndirectOffsetOnAxis(ap=pair_token[:, u, :], axis=0))\
                    .then_inc(gathered[u].sem, 16)

            loop(pool, step, 0)

        @block.scalar
        def _(act):
            grant(act, y_done, hT_done)

            def step(j, u, i, late):
                b = u % 2
                act.wait_ge(up_done.sem, up_done.value(j, 1))
                act.wait_ge(h_steps.sem, h_steps.value(j, -2))
                nc.scalar.activation(gate[:, b, :], up[b][:, 0:HE], ACT.Tanh, scale=0.5).then_inc(gate_done.sem, 1)
                act.wait_ge(h_turned.sem, h_turned.value(j, 1))
                act.wait_ge(down_done.sem, down_done.value(j, -1))
                nc.scalar.activation(hT[:, b, :], hturn[b][:, 0:HE], ACT.Copy).then_inc(hT_done.sem, 1)
                act.wait_ge(down_done.sem, down_done.value(j, 1))
                act.wait_ge(stored[u].sem, stored[u].value(i, 0))
                nc.scalar.activation(y[:, u, :], down[b][:], ACT.Copy).then_inc(y_done.sem, 1)

            loop(act, step, 0)

        @block.vector
        def _(dve):
            V = nc.vector
            grant(dve, h_steps)
            dve.wait_ge(setup, 1)
            dve.wait_ge(table_pe, 1)
            V.tensor_copy(count[:], up[0][0:E, 0:1]).then_inc(table_steps, 1)
            dve.wait_ge(table_steps, 1)
            V.tensor_scalar(over[:], thresholds[:], count[:], None, ALU.is_lt).then_inc(table_steps, 1)
            dve.wait_ge(table_steps, 2)
            V.reduce_sum(blocks[:], over[:], AX.X).then_inc(table_steps, 1)
            dve.wait_ge(table_steps, 3)
            V.tensor_copy(blocks_wide[:], blocks[:].to_broadcast([E, P])).then_inc(table_steps, 1)
            dve.wait_ge(table_pe, 2)
            V.tensor_copy(first_block[:], up[1][0:E, 0:1]).then_inc(table_steps, 1)
            dve.wait_ge(table_steps, 5)
            V.tensor_tensor(end_block[:], first_block[:], blocks[:], ALU.add).then_inc(table_steps, 1)
            V.scalar_tensor_tensor(first_row[:], first_block[:], -float(P), expert_row[:], ALU.mult, ALU.add).then_inc(table_steps, 1)
            V.tensor_scalar(started[:], block_id[:], first_block[:], None, ALU.is_ge).then_inc(table_steps, 1)
            dve.wait_ge(table_steps, 8)
            V.scalar_tensor_tensor(parts[:, 2, :], block_id[:], end_block[:], started[:], ALU.is_lt, ALU.mult).then_inc(table_steps, 1)
            dve.wait_ge(table_steps, 9)
            V.scalar_tensor_tensor(parts[:, 0, :], block_row[:], first_row[:], parts[:, 2, :], ALU.add, ALU.mult).then_inc(table_steps, 1)
            V.tensor_scalar(parts[:, 1, :], parts[:, 2, :], expert_id[:], None, ALU.mult).then_inc(table_steps, 1)
            dve.wait_ge(table_pe, 3)
            V.tensor_scalar(unused[:], up[0][0:1, 2 * NBLOCKS:3 * NBLOCKS], -1.0, 1.0, ALU.mult, ALU.add).then_inc(table_steps, 1)
            dve.wait_ge(table_steps, 12)
            V.tensor_tensor(unused[:], unused[:], spare_row[:], ALU.mult).then_inc(table_steps, 1)
            dve.wait_ge(table_steps, 13)
            V.tensor_tensor(table[:, 0, :], unused[:], up[0][0:1, 0:NBLOCKS], ALU.add).then_inc(table_steps, 1)
            V.tensor_copy(table[:, 1, :], up[0][0:1, NBLOCKS:2 * NBLOCKS]).then_inc(table_steps, 1)

            V.tensor_single_scalar(first_of[:], down[0][:, 0:E], float(P), ALU.mult).then_inc(place_steps, 1)
            for n in range(B * TOPK // PAIRS):
                ps = slice(n * PAIRS, (n + 1) * PAIRS)
                dve.wait_ge(place_steps, 4 * n + 1)
                V.tensor_tensor(one_hot[:], iota_e[:].unsqueeze(1).to_broadcast([P, PAIRS, E]),
                                pair_expert[:, ps].unsqueeze(2).to_broadcast([P, PAIRS, E]), ALU.is_equal).then_inc(place_steps, 1)
                dve.wait_ge(place_steps, 4 * n + 2)
                V.tensor_tensor(one_hot[:], one_hot[:], first_of[:].unsqueeze(1).to_broadcast([P, PAIRS, E]),
                                ALU.mult).then_inc(place_steps, 1)
                dve.wait_ge(place_steps, 4 * n + 3)
                V.reduce_sum(pair_first[:], one_hot[:], AX.X).then_inc(place_steps, 1)
                dve.wait_ge(place_steps, 4 * n + 4)
                V.tensor_tensor(gather_rows[:, ps], pair_first[:], pair_rank[:, ps], ALU.add).then_inc(place_steps, 1)

            def x_turned(j, b):
                dve.wait_ge(turned.sem, turned.value(j, 1))
                dve.wait_ge(up_done.sem, up_done.value(j, -1))
                V.tensor_copy(xgT[:, b, :], turn[b][:]).then_inc(xgT_done.sem, 1)

            for j in range(2):
                dve.wait_ge(turned.sem, turned.value(j, 1))
                V.tensor_copy(xgT[:, j, :], turn[j][:]).then_inc(xgT_done.sem, 1)

            def step(j, u, i, late):
                b = u % 2
                dve.wait_ge(gate_done.sem, gate_done.value(j, 1))
                dve.wait_ge(h_turned.sem, h_turned.value(j, -1))
                V.scalar_tensor_tensor(h[:, b, :], gate[:, b, :], 1.0, up[b][:, 0:HE], ALU.add, ALU.mult).then_inc(h_steps.sem, 1)
                dve.wait_ge(h_steps.sem, h_steps.value(j, 1))
                V.scalar_tensor_tensor(h[:, b, :], h[:, b, :], 0.5, up[b][:, HE:2 * HE], ALU.mult, ALU.mult).then_inc(h_steps.sem, 1)
                if late == 0:
                    x_turned(j + 2, b)

            loop(dve, step, 2)

        @block.tensor
        def _(pe):
            grant(pe, turned, h_turned, down_done)

            def turn_x(j, u, b, i):
                pe.wait_ge(gathered[u].sem, gathered[u].value(i, 16))
                pe.wait_ge(xgT_done.sem, xgT_done.value(j, -1))
                for k in range(KD):
                    last = nc.tensor.transpose(turn[b][:, k * P:(k + 1) * P], xg[:, u, k * P:(k + 1) * P], ident[:])
                last.then_inc(turned.sem, 1)

            def go_up(j, u, b, i):
                pe.wait_ge(xgT_done.sem, xgT_done.value(j, 1))
                pe.wait_ge(weights_landed[u].sem, weights_landed[u].value(i, 16))
                pe.wait_ge(h_steps.sem, h_steps.value(j, -2))
                for k in range(KD):
                    last = nc.tensor.matmul(up[b][:], xgT[:, b, k * P:(k + 1) * P], weights[:, u, k * 2 * HE:(k + 1) * 2 * HE],
                                            start=k == 0, stop=k == KD - 1)
                last.then_inc(up_done.sem, 1)

            pe.wait_ge(const_landed, 32)
            pe.wait_ge(setup, 1)
            nc.tensor.matmul(up[0][0:E, 0:1], expert_count[:], ones[:], start=True, stop=True).then_inc(table_pe, 1)
            pe.wait_ge(table_steps, 4)
            nc.tensor.matmul(down[0][:, 0:E], blocks_wide[:], before[0:E, 0:E], start=True, stop=True)
            nc.tensor.matmul(up[1][0:E, 0:1], before[0:E, 0:E], blocks[:], start=True, stop=True).then_inc(table_pe, 1)
            pe.wait_ge(table_steps, 11)
            nc.tensor.matmul(up[0][0:1, 0:3 * NBLOCKS], ones[0:E, :], parts[:].rearrange("e a j -> e (a j)"), start=True, stop=True).then_inc(table_pe, 1)
            pe.wait_ge(table_steps, 15)
            pe.wait_ge(place_steps, 1)
            for j in range(2):
                pe.wait_ge(gathered[j].sem, 16)
                for k in range(KD):
                    last = nc.tensor.transpose(turn[j][:, k * P:(k + 1) * P], xg[:, j, k * P:(k + 1) * P], ident[:])
                last.then_inc(turned.sem, 1)
            go_up(0, 0, 0, 0)

            def step(j, u, i, late):
                b = u % 2
                if late < 2:
                    v = (u + 1) % UNROLL
                    go_up(j + 1, v, v % 2, i + (u + 1) // UNROLL)
                if late < 1:
                    v = (u + 2) % UNROLL
                    turn_x(j + 2, v, b, i + (u + 2) // UNROLL)
                pe.wait_ge(h_steps.sem, h_steps.value(j, 2))
                pe.wait_ge(hT_done.sem, hT_done.value(j, -1))
                for k in range(KH):
                    last = nc.tensor.transpose(hturn[b][:, k * P:(k + 1) * P], h[:, b, k * P:(k + 1) * P], ident[:])
                last.then_inc(h_turned.sem, 1)
                pe.wait_ge(hT_done.sem, hT_done.value(j, 1))
                pe.wait_ge(y_done.sem, y_done.value(j, -1))
                for k in range(KH):
                    last = nc.tensor.matmul(down[b][:], hT[:, b, k * P:(k + 1) * P], weights[:, u, W13 + k * D:W13 + (k + 1) * D],
                                            start=k == 0, stop=k == KH - 1)
                last.then_inc(down_done.sem, 1)

            loop(pe, step, 2)


def combine(nc, acc_in, y_rows, gather_rows, pair_weight, out):
    with ExitStack() as stack:
        m = Memory(nc, stack, "co")
        acc = m.sb("acc", [P, 2, D])
        rows = m.sb("rows", [P, 2, TOPK], I32)
        weight = m.sb("weight", [P, 2, TOPK])
        y = m.sb("y", [P, 2, TOPK, D])
        acc_landed = [m.tally(f"acc_landed{s}", 16) for s in range(2)]
        y_landed = [[m.tally(f"y_landed{s}{k}", 16) for k in range(TOPK)] for s in range(2)]
        rows_done = m.tally("rows_done", 2)
        sum_steps = m.tally("sum_steps", TOPK)
        stored = [m.tally(f"stored{s}", 16) for s in range(2)]
        block = stack.enter_context(nc.Block())

        @block.sync
        def _(sp):
            for s in range(2):
                sp.dma_start(acc[:, s, :], acc_in[s]).then_inc(acc_landed[s].sem, 16)

            def step(b, s, i, more):
                sp.wait_ge(sum_steps.sem, sum_steps.value(b, TOPK))
                sp.nop(nofuse=True)
                sp.dma_start(out[b], acc[:, s, :]).then_inc(stored[s].sem, 16)
                if more:
                    sp.wait_ge(stored[s].sem, stored[s].value(i, 16))
                    sp.nop(nofuse=True)
                    sp.dma_start(acc[:, s, :], acc_in[b + 2]).then_inc(acc_landed[s].sem, 16)

            with sp.Fori(0, B // 2 - 1) as i:
                for s in range(2):
                    step(i * 2 + s, s, i, True)
            for s in range(2):
                step(B - 2 + s, s, B // 2 - 1, False)
            for s in range(2):
                sp.wait_ge(stored[s].sem, stored[s].value(B // 2 - 1, 16))
                sp.nop(nofuse=True)

        @block.gpsimd
        def _(pool):
            with pool.Fori(0, B // 2) as i:
                for s in range(2):
                    pool.wait_ge(rows_done.sem, rows_done.value(i * 2 + s, 1))
                    pool.nop(nofuse=True)
                    for k in range(TOPK):
                        pool.indirect_dma_start(y[:, s, k, :], None, y_rows, bass.IndirectOffsetOnAxis(ap=rows[:, s, k:k + 1], axis=0))\
                            .then_inc(y_landed[s][k].sem, 16)

        @block.vector
        def _(dve):
            V = nc.vector

            def numbers(b, s):
                V.tensor_copy(rows[:, s, :], gather_rows[:, bass.ds(b * TOPK, TOPK)]).then_inc(rows_done.sem, 1)
                V.tensor_copy(weight[:, s, :], pair_weight[:, bass.ds(b * TOPK, TOPK)]).then_inc(rows_done.sem, 1)

            for s in range(2):
                numbers(s, s)

            def step(b, s, i, more):
                dve.wait_ge(acc_landed[s].sem, acc_landed[s].value(i, 16))
                dve.wait_ge(rows_done.sem, rows_done.value(b, 2))
                for k in range(TOPK):
                    dve.wait_ge(y_landed[s][k].sem, y_landed[s][k].value(i, 16))
                    if k:
                        dve.wait_ge(sum_steps.sem, sum_steps.value(b, k))
                    V.scalar_tensor_tensor(acc[:, s, :], y[:, s, k, :], weight[:, s, k:k + 1], acc[:, s, :], ALU.mult, ALU.add)\
                        .then_inc(sum_steps.sem, 1)
                if more:
                    dve.wait_ge(sum_steps.sem, sum_steps.value(b, TOPK))
                    numbers(b + 2, s)

            with dve.Fori(0, B // 2 - 1) as i:
                for s in range(2):
                    step(i * 2 + s, s, i, True)
            for s in range(2):
                step(B - 2 + s, s, B // 2 - 1, False)


def build(nc, x, ctx_rows, ctx_cols, w_cq, w_c, w_q, b_cq, b_c, b_q, W_lT, b_l, W_qkT, W_vT, W_g, W_s13, W_s2, W_expert,
          ident, before, out):
    x1 = nc.dram_tensor("x1_rows", (B, P, D), F32).ap()
    normed = nc.dram_tensor("normed_rows", (B, P, D), F32).ap()
    acc = nc.dram_tensor("acc_rows", (B, P, D), F32).ap()
    token_of_slot = nc.dram_tensor("token_of_slot", (ROWS, 1), I32).ap()
    y_rows = nc.dram_tensor("y_rows", (NBLOCKS * P, D), F32).ap()
    cross_attention(nc, x, ctx_rows, ctx_cols, w_cq, w_c, w_q, b_cq, b_c, b_q, W_lT, b_l, ident, x1)
    with ExitStack() as stack:
        def kept(name, shape, dt):
            return stack.enter_context(nc.sbuf_tensor(name, shape, dt))

        pair_rank = kept("pair_rank", [P, B * TOPK], F32)
        pair_expert = kept("pair_expert", [P, B * TOPK], F32)
        pair_weight = kept("pair_weight", [P, B * TOPK], F32)
        gather_rows = kept("gather_rows", [P, B * TOPK], I32)
        expert_count = kept("expert_count", [P, E], F32)
        self_attention_and_routing(nc, x1, W_qkT, W_vT, W_g, W_s13, W_s2, ident, before, normed, acc,
                                   token_of_slot, pair_rank, pair_expert, pair_weight, expert_count)
        experts(nc, normed.rearrange("b p d -> (b p) d"), token_of_slot, W_expert, expert_count, pair_rank, pair_expert,
                gather_rows, ident, before, y_rows)
        combine(nc, acc, y_rows, gather_rows, pair_weight, out)


def kernel(x, ctx_1024, L0_xattn_w_cq, L0_xattn_b_cq, L0_xattn_w_c, L0_xattn_b_c, L0_xattn_w_q, L0_xattn_b_q,
           L0_xattn_W_l, L0_xattn_b_l, L0_attn_Wq, L0_attn_Wk, L0_attn_Wv, L0_ffn_Wg, L0_ffn_W1, L0_ffn_W2, L0_ffn_W3,
           L0_ffn_Ws1, L0_ffn_Ws2, L0_ffn_Ws3):
    import numpy as np
    import concourse.bacc as bacc
    from concourse.bass_utils import run_bass_kernel_spmd

    def blocks(w):
        w = np.asarray(w)
        return np.ascontiguousarray(w.reshape(-1, P, w.shape[1]).transpose(1, 0, 2))

    def expert_blocks(w):
        w = np.asarray(w)
        return w.reshape(E, -1, P, w.shape[2]).transpose(0, 2, 1, 3)

    ctx = np.asarray(ctx_1024)
    w13 = np.concatenate([expert_blocks(L0_ffn_W1), expert_blocks(L0_ffn_W3)], axis=3)
    arrays = {
        "x": np.asarray(x),
        "ctx_rows": np.ascontiguousarray(ctx).reshape(B, 8, P, CTX // 8 // P * D),
        "ctx_cols": np.ascontiguousarray(ctx.reshape(B, CTX // BANK, BANK, KD, P).transpose(0, 1, 4, 3, 2)).reshape(B, CTX // BANK, P, KD * BANK),
        "w_cq": np.ascontiguousarray(np.asarray(L0_xattn_w_cq).reshape(KD, P).T),
        "w_c": np.asarray(L0_xattn_w_c),
        "w_q": np.ascontiguousarray(np.asarray(L0_xattn_w_q).reshape(KD, P).T),
        "b_cq": np.asarray(L0_xattn_b_cq).reshape(1),
        "b_c": np.asarray(L0_xattn_b_c).reshape(1),
        "b_q": np.asarray(L0_xattn_b_q).reshape(1),
        "W_lT": blocks(np.asarray(L0_xattn_W_l).T),
        "b_l": np.asarray(L0_xattn_b_l),
        "W_qkT": blocks(np.concatenate([np.asarray(L0_attn_Wq).T, np.asarray(L0_attn_Wk).T], axis=1)),
        "W_vT": blocks(np.asarray(L0_attn_Wv).T),
        "W_g": blocks(L0_ffn_Wg),
        "W_s13": blocks(np.concatenate([np.asarray(L0_ffn_Ws1), np.asarray(L0_ffn_Ws3)], axis=1)),
        "W_s2": blocks(L0_ffn_Ws2),
        "W_expert": np.concatenate([w13.reshape(E, P, -1), expert_blocks(L0_ffn_W2).reshape(E, P, -1)], axis=2),
        "ident": np.eye(P, dtype=np.float32),
        "before": np.triu(np.ones((P, P), np.float32), 1),
    }
    nc = bacc.Bacc("TRN2", target_bir_lowering=False, num_devices=1)
    ins = [nc.dram_tensor(name, a.shape, F32, kind="ExternalInput").ap() for name, a in arrays.items()]
    out = nc.dram_tensor("out", (B, P, D), F32, kind="ExternalOutput").ap()
    build(nc, *ins, out)
    return run_bass_kernel_spmd(nc, [arrays], core_ids=[0]).results[0]["out"]
```

```python
from contextlib import ExitStack

import concourse.bass as bass
from concourse import mybir

ALU = mybir.AluOpType
ACT = mybir.ActivationFunctionType
AX = mybir.AxisListType
F32 = mybir.dt.float32
F32R = mybir.dt.float32r
I32 = mybir.dt.int32
U32 = mybir.dt.uint32
MAX_OVER_PARTITIONS = bass.bass_isa.ReduceOp.max

P = 128
B = 16
D = 512
KD = D // P
CTX = 2048
BANK = 512
EPS = 1e-5


class Tally:

    def __init__(self, sem, per, credit=0):
        self.sem, self.per, self.credit = sem, per, credit

    def value(self, batch, k):
        return batch * self.per + (self.credit + k)


def grant(eng, *tallies):
    for t in tallies:
        if t.credit:
            eng.sem_inc(t.sem, t.credit)


class Memory:

    def __init__(self, nc, stack, phase):
        self.nc, self.stack, self.phase = nc, stack, phase

    def sb(self, name, shape, dt=F32):
        return self.stack.enter_context(self.nc.sbuf_tensor(f"{self.phase}_{name}", shape, dt))

    def ps(self, name, shape):
        return self.stack.enter_context(self.nc.psum_tensor(f"{self.phase}_{name}", shape, F32))

    def sem(self, name):
        return self.stack.enter_context(self.nc.semaphore(f"{self.phase}_{name}"))

    def tally(self, name, per, credit=0):
        return Tally(self.sem(name), per, credit)


def product(nc, out, stationary, moving, first, last):
    (sh, sl), (mh, ml) = stationary, moving
    nc.tensor.matmul(out, sh, mh, start=first, stop=False)
    nc.tensor.matmul(out, sh, ml, start=False, stop=False)
    return nc.tensor.matmul(out, sl, mh, start=False, stop=last)


def cross_attention(nc, x, ctx_rows, ctx_cols, w_cq, w_c, w_q, b_cq, b_c, b_q, W_lT, b_l, ident_in, x1_out):
    QC = CTX // BANK
    RC = 8
    NJ = CTX // RC // P
    KH = KD // 2
    NU = 2 * QC
    UNIT = KH * BANK
    RAW = 4
    RING = 8
    KZ = 4 * KD

    with ExitStack() as stack:
        m = Memory(nc, stack, "xa")
        wl_hi = m.sb("wl_hi", [P, KZ, D], F32R)
        wl_lo = m.sb("wl_lo", [P, KZ, D], F32R)
        ident = m.sb("ident", [P, P])
        ones = m.sb("ones", [P, P])
        w_c_rows = m.sb("w_c_rows", [P, D])
        b_l_rows = m.sb("b_l_rows", [P, D])
        w_cq_col = m.sb("w_cq_col", [P, KD])
        w_q_col = m.sb("w_q_col", [P, KD])
        biases = m.sb("biases", [P, 3])
        bias_sum = m.sb("bias_sum", [P, 1])
        raw = m.sb("raw", [P, RAW, UNIT])
        ctx_hi = m.sb("ctx_hi", [P, RING, 2, D], F32R)
        ctx_lo = m.sb("ctx_lo", [P, RING, 2, D], F32R)
        x_in = m.sb("x_in", [P, D])
        x_bias = m.sb("x_bias", [P, D])
        c = m.sb("c", [P, D])
        stats = m.sb("stats", [P, 6])
        mean_var = m.sb("mean_var", [P, 2])
        eps_pow = m.sb("eps_pow", [P, 2])
        var_eps = m.sb("var_eps", [P, 1])
        rstd = m.sb("rstd", [P, 1])
        row_dot = m.sb("row_dot", [P, 1])
        cT = m.sb("cT", [P, D])
        cT_held = m.sb("cT_held", [P, D])
        cT_hi = m.sb("cT_hi", [P, D], F32R)
        cT_lo = m.sb("cT_lo", [P, D], F32R)
        cw = m.sb("cw", [P, D])
        cw_hi = m.sb("cw_hi", [P, D], F32R)
        cw_lo = m.sb("cw_lo", [P, D], F32R)
        chunk_max = m.sb("chunk_max", [P, QC])
        neg_max = m.sb("neg_max", [P, 1])
        probs = m.sb("probs", [P, CTX])
        chunk_sum = m.sb("chunk_sum", [P, QC])
        row_sum = m.sb("row_sum", [P, 1])
        row_inv = m.sb("row_inv", [P, 1])
        tok_max = m.sb("tok_max", [P, 1])
        all_max = m.sb("all_max", [P, 1])
        tok_exp = m.sb("tok_exp", [P, 1])
        tok_inv = m.sb("tok_inv", [P, 1])
        q2c = m.sb("q2c", [P, KD])
        probsT_hi = m.sb("probsT_hi", [P, 2, BANK], F32R)
        probsT_lo = m.sb("probsT_lo", [P, 2, BANK], F32R)
        cq2c = m.sb("cq2c", [P, D])
        cq2c_hi = m.sb("cq2c_hi", [P, D], F32R)
        cq2c_lo = m.sb("cq2c_lo", [P, D], F32R)
        c2q = m.sb("c2q", [P, D])
        c2qT_hi = m.sb("c2qT_hi", [P, D], F32R)
        c2qT_lo = m.sb("c2qT_lo", [P, D], F32R)
        cc2q, cc2q_hi, cc2q_lo = cq2c, cq2c_hi, cq2c_lo
        x1 = m.sb("x1", [P, D])

        scores = m.ps("scores", [P, QC, BANK])
        turn = [m.ps("turn0", [P, BANK]), m.ps("turn1", [P, BANK])]
        summed = m.ps("summed", [P, BANK])
        projected = m.ps("projected", [P, BANK])
        tok_sum_ps = scores[:, 0, 8:9]
        q2c_ps = scores[:, 0, 0:KD]

        const_landed = m.sem("const_landed")
        ones_done = m.sem("ones_done")
        bias_done = m.sem("bias_done")
        weight_landed = [m.sem(f"weight_landed{s}") for s in range(RAW)]
        weight_hi = m.sem("weight_hi")
        weight_lo = m.sem("weight_lo")
        x_landed = m.tally("x_landed", 16)
        landed = [m.tally(f"landed{s}", 16 * 2 * NU // RAW) for s in range(RAW)]
        hi_done = m.tally("hi_done", 2 * NU)
        lo_done = m.tally("lo_done", 2 * NU, RAW)
        norm_steps = m.tally("norm_steps", 4)
        rstd_steps = m.tally("rstd_steps", 2)
        c_turned = m.tally("c_turned", 1)
        cT_done = m.tally("cT_done", 1)
        cw_done = m.tally("cw_done", KD)
        cT_hi_done = m.tally("cT_hi_done", 1)
        cT_lo_done = m.tally("cT_lo_done", 1)
        cw_hi_done = m.tally("cw_hi_done", 1)
        cw_lo_done = m.tally("cw_lo_done", 1)
        scored = m.tally("scored", QC, QC)
        max_done = m.tally("max_done", QC + 1)
        tok_max_done = m.tally("tok_max_done", 1)
        all_max_done = m.tally("all_max_done", 1)
        exp_done = m.tally("exp_done", QC)
        tok_exp_done = m.tally("tok_exp_done", 1)
        sum_steps = m.tally("sum_steps", 2, 1)
        probs_turned = m.tally("probs_turned", QC, 1)
        probsT_hi_done = m.tally("probsT_hi_done", QC)
        probsT_lo_done = m.tally("probsT_lo_done", QC, QC)
        q2c_summed = m.tally("q2c_summed", 1, 1)
        q2c_steps = m.tally("q2c_steps", 2 + KD)
        cq2c_hi_done = m.tally("cq2c_hi_done", 1)
        cq2c_lo_done = m.tally("cq2c_lo_done", 1)
        held = m.tally("held", 1)
        gathered = m.tally("gathered", QC, QC)
        c_projected = m.tally("c_projected", 2, 2)
        c2q_done = m.tally("c2q_done", 1, 1)
        c2q_turned = m.tally("c2q_turned", 1)
        c2qT_hi_done = m.tally("c2qT_hi_done", 1)
        c2qT_lo_done = m.tally("c2qT_lo_done", 1, 1)
        cc2q_done = m.tally("cc2q_done", 1, 1)
        cc2q_hi_done = m.tally("cc2q_hi_done", 1)
        cc2q_lo_done = m.tally("cc2q_lo_done", 1)
        z_done = m.tally("z_done", 1, 1)
        x1_done = m.tally("x1_done", 1, 1)
        x_bias_done = m.tally("x_bias_done", 1, 1)
        x1_stored = m.tally("x1_stored", 16, 1)
        block = stack.enter_context(nc.Block())

        @block.sync
        def _(sp):
            grant(sp, x1_stored)
            consts = [(ident[:], ident_in), (w_c_rows[:], w_c[None, :].to_broadcast([P, D])),
                      (b_l_rows[:], b_l[None, :].to_broadcast([P, D])),
                      (biases[:, 0:1], b_cq[None, :].to_broadcast([P, 1])),
                      (biases[:, 1:2], b_c[None, :].to_broadcast([P, 1])),
                      (biases[:, 2:3], b_q[None, :].to_broadcast([P, 1]))]
            sp.dma_start(x_in[:], x[0]).then_inc(x_landed.sem, 16)
            for dst, src in consts:
                sp.dma_start(dst, src).then_inc(const_landed, 16)
            sp.dma_start(w_cq_col[:], w_cq).then_inc(const_landed, 16)
            sp.dma_start(w_q_col[:], w_q).then_inc(const_landed, 16)

            def load_x(b):
                sp.wait_ge(x_bias_done.sem, x_bias_done.value(b, 0))
                sp.nop(nofuse=True)
                sp.dma_start(x_in[:], x[b]).then_inc(x_landed.sem, 16)

            def load_cols(b, u):
                sp.wait_ge(lo_done.sem, lo_done.value(b, u - RAW + 1))
                sp.nop(nofuse=True)
                sp.dma_start(raw[:, u % RAW, :], ctx_cols[b, u // 2, :, (u % 2) * UNIT:(u % 2 + 1) * UNIT]
                             ).then_inc(landed[u % RAW].sem, 16)

            def load_rows(b, h):
                sp.wait_ge(lo_done.sem, lo_done.value(b, NU + h - RAW + 1))
                sp.nop(nofuse=True)
                sp.dma_start(raw[:, h % RAW, :], ctx_rows[b, h]).then_inc(landed[h % RAW].sem, 16)

            for u in range(NU):
                load_cols(0, u)
            for w in range(KZ // NJ):
                if w < RAW:
                    sp.wait_ge(lo_done.sem, lo_done.value(0, NU - RAW + w + 1))
                else:
                    sp.wait_ge(weight_lo, w - RAW + 1)
                sp.dma_start(raw[:, w % RAW, :].rearrange("p (j d) -> p j d", j=NJ),
                             W_lT[:, w * NJ:(w + 1) * NJ, :]).then_inc(weight_landed[w % RAW], 16)
            for h in range(NU):
                if h < RAW:
                    sp.wait_ge(weight_lo, KZ // NJ - RAW + h + 1)
                load_rows(0, h)

            load_cols(1, 0)
            load_cols(1, 1)
            load_x(1)
            load_cols(1, 2)
            load_cols(1, 3)

            def step(b, more):
                if more >= 1:
                    for u in range(RAW, NU):
                        load_cols(b + 1, u)
                    for h in range(NU):
                        load_rows(b + 1, h)
                if more >= 2:
                    load_cols(b + 2, 0)
                    load_cols(b + 2, 1)
                sp.wait_ge(x1_done.sem, x1_done.value(b, 1))
                sp.nop(nofuse=True)
                sp.dma_start(x1_out[b], x1[:]).then_inc(x1_stored.sem, 16)
                if more >= 2:
                    load_x(b + 2)
                    load_cols(b + 2, 2)
                    load_cols(b + 2, 3)

            with sp.Fori(0, B - 2) as i:
                step(i, 2)
            step(B - 2, 1)
            step(B - 1, 0)
            sp.wait_ge(x1_stored.sem, x1_stored.value(B - 1, 16))

        @block.gpsimd
        def _(pool):
            nc.gpsimd.memset(eps_pow[:, 0:1], EPS)
            nc.gpsimd.memset(eps_pow[:, 1:2], -0.5)
            nc.gpsimd.memset(ones[:], 1.0).then_inc(ones_done, 1)
            pool.wait_ge(ones_done, 1)

            def inverse_spread(b):
                pool.wait_ge(norm_steps.sem, norm_steps.value(b, 2))
                pool.nop(nofuse=True)
                nc.gpsimd.tensor_tensor(var_eps[:], mean_var[:, 1:2], eps_pow[:, 0:1], ALU.add).then_inc(rstd_steps.sem, 1)
                pool.wait_ge(rstd_steps.sem, rstd_steps.value(b, 1))
                pool.nop(nofuse=True)
                nc.gpsimd.tensor_tensor(rstd[:], var_eps[:], eps_pow[:, 1:2], ALU.pow).then_inc(rstd_steps.sem, 1)

            def token_maximum(b):
                pool.wait_ge(tok_max_done.sem, tok_max_done.value(b, 1))
                pool.nop(nofuse=True)
                nc.gpsimd.partition_all_reduce(all_max[:], tok_max[:], P, MAX_OVER_PARTITIONS).then_inc(all_max_done.sem, 1)

            def x_plus_bias(b):
                pool.wait_ge(x_landed.sem, x_landed.value(b, 16))
                pool.wait_ge(x1_done.sem, x1_done.value(b, 0))
                pool.nop(nofuse=True)
                nc.gpsimd.tensor_tensor(x_bias[:], x_in[:], b_l_rows[:], ALU.add).then_inc(x_bias_done.sem, 1)

            def hold(b):
                pool.wait_ge(cT_done.sem, cT_done.value(b, 1))
                pool.nop(nofuse=True)
                nc.gpsimd.tensor_copy(cT_held[:], cT[:]).then_inc(held.sem, 1)

            def token_part_low(b):
                pool.wait_ge(cq2c_hi_done.sem, cq2c_hi_done.value(b, 1))
                pool.nop(nofuse=True)
                nc.gpsimd.tensor_tensor(cq2c_lo[:], cq2c[:], cq2c_hi[:].bitcast(F32), ALU.subtract).then_inc(cq2c_lo_done.sem, 1)

            def normed_low(b):
                pool.wait_ge(cT_hi_done.sem, cT_hi_done.value(b, 1))
                pool.nop(nofuse=True)
                nc.gpsimd.tensor_tensor(cT_lo[:], cT[:], cT_hi[:].bitcast(F32), ALU.subtract).then_inc(cT_lo_done.sem, 1)

            grant(pool, x_bias_done)
            pool.wait_ge(const_landed, 16 * 8)
            inverse_spread(0)
            normed_low(0)

            def step(b, more):
                token_maximum(b)
                x_plus_bias(b)
                hold(b)
                if more:
                    inverse_spread(b + 1)
                token_part_low(b)
                if more:
                    normed_low(b + 1)

            with pool.Fori(0, B - 1) as i:
                step(i, True)
            step(B - 1, False)

        @block.scalar
        def _(act):
            def high(out, src):
                return nc.scalar.activation(out, src, ACT.Copy)

            def cols_high(b, u):
                act.wait_ge(landed[u % RAW].sem, landed[u % RAW].value(b, 16 * (u // RAW + 1)))
                act.wait_ge(gathered.sem, gathered.value(b, u // 2 + 1 - QC))
                high(ctx_hi[:, u].rearrange("p j d -> p (j d)"), raw[:, u % RAW, :]).then_inc(hi_done.sem, 1)

            def rows_high(b, h):
                act.wait_ge(landed[h % RAW].sem, landed[h % RAW].value(b, 16 * ((NU + h) // RAW + 1)))
                act.wait_ge(scored.sem, scored.value(b, h // 2 + 1))
                high(ctx_hi[:, h].rearrange("p j d -> p (j d)"), raw[:, h % RAW, :]).then_inc(hi_done.sem, 1)

            def exps(b):
                act.wait_ge(max_done.sem, max_done.value(b, QC + 1))
                act.wait_ge(sum_steps.sem, sum_steps.value(b, 0))
                act.wait_ge(probs_turned.sem, probs_turned.value(b, 0))
                for q in range(QC):
                    nc.scalar.activation(probs[:, q * BANK:(q + 1) * BANK], scores[:, q, :], ACT.Exp,
                                         bias=neg_max[:], accum_out=chunk_sum[:, q:q + 1]).then_inc(exp_done.sem, 1)

            def probsT_high(b, g):
                act.wait_ge(probs_turned.sem, probs_turned.value(b, g + 1))
                act.wait_ge(gathered.sem, gathered.value(b, g - 1))
                high(probsT_hi[:, g % 2, :], turn[g % 2][:] if g < 3 else turn[0][:]).then_inc(probsT_hi_done.sem, 1)

            def token_exp(b):
                act.wait_ge(all_max_done.sem, all_max_done.value(b, 1))
                act.wait_ge(q2c_summed.sem, q2c_summed.value(b, 0))
                nc.scalar.activation(tok_exp[:], all_max[:], ACT.Exp, bias=tok_max[:], scale=-1.0).then_inc(tok_exp_done.sem, 1)

            def normed_turned(b):
                act.wait_ge(c_turned.sem, c_turned.value(b, 1))
                act.wait_ge(held.sem, held.value(b, 0))
                nc.scalar.activation(cT[:], turn[1][:], ACT.Copy).then_inc(cT_done.sem, 1)

            def normed_high(b):
                act.wait_ge(cT_done.sem, cT_done.value(b, 1))
                act.wait_ge(c_projected.sem, c_projected.value(b, -1))
                high(cT_hi[:], cT[:]).then_inc(cT_hi_done.sem, 1)

            def normed_weighted_high(b):
                act.wait_ge(cw_done.sem, cw_done.value(b, KD))
                act.wait_ge(scored.sem, scored.value(b, 0))
                high(cw_hi[:], cw[:]).then_inc(cw_hi_done.sem, 1)

            def weighted_out(b):
                act.wait_ge(gathered.sem, gathered.value(b, QC))
                act.wait_ge(sum_steps.sem, sum_steps.value(b, 2))
                nc.scalar.activation(c2q[:], summed[:], ACT.Copy, scale=row_inv[:]).then_inc(c2q_done.sem, 1)

            def weighted_high(b):
                act.wait_ge(c2q_turned.sem, c2q_turned.value(b, 1))
                act.wait_ge(z_done.sem, z_done.value(b, 0))
                high(c2qT_hi[:], turn[1][:]).then_inc(c2qT_hi_done.sem, 1)

            def weighted_product_high(b):
                act.wait_ge(cc2q_done.sem, cc2q_done.value(b, 1))
                high(cc2q_hi[:], cc2q[:]).then_inc(cc2q_hi_done.sem, 1)

            def weight_high_part(w):
                act.wait_ge(weight_landed[w % RAW], 16 * (w // RAW + 1))
                nc.scalar.activation(wl_hi[:, w * NJ:(w + 1) * NJ, :].rearrange("p j d -> p (j d)"),
                                     raw[:, w % RAW, :], ACT.Copy).then_inc(weight_hi, 1)

            def token_part_high(b):
                act.wait_ge(q2c_steps.sem, q2c_steps.value(b, 2 + KD))
                act.wait_ge(z_done.sem, z_done.value(b, 0))
                high(cq2c_hi[:], cq2c[:]).then_inc(cq2c_hi_done.sem, 1)

            grant(act, c2q_done)
            cols_high(0, 0)
            cols_high(0, 1)
            normed_turned(0)
            normed_high(0)
            normed_weighted_high(0)
            for u in range(2, NU):
                cols_high(0, u)
            for w in range(KZ // NJ - 2):
                weight_high_part(w)
            exps(0)
            token_exp(0)
            for w in range(KZ // NJ - 2, KZ // NJ):
                weight_high_part(w)
            for h in range(NU - 2):
                rows_high(0, h)

            def step(b, more):
                probsT_high(b, 0)
                probsT_high(b, 1)
                rows_high(b, NU - 2)
                rows_high(b, NU - 1)
                if more:
                    cols_high(b + 1, 0)
                    cols_high(b + 1, 1)
                probsT_high(b, 2)
                token_part_high(b)
                if more:
                    cols_high(b + 1, 2)
                    normed_turned(b + 1)
                    cols_high(b + 1, 3)
                    normed_high(b + 1)
                    normed_weighted_high(b + 1)
                probsT_high(b, 3)
                if more:
                    cols_high(b + 1, 4)
                    cols_high(b + 1, 5)
                weighted_out(b)
                if more:
                    cols_high(b + 1, 6)
                    cols_high(b + 1, 7)
                    rows_high(b + 1, 0)
                    rows_high(b + 1, 1)
                weighted_high(b)
                if more:
                    rows_high(b + 1, 2)
                weighted_product_high(b)
                if more:
                    for h in range(3, NU - 2):
                        rows_high(b + 1, h)
                    exps(b + 1)
                    token_exp(b + 1)

            with act.Fori(0, B - 1) as i:
                step(i, True)
            step(B - 1, False)

        @block.vector
        def _(dve):
            V = nc.vector

            def low(out, raw, hi):
                return V.tensor_tensor(out, raw, hi.bitcast(F32), ALU.subtract)

            def unit_low(slot, done):
                dve.wait_ge(hi_done.sem, done)
                low(ctx_lo[:, slot].rearrange("p j d -> p (j d)"), raw[:, slot % RAW, :],
                    ctx_hi[:, slot].rearrange("p j d -> p (j d)")).then_inc(lo_done.sem, 1)

            def cols_low(b, u):
                unit_low(u, hi_done.value(b, u + 1))

            def rows_low(b, h):
                unit_low(h, hi_done.value(b, NU + h + 1))

            def norm_moments(b):
                dve.wait_ge(x_landed.sem, x_landed.value(b, 16))
                V.bn_stats(stats[:], x_in[:]).then_inc(norm_steps.sem, 1)
                dve.wait_ge(norm_steps.sem, norm_steps.value(b, 1))
                dve.nop(nofuse=True)
                V.bn_aggr(mean_var[:], stats[:]).then_inc(norm_steps.sem, 1)

            def norm(b):
                dve.wait_ge(rstd_steps.sem, rstd_steps.value(b, 2))
                V.tensor_scalar(c[:], x_in[:], mean_var[:, 0:1], rstd[:], ALU.subtract, ALU.mult).then_inc(norm_steps.sem, 1)
                dve.wait_ge(norm_steps.sem, norm_steps.value(b, 3))
                V.tensor_tensor_reduce(out=cw[:], in0=c[:], in1=w_c_rows[:], scale=1.0, scalar=0.0,
                                       op0=ALU.mult, op1=ALU.add, accum_out=row_dot[:]).then_inc(norm_steps.sem, 1)

            def normed_weighted(b):
                dve.wait_ge(cT_done.sem, cT_done.value(b, 1))
                dve.wait_ge(norm_steps.sem, norm_steps.value(b, 4))
                for k in range(KD):
                    V.tensor_scalar(cw[:, k * P:(k + 1) * P], cT[:, k * P:(k + 1) * P], w_cq_col[:, k:k + 1],
                                    w_q_col[:, k:k + 1], ALU.mult, ALU.add).then_inc(cw_done.sem, 1)

            def normed_weighted_low(b):
                dve.wait_ge(cw_hi_done.sem, cw_hi_done.value(b, 1))
                low(cw_lo[:], cw[:], cw_hi[:]).then_inc(cw_lo_done.sem, 1)

            def chunk_maximum(b, q):
                dve.wait_ge(scored.sem, scored.value(b, q + 1))
                V.reduce_max(chunk_max[:, q:q + 1], scores[:, q, :], AX.X).then_inc(max_done.sem, 1)

            def row_maximum(b):
                dve.wait_ge(max_done.sem, max_done.value(b, QC))
                V.tensor_reduce(neg_max[:], chunk_max[:], AX.X, ALU.max, negate=True).then_inc(max_done.sem, 1)
                dve.wait_ge(max_done.sem, max_done.value(b, QC + 1))
                V.tensor_scalar(tok_max[:], row_dot[:], neg_max[:], bias_sum[:], ALU.subtract, ALU.add).then_inc(tok_max_done.sem, 1)

            def probsT_low(b, g):
                dve.wait_ge(probsT_hi_done.sem, probsT_hi_done.value(b, g + 1))
                low(probsT_lo[:, g % 2, :], turn[g % 2][:] if g < 3 else turn[0][:], probsT_hi[:, g % 2, :]).then_inc(probsT_lo_done.sem, 1)

            def sums(b):
                dve.wait_ge(exp_done.sem, exp_done.value(b, QC))
                V.reduce_sum(row_sum[:], chunk_sum[:], AX.X).then_inc(sum_steps.sem, 1)
                dve.wait_ge(sum_steps.sem, sum_steps.value(b, 1))
                dve.wait_ge(c2q_done.sem, c2q_done.value(b, 0))
                V.reciprocal(row_inv[:], row_sum[:]).then_inc(sum_steps.sem, 1)

            def token_part(b):
                dve.wait_ge(q2c_summed.sem, q2c_summed.value(b, 1))
                V.reciprocal(tok_inv[:], tok_sum_ps).then_inc(q2c_steps.sem, 1)
                dve.wait_ge(q2c_steps.sem, q2c_steps.value(b, 1))
                V.tensor_scalar(q2c[:], q2c_ps, tok_inv[:], None, ALU.mult).then_inc(q2c_steps.sem, 1)
                dve.wait_ge(q2c_steps.sem, q2c_steps.value(b, 2))
                for k in range(KD):
                    V.tensor_scalar(cq2c[:, k * P:(k + 1) * P], cT[:, k * P:(k + 1) * P], q2c[:, k:k + 1],
                                    None, ALU.mult).then_inc(q2c_steps.sem, 1)

            grant(dve, sum_steps, c2qT_lo_done, lo_done, probsT_lo_done, cc2q_done, x1_done)
            dve.wait_ge(const_landed, 16 * 8)
            V.reduce_sum(bias_sum[:], biases[:], AX.X).then_inc(bias_done, 1)
            dve.wait_ge(bias_done, 1)
            norm_moments(0)
            norm(0)
            cols_low(0, 0)
            cols_low(0, 1)
            normed_weighted(0)
            normed_weighted_low(0)

            def weight_low_part(w):
                dve.wait_ge(weight_hi, w + 1)
                V.tensor_tensor(wl_lo[:, w * NJ:(w + 1) * NJ, :].rearrange("p j d -> p (j d)"), raw[:, w % RAW, :],
                                wl_hi[:, w * NJ:(w + 1) * NJ, :].rearrange("p j d -> p (j d)").bitcast(F32),
                                ALU.subtract).then_inc(weight_lo, 1)

            for u in range(2, NU):
                cols_low(0, u)
            for q in range(QC):
                chunk_maximum(0, q)
                if q == QC - 1:
                    row_maximum(0)
                weight_low_part(2 * q)
                weight_low_part(2 * q + 1)
            for h in range(NU - 2):
                rows_low(0, h)

            def result(b):
                dve.wait_ge(z_done.sem, z_done.value(b, 1))
                dve.wait_ge(x_bias_done.sem, x_bias_done.value(b, 1))
                dve.wait_ge(x1_stored.sem, x1_stored.value(b, 0))
                V.tensor_tensor(x1[:], projected[:], x_bias[:], ALU.add).then_inc(x1_done.sem, 1)

            def step(b, more):
                probsT_low(b, 0)
                probsT_low(b, 1)
                rows_low(b, NU - 2)
                rows_low(b, NU - 1)
                sums(b)
                if more:
                    norm_moments(b + 1)
                token_part(b)
                if more:
                    norm(b + 1)
                probsT_low(b, 2)
                if more:
                    cols_low(b + 1, 0)
                    cols_low(b + 1, 1)
                    cols_low(b + 1, 2)
                    normed_weighted(b + 1)
                    cols_low(b + 1, 3)
                    normed_weighted_low(b + 1)
                probsT_low(b, 3)
                if more:
                    for u in range(4, NU):
                        cols_low(b + 1, u)
                    chunk_maximum(b + 1, 0)
                    rows_low(b + 1, 0)
                    rows_low(b + 1, 1)
                    chunk_maximum(b + 1, 1)
                dve.wait_ge(held.sem, held.value(b, 1))
                dve.wait_ge(c2qT_hi_done.sem, c2qT_hi_done.value(b, 1))
                V.tensor_tensor(cc2q[:], turn[1][:], cT_held[:], ALU.mult).then_inc(cc2q_done.sem, 1)
                low(c2qT_lo[:], turn[1][:], c2qT_hi[:]).then_inc(c2qT_lo_done.sem, 1)
                if more:
                    rows_low(b + 1, 2)
                dve.wait_ge(cc2q_hi_done.sem, cc2q_hi_done.value(b, 1))
                low(cc2q_lo[:], cc2q[:], cc2q_hi[:]).then_inc(cc2q_lo_done.sem, 1)
                if more:
                    rows_low(b + 1, 3)
                    chunk_maximum(b + 1, 2)
                    rows_low(b + 1, 4)
                    chunk_maximum(b + 1, 3)
                    row_maximum(b + 1)
                    rows_low(b + 1, NU - 3)
                result(b)

            with dve.Fori(0, B - 1) as i:
                step(i, True)
            step(B - 1, False)

        @block.tensor
        def _(pe):
            def turn_normed(b):
                pe.wait_ge(norm_steps.sem, norm_steps.value(b, 3))
                pe.wait_ge(probsT_lo_done.sem, probsT_lo_done.value(b, -2))
                for k in range(KD):
                    last = nc.tensor.transpose(turn[1][:, k * P:(k + 1) * P], c[:, k * P:(k + 1) * P], ident[:])
                last.then_inc(c_turned.sem, 1)

            def score(b, q):
                for k in range(KD):
                    u = 2 * q + k // KH
                    if k % KH == 0:
                        pe.wait_ge(lo_done.sem, lo_done.value(b, u + 1))
                    ks = slice(k * P, (k + 1) * P)
                    last = product(nc, scores[:, q, :], (cw_hi[:, ks], cw_lo[:, ks]),
                                   (ctx_hi[:, u, k % KH, :], ctx_lo[:, u, k % KH, :]), k == 0, k == KD - 1)
                last.then_inc(scored.sem, 1)

            def turn_probs(b, g):
                pe.wait_ge(exp_done.sem, exp_done.value(b, g + 1))
                if g == 0:
                    pe.wait_ge(probsT_lo_done.sem, probsT_lo_done.value(b, 0))
                elif g == 1:
                    pe.wait_ge(cc2q_done.sem, cc2q_done.value(b, 0))
                    pe.wait_ge(c2qT_lo_done.sem, c2qT_lo_done.value(b, 0))
                    pe.wait_ge(cT_done.sem, cT_done.value(b, 1))
                else:
                    pe.wait_ge(probsT_lo_done.sem, probsT_lo_done.value(b, g - 1 if g == 2 else 3))
                to = turn[g % 2] if g < 3 else turn[0]
                for t in range(4):
                    h, j = 2 * g + t // NJ, t % NJ
                    last = nc.tensor.transpose(to[:, t * P:(t + 1) * P],
                                               probs[:, h * NJ * P + j:(h + 1) * NJ * P:NJ], ident[:])
                last.then_inc(probs_turned.sem, 1)

            def gather(b, g):
                pe.wait_ge(probsT_lo_done.sem, probsT_lo_done.value(b, g + 1))
                pe.wait_ge(lo_done.sem, lo_done.value(b, NU + 2 * g + 2))
                if g == 0:
                    pe.wait_ge(c2q_done.sem, c2q_done.value(b, 0))
                for t in range(4):
                    h, j = 2 * g + t // NJ, t % NJ
                    last = product(nc, summed[:], (probsT_hi[:, g % 2, t * P:(t + 1) * P], probsT_lo[:, g % 2, t * P:(t + 1) * P]),
                                   (ctx_hi[:, h, j, :], ctx_lo[:, h, j, :]), g == 0 and t == 0, g == QC - 1 and t == 3)
                last.then_inc(gathered.sem, 1)

            def project(part, hi, lo, first, last):
                for k in range(KD):
                    ks = slice(k * P, (k + 1) * P)
                    z = part * KD + k
                    made = product(nc, projected[:], (hi[:, ks], lo[:, ks]), (wl_hi[:, z, :], wl_lo[:, z, :]),
                                   first and k == 0, last and k == KD - 1)
                return made

            def sum_tokens(b):
                pe.wait_ge(tok_exp_done.sem, tok_exp_done.value(b, 1))
                pe.wait_ge(exp_done.sem, exp_done.value(b, QC))
                nc.tensor.matmul(tok_sum_ps, ones[:], tok_exp[:], start=True, stop=True)
                for k in range(KD):
                    last = nc.tensor.matmul(q2c_ps[:, k:k + 1], c[:, k * P:(k + 1) * P], tok_exp[:], start=True, stop=True)
                last.then_inc(q2c_summed.sem, 1)

            grant(pe, probs_turned, q2c_summed, scored, gathered, c_projected, z_done)
            pe.wait_ge(const_landed, 16 * 8)
            pe.wait_ge(ones_done, 1)
            turn_normed(0)
            pe.wait_ge(cw_lo_done.sem, cw_lo_done.value(0, 1))
            for q in range(QC):
                score(0, q)

            def step(b, more):
                turn_probs(b, 0)
                turn_probs(b, 1)
                pe.wait_ge(x1_done.sem, x1_done.value(b, 0))
                pe.wait_ge(cT_lo_done.sem, cT_lo_done.value(b, 1))
                pe.wait_ge(weight_lo, KZ // NJ)
                project(0, cT_hi, cT_lo, True, False).then_inc(c_projected.sem, 1)
                gather(b, 0)
                sum_tokens(b)
                turn_probs(b, 2)
                gather(b, 1)
                if more:
                    turn_normed(b + 1)
                gather(b, 2)
                turn_probs(b, 3)
                pe.wait_ge(cq2c_lo_done.sem, cq2c_lo_done.value(b, 1))
                project(3, cq2c_hi, cq2c_lo, False, False).then_inc(c_projected.sem, 1)
                gather(b, 3)
                if more:
                    pe.wait_ge(cw_lo_done.sem, cw_lo_done.value(b + 1, 1))
                    pe.wait_ge(q2c_steps.sem, q2c_steps.value(b, 2))
                    score(b + 1, 0)
                    score(b + 1, 1)
                pe.wait_ge(c2q_done.sem, c2q_done.value(b, 1))
                if more:
                    pe.wait_ge(cT_done.sem, cT_done.value(b + 1, 1))
                for k in range(KD):
                    last = nc.tensor.transpose(turn[1][:, k * P:(k + 1) * P], c2q[:, k * P:(k + 1) * P], ident[:])
                last.then_inc(c2q_turned.sem, 1)
                if more:
                    score(b + 1, 2)
                    score(b + 1, 3)
                pe.wait_ge(c2qT_lo_done.sem, c2qT_lo_done.value(b, 1))
                project(1, c2qT_hi, c2qT_lo, False, False)
                pe.wait_ge(cc2q_lo_done.sem, cc2q_lo_done.value(b, 1))
                project(2, cc2q_hi, cc2q_lo, False, True).then_inc(z_done.sem, 1)

            with pe.Fori(0, B - 1) as i:
                step(i, True)
            step(B - 1, False)


H = 16
HD = D // H
E = 32
TOPK = 4
CAP = 1024
G = 4
NG = B // G
NBLOCKS = 96
NONE = E * CAP
ROWS = NONE + NBLOCKS * P


def self_attention_and_routing(nc, x1_in, W_qkT, W_vT, W_g, W_s13, W_s2, ident_in, before_in, normed_out, acc_out,
                               token_of_slot, pair_rank, pair_expert, pair_weight, expert_count):
    CQ = 2 * D // P
    CF = 512 // P
    QUARTER = H // 4
    VW = HD + 1
    with ExitStack() as stack:
        m = Memory(nc, stack, "sa")
        wqk = [m.sb("wqk_hi", [P, KD, 2 * D], F32R), m.sb("wqk_lo", [P, KD, 2 * D], F32R)]
        wv = [m.sb("wv_hi", [P, KD, D], F32R), m.sb("wv_lo", [P, KD, D], F32R)]
        ws13 = [m.sb("ws13_hi", [P, KD, 2 * D], F32R), m.sb("ws13_lo", [P, KD, 2 * D], F32R)]
        ws2 = [m.sb("ws2_hi", [P, CF, D], F32R), m.sb("ws2_lo", [P, CF, D], F32R)]
        wg = [m.sb("wg_hi", [P, KD, E], F32R), m.sb("wg_lo", [P, KD, E], F32R)]
        wg_raw = m.sb("wg_raw", [P, KD, E])
        ident = m.sb("ident", [P, P])
        before = m.sb("before", [P, P])
        ones = m.sb("ones", [P, P])
        eps_pow = m.sb("eps_pow", [P, 2])
        x = m.sb("x", [P, G, D])
        xn = m.sb("xn", [P, 4, D])
        xnT_hi = m.sb("xnT_hi", [P, KD, G * P], F32R)
        xnT_lo = m.sb("xnT_lo", [P, KD, G * P], F32R)
        stats = m.sb("stats", [P, 6])
        mean_var = m.sb("mean_var", [P, 2])
        var_eps = m.sb("var_eps", [P, 1])
        rstd = m.sb("rstd", [P, 1])
        qkT = m.sb("qkT", [P, CQ, G * P])
        v = m.sb("v", [P, G, H, VW])
        probs = m.sb("probs", [P, H, P])
        probsT = m.sb("probsT", [P, H, P])
        head_max = m.sb("head_max", [P, H])
        head_inv = m.sb("head_inv", [P, H])
        mixed = m.sb("mixed", [P, D])
        gate = m.sb("gate", [P, G * P])
        hT = m.sb("hT", [P, G * P])
        hT_hi = m.sb("hT_hi", [P, CF, G * P], F32R)
        hT_lo = m.sb("hT_lo", [P, CF, G * P], F32R)
        acc = m.sb("acc", [P, 2, D])
        logitsT = m.sb("logitsT", [E, G * P])
        logits = m.sb("logits", [P, G, E])
        top = m.sb("top", [P, G, 8])
        top_at = m.sb("top_at", [P, G, 8], U32)
        expert = m.sb("expert", [P, G, TOPK])
        shifted = m.sb("shifted", [P, G, E])
        top_shifted = m.sb("top_shifted", [P, G, TOPK])
        exp_sum = m.sb("exp_sum", [P, G])
        exp_inv = m.sb("exp_inv", [P, G])
        iota_e = m.sb("iota_e", [P, E])
        one_hot = m.sb("one_hot", [P, G, TOPK, E])
        taken = m.sb("taken", [P, G, E])
        counted = expert_count
        group_taken = m.sb("group_taken", [P, E])
        ranked = m.sb("ranked", [P, G, TOPK, E])
        rank = m.sb("rank", [P, G * TOPK])
        kept = m.sb("kept", [P, G * TOPK])
        base = m.sb("base", [P, G * TOPK])
        slot = m.sb("slot", [P, G * TOPK])
        scatter_to = m.sb("scatter_to", [P, G * TOPK], I32)
        tokens_f = m.sb("tokens_f", [P, G])
        tokens = m.sb("tokens", [P, G], I32)
        zeros = gate[:, 0:ROWS // P].bitcast(I32)

        S = m.ps("scores", [P, 4, BANK])
        turn = [m.ps("turn0", [P, BANK]), m.ps("turn1", [P, BANK])]
        work = [m.ps("work0", [P, BANK]), m.ps("work1", [P, BANK])]

        const_landed = m.sem("const_landed")
        setup = m.sem("setup")
        NW = 6
        w_landed = [m.sem("w_landed0"), m.sem("w_landed1")]
        w_hi = m.sem("w_hi")
        w_lo = m.sem("w_lo")
        x_landed = m.tally("x_landed", 16)
        x_moved = m.tally("x_moved", G, 1)
        norm_steps = m.tally("norm_steps", 3 * 2 * G)
        rstd_steps = m.tally("rstd_steps", 2 * 2 * G)
        turned = m.tally("turned", 2 * G, 1)
        xnT_hi_done = m.tally("xnT_hi_done", 2 * G)
        xnT_lo_done = m.tally("xnT_lo_done", 2 * G, 2 * G)
        normed_stored = [m.tally("normed_stored0", 16 * G // 2, 1), m.tally("normed_stored1", 16 * G // 2, 1)]
        qk_done = m.tally("qk_done", CQ)
        qk_read = m.tally("qk_read", CQ)
        v_done = m.tally("v_done", G)
        v_read = m.tally("v_read", G)
        scored = m.tally("scored", G, 1)
        max_done = m.tally("max_done", G)
        shift_done = m.tally("shift_done", G)
        exp_done = m.tally("exp_done", G)
        probs_turned = m.tally("probs_turned", 4 * G, 1)
        probsT_read = m.tally("probsT_read", 4 * G, 4 * G)
        mixed_done = m.tally("mixed_done", G, 1)
        mix_steps = m.tally("mix_steps", 6 * G, 1)
        logitsT_done = m.tally("logitsT_done", 1)
        logitsT_read = m.tally("logitsT_read", 1)
        logits_done = m.tally("logits_done", 1, 1)
        logits_steps = m.tally("logits_steps", 1)
        up_done = m.tally("up_done", CF, 1)
        gate_done = m.tally("gate_done", CF)
        h_steps = m.tally("h_steps", 2 * CF, 2 * CF)
        hT_hi_done = m.tally("hT_hi_done", CF, 1)
        hT_lo_done = m.tally("hT_lo_done", CF, 1)
        down_done = m.tally("down_done", G, 1)
        acc_done = m.tally("acc_done", G, 1)
        acc_stored = [m.tally("acc_stored0", 16 * G // 2, 1), m.tally("acc_stored1", 16 * G // 2, 1)]
        R_SHIFTED, R_TAKEN, R_RANKED, ROUTE_STEPS = 11, 13, 16, 30
        route_steps = m.tally("route_steps", ROUTE_STEPS, 1)
        route_exp_done = m.tally("route_exp_done", 2)
        ranks_done = m.tally("ranks_done", 1)
        scattered = m.tally("scattered", 16 * G * TOPK)
        scatter_over = m.tally("scatter_over", 1, 1)
        zeroed = m.sem("zeroed")
        block = stack.enter_context(nc.Block())

        stage = [probs[:].rearrange("p h n -> p (h n)"), probsT[:].rearrange("p h n -> p (h n)")]
        half = KD // 2
        x_next = stage[0].rearrange("p (j d) -> p j d", j=G)

        def flat(ap):
            return ap.rearrange("p k n -> p (k n)")

        pieces = [(flat(W_qkT[:, :half, :]), wqk, slice(0, half)), (flat(W_qkT[:, half:, :]), wqk, slice(half, KD)),
                  (flat(W_vT), wv, slice(0, KD)),
                  (flat(W_s13[:, :half, :]), ws13, slice(0, half)), (flat(W_s13[:, half:, :]), ws13, slice(half, KD)),
                  (flat(W_s2), ws2, slice(0, CF))]

        @block.sync
        def _(sp):
            grant(sp, normed_stored[0], normed_stored[1], acc_stored[0], acc_stored[1])
            sp.dma_start(x[:], x1_in[0:G].rearrange("b p d -> p b d")).then_inc(x_landed.sem, 16)
            for dst, src in ((ident[:], ident_in), (before[:], before_in), (wg_raw[:], W_g)):
                sp.dma_start(dst, src).then_inc(const_landed, 16)
            sp.wait_ge(setup, 1)
            sp.dma_start(token_of_slot.rearrange("(p n) one -> p (n one)", p=P), zeros).then_inc(zeroed, 16)
            for n, (src, _, _) in enumerate(pieces):
                if n >= 2:
                    sp.wait_ge(w_lo, n)
                sp.dma_start(stage[n % 2], src).then_inc(w_landed[n % 2], 16)

            def step(g, more):
                for j in range(G):
                    if more and j == G - 1:
                        sp.wait_ge(probs_turned.sem, probs_turned.value(g, 4 * G))
                        sp.dma_start(x_next, x1_in[bass.ds(g * G + G, G)].rearrange("b p d -> p b d")).then_inc(x_landed.sem, 16)
                    sp.wait_ge(norm_steps.sem, norm_steps.value(g, 3 * (G + j) + 3))
                    sp.dma_start(normed_out[g * G + j], xn[:, 2 + j % 2, :]).then_inc(normed_stored[j % 2].sem, 16)
                for j in range(G):
                    sp.wait_ge(acc_done.sem, acc_done.value(g, j + 1))
                    sp.dma_start(acc_out[g * G + j], acc[:, j % 2, :]).then_inc(acc_stored[j % 2].sem, 16)

            with sp.Fori(0, NG - 1) as i:
                step(i, True)
            step(NG - 1, False)
            for j in range(2):
                sp.wait_ge(normed_stored[j].sem, normed_stored[j].value(NG - 1, 16 * G // 2))
                sp.wait_ge(acc_stored[j].sem, acc_stored[j].value(NG - 1, 16 * G // 2))

        @block.gpsimd
        def _(pool):
            nc.gpsimd.memset(eps_pow[:, 0:1], EPS)
            nc.gpsimd.memset(eps_pow[:, 1:2], -0.5)
            nc.gpsimd.memset(ones[:], 1.0)
            nc.gpsimd.memset(zeros, 0)
            nc.gpsimd.memset(counted[:], 0.0)
            for j in range(G):
                nc.gpsimd.memset(v[:, j, :, HD:VW], 1.0)
            nc.gpsimd.iota(iota_e[:], pattern=[[1, E]], base=0, channel_multiplier=0, allow_small_or_imprecise_dtypes=True)
            nc.gpsimd.iota(tokens_f[:], pattern=[[P, G]], base=0, channel_multiplier=1, allow_small_or_imprecise_dtypes=True).then_inc(setup, 1)
            grant(pool, scatter_over)
            pool.wait_ge(setup, 1)

            def inverse_spread(g, n):
                pool.wait_ge(norm_steps.sem, norm_steps.value(g, 3 * n + 2))
                pool.nop(nofuse=True)
                nc.gpsimd.tensor_tensor(var_eps[:], mean_var[:, 1:2], eps_pow[:, 0:1], ALU.add).then_inc(rstd_steps.sem, 1)
                pool.wait_ge(rstd_steps.sem, rstd_steps.value(g, 2 * n + 1))
                pool.nop(nofuse=True)
                nc.gpsimd.tensor_tensor(rstd[:], var_eps[:], eps_pow[:, 1:2], ALU.pow).then_inc(rstd_steps.sem, 1)

            for n in range(G):
                inverse_spread(0, n)

            def step(g, more):
                for n in range(G, 2 * G):
                    inverse_spread(g, n)
                if more:
                    for n in range(G):
                        inverse_spread(g + 1, n)
                pool.wait_ge(zeroed, 16)
                pool.wait_ge(route_steps.sem, route_steps.value(g, ROUTE_STEPS))
                pool.nop(nofuse=True)
                for j in range(G):
                    for k in range(TOPK):
                        n = j * TOPK + k
                        pool.indirect_dma_start(token_of_slot, bass.IndirectOffsetOnAxis(ap=scatter_to[:, n:n + 1], axis=0),
                                                tokens[:, j:j + 1], None, bounds_check=NONE - 1, oob_is_err=False)\
                            .then_inc(scattered.sem, 16)
                pool.wait_ge(scattered.sem, scattered.value(g, 16 * G * TOPK))
                pool.nop(nofuse=True)
                pool.sem_inc(scatter_over.sem, 1)

            with pool.Fori(0, NG - 1) as i:
                step(i, True)
            step(NG - 1, False)

        @block.scalar
        def _(act):
            def copy(out, src):
                return nc.scalar.activation(out, src, ACT.Copy)

            grant(act, probsT_read, hT_hi_done, x_moved)

            def normed_high(g, n):
                j = n % G
                act.wait_ge(turned.sem, turned.value(g, n + 1))
                if n < G:
                    act.wait_ge(up_done.sem, up_done.value(g, 0))
                else:
                    act.wait_ge(v_done.sem, v_done.value(g, G))
                copy(xnT_hi[:, :, j * P:(j + 1) * P], turn[n % 2][:].rearrange("p (k t) -> p k t", k=KD)).then_inc(xnT_hi_done.sem, 1)

            def project_out(g, c):
                act.wait_ge(qk_done.sem, qk_done.value(g, c + 1))
                if c == 0:
                    act.wait_ge(scored.sem, scored.value(g, 0))
                copy(qkT[:, c, :], S[:, c % 4, :]).then_inc(qk_read.sem, 1)

            def attend(g, j):
                act.wait_ge(shift_done.sem, shift_done.value(g, j + 1))
                nc.scalar.activation(probs[:], probs[:], ACT.Exp, scale=float(D) ** -0.5).then_inc(exp_done.sem, 1)

            def probsT_out(g, j):
                for q in range(4):
                    act.wait_ge(probs_turned.sem, probs_turned.value(g, 4 * j + q + 1))
                    act.wait_ge(mixed_done.sem, mixed_done.value(g, j))
                    copy(probsT[:, q * 4:q * 4 + 4, :], turn[q % 2][:].rearrange("p (h t) -> p h t", h=4)).then_inc(probsT_read.sem, 1)

            act.wait_ge(const_landed, 16 * 3)
            copy(flat(wg[0][:]), flat(wg_raw[:])).then_inc(w_hi, 1)

            def weight_high(n):
                _, (hi, _), ks = pieces[n]
                act.wait_ge(w_landed[n % 2], 16 * (n // 2 + 1))
                copy(flat(hi[:, ks, :]), stage[n % 2]).then_inc(w_hi, 1)

            normed_high(0, 0)
            weight_high(0)
            normed_high(0, 1)
            weight_high(1)
            normed_high(0, 2)
            normed_high(0, 3)
            for n in range(2, NW):
                weight_high(n)
            act.wait_ge(zeroed, 16)

            def move_x(g, j):
                act.wait_ge(x_landed.sem, x_landed.value(g + 1, 16))
                act.wait_ge(acc_done.sem, acc_done.value(g, j + 1))
                copy(x[:, j, :], x_next[:, j, :]).then_inc(x_moved.sem, 1)

            def logits_out(g):
                act.wait_ge(logitsT_done.sem, logitsT_done.value(g, 1))
                act.wait_ge(logits_done.sem, logits_done.value(g, 0))
                copy(logitsT[:], work[1][0:E, :]).then_inc(logitsT_read.sem, 1)

            def shared_gate(g, c):
                act.wait_ge(up_done.sem, up_done.value(g, c + 1))
                act.wait_ge(h_steps.sem, h_steps.value(g, 2 * c - 1))
                nc.scalar.activation(gate[:], S[:, 2 * (c % 2), :], ACT.Tanh, scale=0.5).then_inc(gate_done.sem, 1)
                act.wait_ge(h_steps.sem, h_steps.value(g, 2 * c + 2))
                act.wait_ge(down_done.sem, down_done.value(g, 0))
                copy(hT_hi[:, c, :], hT[:]).then_inc(hT_hi_done.sem, 1)

            def step(g, more):
                for c in range(CQ):
                    project_out(g, c)
                attend(g, 0)
                act.wait_ge(w_lo, NW + 1)
                for j in range(G):
                    probsT_out(g, j)
                    if j + 1 < G:
                        attend(g, j + 1)
                    if j:
                        normed_high(g, G + j - 1)
                normed_high(g, 2 * G - 1)
                logits_out(g)
                shared_gate(g, 0)
                act.wait_ge(route_steps.sem, route_steps.value(g, R_SHIFTED))
                nc.scalar.activation(shifted[:], shifted[:], ACT.Exp).then_inc(route_exp_done.sem, 1)
                nc.scalar.activation(top_shifted[:], top_shifted[:], ACT.Exp).then_inc(route_exp_done.sem, 1)
                for c in range(1, CF):
                    shared_gate(g, c)
                if more:
                    for n in range(G - 1):
                        normed_high(g + 1, n)
                    move_x(g, 0)
                    normed_high(g + 1, G - 1)
                    for j in range(1, G):
                        move_x(g, j)

            with act.Fori(0, NG - 1) as i:
                step(i, True)
            step(NG - 1, False)

        @block.vector
        def _(dve):
            V = nc.vector
            grant(dve, xnT_lo_done, h_steps, route_steps, hT_lo_done, acc_done, mix_steps)

            def low(out, raw, hi):
                return V.tensor_tensor(out, raw, hi.bitcast(F32), ALU.subtract)

            def norm(g, n, x=x):
                j = n % G
                if n == 0:
                    dve.wait_ge(x_landed.sem, x_landed.value(g, 16))
                if n >= G:
                    dve.wait_ge(mix_steps.sem, mix_steps.value(g, 6 * j + 6))
                V.bn_stats(stats[:], x[:, j, :]).then_inc(norm_steps.sem, 1)
                dve.wait_ge(norm_steps.sem, norm_steps.value(g, 3 * n + 1))
                dve.nop(nofuse=True)
                V.bn_aggr(mean_var[:], stats[:]).then_inc(norm_steps.sem, 1)
                dve.wait_ge(rstd_steps.sem, rstd_steps.value(g, 2 * n + 2))
                dve.wait_ge(turned.sem, turned.value(g, n - 1 if j >= 2 else 0))
                if n >= G:
                    dve.wait_ge(normed_stored[j % 2].sem, normed_stored[j % 2].value(g, 16 * (j // 2)))
                V.tensor_scalar(xn[:, 2 * (n // G) + j % 2, :], x[:, j, :], mean_var[:, 0:1], rstd[:], ALU.subtract, ALU.mult)\
                    .then_inc(norm_steps.sem, 1)

            def normed_low(g, n):
                j = n % G
                dve.wait_ge(xnT_hi_done.sem, xnT_hi_done.value(g, n + 1))
                low(xnT_lo[:, :, j * P:(j + 1) * P], turn[n % 2][:].rearrange("p (k t) -> p k t", k=KD),
                    xnT_hi[:, :, j * P:(j + 1) * P]).then_inc(xnT_lo_done.sem, 1)

            def maximum_and_shift(g, j):
                dve.wait_ge(scored.sem, scored.value(g, j + 1))
                V.reduce_max(head_max[:].rearrange("p (c r) -> p r c", r=4), S[:].rearrange("p r (c n) -> p r c n", n=P), AX.X).then_inc(max_done.sem, 1)
                dve.wait_ge(max_done.sem, max_done.value(g, j + 1))
                if j == 0:
                    dve.wait_ge(x_moved.sem, x_moved.value(g, 0))
                dve.wait_ge(probs_turned.sem, probs_turned.value(g, 4 * j))
                for r in range(4):
                    last = V.tensor_tensor(probs[:].rearrange("p (c r) n -> p r c n", r=4)[:, r],
                                           S[:, r, :].rearrange("p (c n) -> p c n", n=P),
                                           head_max[:].rearrange("p (c r) -> p r c", r=4)[:, r].unsqueeze(2).to_broadcast([P, QUARTER, P]),
                                           ALU.subtract)
                last.then_inc(shift_done.sem, 1)

            def mix_out(g, j):
                dve.wait_ge(mixed_done.sem, mixed_done.value(g, j + 1))
                k0 = 6 * j
                for w in range(2):
                    hs = slice(w * 8, w * 8 + 8)
                    o = work[w][:, 0:8 * VW].rearrange("p (h n) -> p h n", n=VW)
                    mw = mixed[:, w * 256:(w + 1) * 256].rearrange("p (h n) -> p h n", n=HD)
                    V.reciprocal(head_inv[:, hs], o[:, :, HD:VW].rearrange("p h n -> p (h n)")).then_inc(mix_steps.sem, 1)
                    dve.wait_ge(mix_steps.sem, mix_steps.value(g, k0 + 3 * w + 1))
                    V.tensor_tensor(mw, o[:, :, 0:HD], head_inv[:, hs].unsqueeze(2).to_broadcast([P, 8, HD]), ALU.mult).then_inc(mix_steps.sem, 1)
                    dve.wait_ge(mix_steps.sem, mix_steps.value(g, k0 + 3 * w + 2))
                    xw = x[:, j, w * 256:(w + 1) * 256]
                    V.tensor_tensor(xw, xw, mixed[:, w * 256:(w + 1) * 256], ALU.add).then_inc(mix_steps.sem, 1)

            dve.wait_ge(const_landed, 16 * 3)
            dve.wait_ge(setup, 1)

            def weight_low(n):
                _, (hi, lo), ks = pieces[n]
                dve.wait_ge(w_hi, n + 2)
                low(flat(lo[:, ks, :]), stage[n % 2], flat(hi[:, ks, :])).then_inc(w_lo, 1)

            norm(0, 0)
            dve.wait_ge(w_hi, 1)
            low(flat(wg[1][:]), flat(wg_raw[:]), flat(wg[0][:])).then_inc(w_lo, 1)
            norm(0, 1)
            normed_low(0, 0)
            weight_low(0)
            norm(0, 2)
            normed_low(0, 1)
            weight_low(1)
            norm(0, 3)
            normed_low(0, 2)
            normed_low(0, 3)
            for n in range(2, NW):
                weight_low(n)

            def choose(g):
                dve.wait_ge(logits_done.sem, logits_done.value(g, 1))
                dve.wait_ge(route_steps.sem, route_steps.value(g, 0))
                V.tensor_copy(logits[:], work[0][:, 0:G * E].rearrange("p (j e) -> p j e", e=E)).then_inc(logits_steps.sem, 1)
                dve.wait_ge(logits_steps.sem, logits_steps.value(g, 1))
                dve.nop(nofuse=True)
                for j in range(G):
                    V.max(top[:, j, :], logits[:, j, :]).then_inc(route_steps.sem, 1)
                dve.wait_ge(route_steps.sem, route_steps.value(g, 4))
                dve.nop(nofuse=True)
                for j in range(G):
                    V.max_index(top_at[:, j, :], top[:, j, :], logits[:, j, :]).then_inc(route_steps.sem, 1)
                dve.wait_ge(route_steps.sem, route_steps.value(g, 8))
                V.tensor_copy(expert[:], top_at[:, :, 0:TOPK]).then_inc(route_steps.sem, 1)
                V.tensor_tensor(shifted[:], logits[:], top[:, :, 0:1].to_broadcast([P, G, E]), ALU.subtract).then_inc(route_steps.sem, 1)
                V.tensor_tensor(top_shifted[:], top[:, :, 0:TOPK], top[:, :, 0:1].to_broadcast([P, G, TOPK]), ALU.subtract).then_inc(route_steps.sem, 1)
                dve.wait_ge(route_steps.sem, route_steps.value(g, 11))
                V.tensor_tensor(one_hot[:], iota_e[:].unsqueeze(1).unsqueeze(1).to_broadcast([P, G, TOPK, E]),
                                     expert[:].unsqueeze(3).to_broadcast([P, G, TOPK, E]), ALU.is_equal).then_inc(route_steps.sem, 1)
                dve.wait_ge(route_steps.sem, route_steps.value(g, 12))
                V.tensor_reduce(taken[:], one_hot[:].rearrange("p j k e -> p j e k"), AX.X, ALU.add).then_inc(route_steps.sem, 1)

            def place(g):
                pairs = slice(0, G * TOPK)
                dve.wait_ge(route_exp_done.sem, route_exp_done.value(g, 2))
                V.reduce_sum(exp_sum[:], shifted[:], AX.X).then_inc(route_steps.sem, 1)
                dve.wait_ge(route_steps.sem, route_steps.value(g, 14))
                V.reciprocal(exp_inv[:], exp_sum[:]).then_inc(route_steps.sem, 1)
                dve.wait_ge(ranks_done.sem, ranks_done.value(g, 1))
                V.tensor_tensor(ranked[:], one_hot[:], work[1][:, 0:G * E].rearrange("p (j e) -> p j e", e=E).unsqueeze(2)
                                     .to_broadcast([P, G, TOPK, E]), ALU.mult).then_inc(route_steps.sem, 1)
                V.tensor_reduce(group_taken[:], taken[:].rearrange("p j e -> p e j"), AX.X, ALU.add).then_inc(route_steps.sem, 1)
                dve.wait_ge(route_steps.sem, route_steps.value(g, 17))
                V.tensor_tensor(counted[:], counted[:], group_taken[:], ALU.add).then_inc(route_steps.sem, 1)
                V.reduce_sum(rank[:], ranked[:].rearrange("p j k e -> p (j k) e"), AX.X).then_inc(route_steps.sem, 1)
                dve.wait_ge(route_steps.sem, route_steps.value(g, 19))
                V.tensor_single_scalar(kept[:], rank[:], float(CAP), ALU.is_lt).then_inc(route_steps.sem, 1)
                V.tensor_single_scalar(base[:], expert[:].rearrange("p j k -> p (j k)"), float(CAP), ALU.mult).then_inc(route_steps.sem, 1)
                V.tensor_tensor(top_shifted[:], top_shifted[:], exp_inv[:].unsqueeze(2).to_broadcast([P, G, TOPK]), ALU.mult).then_inc(route_steps.sem, 1)
                dve.wait_ge(route_steps.sem, route_steps.value(g, 22))
                V.tensor_tensor(pair_weight[:, bass.ds(g * (G * TOPK), G * TOPK)], top_shifted[:].rearrange("p j k -> p (j k)"),
                                     kept[:], ALU.mult).then_inc(route_steps.sem, 1)
                V.tensor_single_scalar(pair_rank[:, bass.ds(g * (G * TOPK), G * TOPK)], rank[:], float(CAP - 1), ALU.min).then_inc(route_steps.sem, 1)
                V.tensor_copy(pair_expert[:, bass.ds(g * (G * TOPK), G * TOPK)], expert[:].rearrange("p j k -> p (j k)")).then_inc(route_steps.sem, 1)
                V.tensor_tensor(slot[:], rank[:], base[:], ALU.add).then_inc(route_steps.sem, 1)
                V.tensor_scalar(kept[:], kept[:], -float(NONE), float(NONE), ALU.mult, ALU.add).then_inc(route_steps.sem, 1)
                dve.wait_ge(route_steps.sem, route_steps.value(g, 27))
                dve.wait_ge(scatter_over.sem, scatter_over.value(g, 0))
                V.tensor_tensor(scatter_to[:], slot[:], kept[:], ALU.add).then_inc(route_steps.sem, 1)
                V.tensor_copy(tokens[:], tokens_f[:]).then_inc(route_steps.sem, 1)
                dve.wait_ge(route_steps.sem, route_steps.value(g, 29))
                V.tensor_single_scalar(tokens_f[:], tokens_f[:], float(G * P), ALU.add).then_inc(route_steps.sem, 1)

            def shared_inner(g, c):
                dve.wait_ge(gate_done.sem, gate_done.value(g, c + 1))
                dve.wait_ge(hT_hi_done.sem, hT_hi_done.value(g, c))
                dve.wait_ge(hT_lo_done.sem, hT_lo_done.value(g, c))
                V.scalar_tensor_tensor(hT[:], gate[:], 1.0, S[:, 2 * (c % 2), :], ALU.add, ALU.mult).then_inc(h_steps.sem, 1)
                dve.wait_ge(h_steps.sem, h_steps.value(g, 2 * c + 1))
                V.scalar_tensor_tensor(hT[:], hT[:], 0.5, S[:, 2 * (c % 2) + 1, :], ALU.mult, ALU.mult).then_inc(h_steps.sem, 1)
                dve.wait_ge(hT_hi_done.sem, hT_hi_done.value(g, c + 1))
                low(hT_lo[:, c, :], hT[:], hT_hi[:, c, :]).then_inc(hT_lo_done.sem, 1)

            def shared_out(g, j):
                dve.wait_ge(down_done.sem, down_done.value(g, j + 1))
                dve.wait_ge(acc_stored[j % 2].sem, acc_stored[j % 2].value(g, 16 * (j // 2)))
                V.tensor_tensor(acc[:, j % 2, :], work[j % 2][:], x[:, j, :], ALU.add).then_inc(acc_done.sem, 1)

            def v_out(g, j):
                dve.wait_ge(v_done.sem, v_done.value(g, j + 1))
                dve.wait_ge(mixed_done.sem, mixed_done.value(g, 0))
                V.tensor_copy(v[:, j, :, 0:HD], work[j % 2][:].rearrange("p (h n) -> p h n", n=HD)).then_inc(v_read.sem, 1)

            def step(g, more):
                maximum_and_shift(g, 0)
                v_out(g, 0)
                v_out(g, 1)
                maximum_and_shift(g, 1)
                v_out(g, 2)
                v_out(g, 3)
                mix_out(g, 0)
                norm(g, G)
                for j in range(1, G):
                    if j + 1 < G:
                        maximum_and_shift(g, j + 1)
                    mix_out(g, j)
                    if j + 1 < G:
                        normed_low(g, G + j - 1)
                    norm(g, G + j)
                normed_low(g, 2 * G - 2)
                normed_low(g, 2 * G - 1)
                shared_inner(g, 0)
                choose(g)
                shared_inner(g, 1)
                if more:
                    norm(g + 1, 0, x_next)
                place(g)
                shared_inner(g, 2)
                if more:
                    norm(g + 1, 1, x_next)
                shared_inner(g, 3)
                if more:
                    normed_low(g + 1, 0)
                    norm(g + 1, 2, x_next)
                    normed_low(g + 1, 1)
                shared_out(g, 0)
                if more:
                    norm(g + 1, 3, x_next)
                    normed_low(g + 1, 2)
                shared_out(g, 1)
                if more:
                    normed_low(g + 1, 3)
                shared_out(g, 2)
                shared_out(g, 3)

            with dve.Fori(0, NG - 1) as i:
                step(i, True)
            step(NG - 1, False)

        @block.tensor
        def _(pe):
            grant(pe, up_done, scored, mixed_done, down_done, turned, probs_turned, logits_done)

            def turn_normed(g, n):
                j = n % G
                pe.wait_ge(norm_steps.sem, norm_steps.value(g, 3 * n + 3))
                pe.wait_ge(xnT_lo_done.sem, xnT_lo_done.value(g, n - 1))
                if n >= G:
                    pe.wait_ge(probsT_read.sem, probsT_read.value(g, 4 * (min(j + 1, G - 1) + 1)))
                for k in range(KD):
                    last = nc.tensor.transpose(turn[n % 2][:, k * P:(k + 1) * P], xn[:, 2 * (n // G) + j % 2, k * P:(k + 1) * P], ident[:])
                last.then_inc(turned.sem, 1)

            def tokens_of(j):
                return slice(j * P, (j + 1) * P)

            def project_qk(g, c):
                if c < 4:
                    pe.wait_ge(h_steps.sem, h_steps.value(g, 0))
                else:
                    pe.wait_ge(qk_read.sem, qk_read.value(g, c - 3))
                for k in range(KD):
                    cs = slice(c * P, (c + 1) * P)
                    last = product(nc, S[:, c % 4, :], (wqk[0][:, k, cs], wqk[1][:, k, cs]),
                                   (xnT_hi[:, k, :], xnT_lo[:, k, :]), k == 0, k == KD - 1)
                last.then_inc(qk_done.sem, 1)

            def from_tokens(out, j, a, w, ks, first=True):
                for k in range(ks):
                    last = product(nc, out, (a[0][:, k, tokens_of(j)], a[1][:, k, tokens_of(j)]), (w[0][:, k, :], w[1][:, k, :]), k == 0, k == ks - 1)
                return last

            def project_v(g, j):
                pe.wait_ge(acc_done.sem, acc_done.value(g, 0))
                if j >= 2:
                    pe.wait_ge(v_read.sem, v_read.value(g, j - 1))
                from_tokens(work[j % 2][:], j, (xnT_hi, xnT_lo), wv, KD).then_inc(v_done.sem, 1)

            def score(g, j):
                if j == 0:
                    pe.wait_ge(qk_read.sem, qk_read.value(g, CQ))
                else:
                    pe.wait_ge(shift_done.sem, shift_done.value(g, j))
                for h in range(H):
                    c, r = h // 4, h % 4
                    rows = slice(r * HD, (r + 1) * HD)
                    last = nc.tensor.matmul(S[:, r, c * P:(c + 1) * P], qkT[rows, c, tokens_of(j)], qkT[rows, CQ // 2 + c, tokens_of(j)],
                                            start=True, stop=True)
                last.then_inc(scored.sem, 1)

            def turn_probs(g, j):
                pe.wait_ge(exp_done.sem, exp_done.value(g, j + 1))
                pe.wait_ge(xnT_lo_done.sem, xnT_lo_done.value(g, G if j == 0 else G + max(0, j - 1)))
                for q in range(4):
                    pe.wait_ge(probsT_read.sem, probsT_read.value(g, 4 * j + q - 1))
                    for t in range(4):
                        last = nc.tensor.transpose(turn[q % 2][:, t * P:(t + 1) * P], probs[:, 4 * q + t, :], ident[:])
                    last.then_inc(probs_turned.sem, 1)

            def mix(g, j):
                pe.wait_ge(probsT_read.sem, probsT_read.value(g, 4 * j + 4))
                pe.wait_ge(v_read.sem, v_read.value(g, G))
                pe.wait_ge(mix_steps.sem, mix_steps.value(g, 6 * j))
                for h in range(H):
                    last = nc.tensor.matmul(work[h // 8][:, (h % 8) * VW:(h % 8 + 1) * VW], probsT[:, h, :], v[:, j, h, :], start=True, stop=True)
                last.then_inc(mixed_done.sem, 1)

            def gate_logits(g):
                pe.wait_ge(mix_steps.sem, mix_steps.value(g, 6 * G))
                for k in range(KD):
                    last = product(nc, work[1][0:E, :], (wg[0][:, k, :], wg[1][:, k, :]), (xnT_hi[:, k, :], xnT_lo[:, k, :]), k == 0, k == KD - 1)
                last.then_inc(logitsT_done.sem, 1)

            def turn_logits(g):
                pe.wait_ge(logitsT_read.sem, logitsT_read.value(g, 1))
                pe.nop(nofuse=True)
                for j in range(G):
                    last = nc.tensor.transpose(work[0][:, j * E:(j + 1) * E], logitsT[:, tokens_of(j)], ident[0:E, 0:E])
                last.then_inc(logits_done.sem, 1)

            def rank_pairs(g):
                pe.wait_ge(route_steps.sem, route_steps.value(g, R_TAKEN))
                for j in range(G):
                    out = work[1][:, j * E:(j + 1) * E]
                    nc.tensor.matmul(out, before[:], taken[:, j, :], start=True, stop=False)
                    for i in range(j):
                        nc.tensor.matmul(out, ones[:], taken[:, i, :], start=False, stop=False)
                    last = nc.tensor.matmul(out, ones[:], counted[:], start=False, stop=True)
                last.then_inc(ranks_done.sem, 1)

            def shared_up(g, c):
                if c < 2:
                    pe.wait_ge(shift_done.sem, shift_done.value(g, G))
                else:
                    pe.wait_ge(h_steps.sem, h_steps.value(g, 2 * (c - 1)))
                for part in range(2):
                    cs = slice((part * CF + c) * P, (part * CF + c + 1) * P)
                    for k in range(KD):
                        last = product(nc, S[:, 2 * (c % 2) + part, :], (ws13[0][:, k, cs], ws13[1][:, k, cs]),
                                       (xnT_hi[:, k, :], xnT_lo[:, k, :]), k == 0, k == KD - 1)
                last.then_inc(up_done.sem, 1)

            def shared_down(g, j):
                pe.wait_ge(hT_lo_done.sem, hT_lo_done.value(g, CF))
                if j == 0:
                    pe.wait_ge(logits_steps.sem, logits_steps.value(g, 1))
                elif j == 1:
                    pe.wait_ge(route_steps.sem, route_steps.value(g, R_RANKED))
                else:
                    pe.wait_ge(acc_done.sem, acc_done.value(g, j - 1))
                from_tokens(work[j % 2][:], j, (hT_hi, hT_lo), ws2, CF).then_inc(down_done.sem, 1)

            def step(g, more):
                pe.wait_ge(xnT_lo_done.sem, xnT_lo_done.value(g, G))
                pe.wait_ge(w_lo, 3)
                for c in range(CQ):
                    project_qk(g, c)
                score(g, 0)
                pe.wait_ge(w_lo, 4)
                project_v(g, 0)
                project_v(g, 1)
                score(g, 1)
                turn_probs(g, 0)
                project_v(g, 2)
                project_v(g, 3)
                mix(g, 0)
                for j in range(1, G):
                    if j + 1 < G:
                        score(g, j + 1)
                    turn_probs(g, j)
                    mix(g, j)
                    turn_normed(g, G + j - 1)
                turn_normed(g, 2 * G - 1)
                pe.wait_ge(xnT_lo_done.sem, xnT_lo_done.value(g, 2 * G))
                pe.wait_ge(w_lo, NW + 1)
                gate_logits(g)
                shared_up(g, 0)
                turn_logits(g)
                shared_up(g, 1)
                rank_pairs(g)
                shared_up(g, 2)
                shared_up(g, 3)
                if more:
                    turn_normed(g + 1, 0)
                    turn_normed(g + 1, 1)
                shared_down(g, 0)
                if more:
                    turn_normed(g + 1, 2)
                shared_down(g, 1)
                if more:
                    turn_normed(g + 1, 3)
                shared_down(g, 2)
                shared_down(g, 3)

            pe.wait_ge(const_landed, 16 * 3)
            pe.wait_ge(setup, 1)
            for n in range(G):
                turn_normed(0, n)
            with pe.Fori(0, NG - 1) as i:
                step(i, True)
            step(NG - 1, False)


HE = 256
KH = HE // P
UNROLL = 4


def experts(nc, normed, token_of_slot, W_expert, expert_count, pair_rank, pair_expert, gather_rows,
            ident_in, before_in, y_rows):
    W13 = KD * 2 * HE
    WE = W13 + KH * D
    PAIRS = 16
    with ExitStack() as stack:
        m = Memory(nc, stack, "ex")
        weights = m.sb("weights", [P, UNROLL, WE])
        pair_token = m.sb("pair_token", [P, UNROLL, 1], I32)
        xg = m.sb("xg", [P, UNROLL, D])
        xgT = m.sb("xgT", [P, 2, D])
        gate = m.sb("gate", [P, 2, HE])
        h = m.sb("h", [P, 2, HE])
        hT = m.sb("hT", [P, 2, HE])
        y = m.sb("y", [P, UNROLL, D])
        ident = m.sb("ident", [P, P])
        before = m.sb("before", [P, P])
        ones = m.sb("ones", [P, 1])
        thresholds = m.sb("thresholds", [E, CAP // P])
        over = m.sb("over", [E, CAP // P])
        count = m.sb("count", [E, 1])
        blocks = m.sb("blocks", [E, 1])
        first_block = m.sb("first_block", [E, 1])
        end_block = m.sb("end_block", [E, 1])
        expert_id = m.sb("expert_id", [E, 1])
        expert_row = m.sb("expert_row", [E, 1])
        first_row = m.sb("first_row", [E, 1])
        block_id = m.sb("block_id", [E, NBLOCKS])
        block_row = m.sb("block_row", [E, NBLOCKS])
        started = m.sb("started", [E, NBLOCKS])
        parts = m.sb("parts", [E, 3, NBLOCKS])
        spare_row = m.sb("spare_row", [1, NBLOCKS])
        unused = m.sb("unused", [1, NBLOCKS])
        blocks_wide = m.sb("blocks_wide", [E, P])
        first_of = m.sb("first_of", [P, E])
        iota_e = m.sb("iota_e", [P, E])
        one_hot = m.sb("one_hot", [P, PAIRS, E])
        pair_first = m.sb("pair_first", [P, PAIRS])
        table = m.sb("table", [1, 2, NBLOCKS], I32)

        turn = [m.ps("turn0", [P, BANK]), m.ps("turn1", [P, BANK])]
        up = [m.ps("up0", [P, BANK]), m.ps("up1", [P, BANK])]
        hturn = [m.ps("hturn0", [P, BANK]), m.ps("hturn1", [P, BANK])]
        down = [m.ps("down0", [P, BANK]), m.ps("down1", [P, BANK])]

        const_landed = m.sem("const_landed")
        setup = m.sem("setup")
        table_pe = m.sem("table_pe")
        table_steps = m.sem("table_steps")
        place_steps = m.sem("place_steps")
        weights_landed = [m.tally(f"weights_landed{u}", 16) for u in range(UNROLL)]
        pairs_landed = [m.tally(f"pairs_landed{u}", 16) for u in range(UNROLL)]
        gathered = [m.tally(f"gathered{u}", 16) for u in range(UNROLL)]
        stored = [m.tally(f"stored{u}", 16, 1) for u in range(UNROLL)]
        turned = m.tally("turned", 1, UNROLL)
        xgT_done = m.tally("xgT_done", 1)
        up_done = m.tally("up_done", 1)
        gate_done = m.tally("gate_done", 1)
        h_steps = m.tally("h_steps", 2, 4)
        h_turned = m.tally("h_turned", 1, 2)
        hT_done = m.tally("hT_done", 1, 2)
        down_done = m.tally("down_done", 1, UNROLL)
        y_done = m.tally("y_done", 1, 2)
        block = stack.enter_context(nc.Block())

        def loop(eng, step, ahead):
            with eng.Fori(0, NBLOCKS // UNROLL - 1) as i:
                for u in range(UNROLL):
                    step(i * UNROLL + u, u, i, 0)
            for u in range(UNROLL):
                j = NBLOCKS - UNROLL + u
                step(j, u, NBLOCKS // UNROLL - 1, max(0, j + ahead - NBLOCKS + 1))

        @block.sync
        def _(sp):
            grant(sp, *stored)
            sp.dma_start(ident[:], ident_in).then_inc(const_landed, 16)
            sp.dma_start(before[:], before_in).then_inc(const_landed, 16)
            sp.wait_ge(table_steps, 15)

            def fetch(j, u, i):
                row = sp.value_load(table[0:1, 0, bass.ds(j, 1)], min_val=0, max_val=ROWS - P)
                expert = sp.value_load(table[0:1, 1, bass.ds(j, 1)], min_val=0, max_val=E - 1)
                sp.wait_ge(turned.sem, turned.value(j, 1 - UNROLL))
                sp.nop(nofuse=True)
                sp.dma_start(pair_token[:, u, :], token_of_slot[bass.ds(row, P), :]).then_inc(pairs_landed[u].sem, 16)
                sp.wait_ge(down_done.sem, down_done.value(j, 1 - UNROLL))
                sp.nop(nofuse=True)
                sp.dma_start(weights[:, u, :], W_expert[bass.ds(expert, 1)].rearrange("one p n -> p (one n)")).then_inc(weights_landed[u].sem, 16)

            def store(j, u):
                sp.wait_ge(y_done.sem, y_done.value(j, 1))
                sp.nop(nofuse=True)
                sp.dma_start(y_rows[bass.ds(j * P, P), :], y[:, u, :]).then_inc(stored[u].sem, 16)

            AHEAD = UNROLL - 1
            for j in range(AHEAD):
                fetch(j, j, 0)

            def step(j, u, i, late):
                if late == 0:
                    v = (u + AHEAD) % UNROLL
                    fetch(j + AHEAD, v, i)
                store(j, u)

            loop(sp, step, AHEAD)
            for u in range(UNROLL):
                sp.wait_ge(stored[u].sem, stored[u].value(NBLOCKS // UNROLL - 1, 16))
                sp.nop(nofuse=True)

        @block.gpsimd
        def _(pool):
            nc.gpsimd.memset(ones[:], 1.0)
            nc.gpsimd.iota(thresholds[:], pattern=[[P, CAP // P]], base=0, channel_multiplier=0, allow_small_or_imprecise_dtypes=True)
            nc.gpsimd.iota(expert_id[:], pattern=[[0, 1]], base=0, channel_multiplier=1, allow_small_or_imprecise_dtypes=True)
            nc.gpsimd.iota(expert_row[:], pattern=[[0, 1]], base=0, channel_multiplier=CAP, allow_small_or_imprecise_dtypes=True)
            nc.gpsimd.iota(iota_e[:], pattern=[[1, E]], base=0, channel_multiplier=0, allow_small_or_imprecise_dtypes=True)
            nc.gpsimd.iota(block_id[:], pattern=[[1, NBLOCKS]], base=0, channel_multiplier=0, allow_small_or_imprecise_dtypes=True)
            nc.gpsimd.iota(block_row[:], pattern=[[P, NBLOCKS]], base=0, channel_multiplier=0, allow_small_or_imprecise_dtypes=True)
            nc.gpsimd.iota(spare_row[:], pattern=[[P, NBLOCKS]], base=NONE, channel_multiplier=0, allow_small_or_imprecise_dtypes=True).then_inc(setup, 1)

            def step(j, u, i, late):
                pool.wait_ge(pairs_landed[u].sem, pairs_landed[u].value(i, 16))
                pool.nop(nofuse=True)
                pool.wait_ge(turned.sem, turned.value(j, 1 - UNROLL))
                pool.nop(nofuse=True)
                pool.indirect_dma_start(xg[:, u, :], None, normed, bass.IndirectOffsetOnAxis(ap=pair_token[:, u, :], axis=0))\
                    .then_inc(gathered[u].sem, 16)

            loop(pool, step, 0)

        @block.scalar
        def _(act):
            grant(act, y_done, hT_done)

            def step(j, u, i, late):
                b = u % 2
                act.wait_ge(up_done.sem, up_done.value(j, 1))
                act.wait_ge(h_steps.sem, h_steps.value(j, -2))
                nc.scalar.activation(gate[:, b, :], up[b][:, 0:HE], ACT.Tanh, scale=0.5).then_inc(gate_done.sem, 1)
                act.wait_ge(h_turned.sem, h_turned.value(j, 1))
                act.wait_ge(down_done.sem, down_done.value(j, -1))
                nc.scalar.activation(hT[:, b, :], hturn[b][:, 0:HE], ACT.Copy).then_inc(hT_done.sem, 1)
                act.wait_ge(down_done.sem, down_done.value(j, 1))
                act.wait_ge(stored[u].sem, stored[u].value(i, 0))
                nc.scalar.activation(y[:, u, :], down[b][:], ACT.Copy).then_inc(y_done.sem, 1)

            loop(act, step, 0)

        @block.vector
        def _(dve):
            V = nc.vector
            grant(dve, h_steps)
            dve.wait_ge(setup, 1)
            dve.wait_ge(table_pe, 1)
            V.tensor_copy(count[:], up[0][0:E, 0:1]).then_inc(table_steps, 1)
            dve.wait_ge(table_steps, 1)
            V.tensor_scalar(over[:], thresholds[:], count[:], None, ALU.is_lt).then_inc(table_steps, 1)
            dve.wait_ge(table_steps, 2)
            V.reduce_sum(blocks[:], over[:], AX.X).then_inc(table_steps, 1)
            dve.wait_ge(table_steps, 3)
            V.tensor_copy(blocks_wide[:], blocks[:].to_broadcast([E, P])).then_inc(table_steps, 1)
            dve.wait_ge(table_pe, 2)
            V.tensor_copy(first_block[:], up[1][0:E, 0:1]).then_inc(table_steps, 1)
            dve.wait_ge(table_steps, 5)
            V.tensor_tensor(end_block[:], first_block[:], blocks[:], ALU.add).then_inc(table_steps, 1)
            V.scalar_tensor_tensor(first_row[:], first_block[:], -float(P), expert_row[:], ALU.mult, ALU.add).then_inc(table_steps, 1)
            V.tensor_scalar(started[:], block_id[:], first_block[:], None, ALU.is_ge).then_inc(table_steps, 1)
            dve.wait_ge(table_steps, 8)
            V.scalar_tensor_tensor(parts[:, 2, :], block_id[:], end_block[:], started[:], ALU.is_lt, ALU.mult).then_inc(table_steps, 1)
            dve.wait_ge(table_steps, 9)
            V.scalar_tensor_tensor(parts[:, 0, :], block_row[:], first_row[:], parts[:, 2, :], ALU.add, ALU.mult).then_inc(table_steps, 1)
            V.tensor_scalar(parts[:, 1, :], parts[:, 2, :], expert_id[:], None, ALU.mult).then_inc(table_steps, 1)
            dve.wait_ge(table_pe, 3)
            V.tensor_scalar(unused[:], up[0][0:1, 2 * NBLOCKS:3 * NBLOCKS], -1.0, 1.0, ALU.mult, ALU.add).then_inc(table_steps, 1)
            dve.wait_ge(table_steps, 12)
            V.tensor_tensor(unused[:], unused[:], spare_row[:], ALU.mult).then_inc(table_steps, 1)
            dve.wait_ge(table_steps, 13)
            V.tensor_tensor(table[:, 0, :], unused[:], up[0][0:1, 0:NBLOCKS], ALU.add).then_inc(table_steps, 1)
            V.tensor_copy(table[:, 1, :], up[0][0:1, NBLOCKS:2 * NBLOCKS]).then_inc(table_steps, 1)

            V.tensor_single_scalar(first_of[:], down[0][:, 0:E], float(P), ALU.mult).then_inc(place_steps, 1)
            for n in range(B * TOPK // PAIRS):
                ps = slice(n * PAIRS, (n + 1) * PAIRS)
                dve.wait_ge(place_steps, 4 * n + 1)
                V.tensor_tensor(one_hot[:], iota_e[:].unsqueeze(1).to_broadcast([P, PAIRS, E]),
                                pair_expert[:, ps].unsqueeze(2).to_broadcast([P, PAIRS, E]), ALU.is_equal).then_inc(place_steps, 1)
                dve.wait_ge(place_steps, 4 * n + 2)
                V.tensor_tensor(one_hot[:], one_hot[:], first_of[:].unsqueeze(1).to_broadcast([P, PAIRS, E]),
                                ALU.mult).then_inc(place_steps, 1)
                dve.wait_ge(place_steps, 4 * n + 3)
                V.reduce_sum(pair_first[:], one_hot[:], AX.X).then_inc(place_steps, 1)
                dve.wait_ge(place_steps, 4 * n + 4)
                V.tensor_tensor(gather_rows[:, ps], pair_first[:], pair_rank[:, ps], ALU.add).then_inc(place_steps, 1)

            def x_turned(j, b):
                dve.wait_ge(turned.sem, turned.value(j, 1))
                dve.wait_ge(up_done.sem, up_done.value(j, -1))
                V.tensor_copy(xgT[:, b, :], turn[b][:]).then_inc(xgT_done.sem, 1)

            for j in range(2):
                dve.wait_ge(turned.sem, turned.value(j, 1))
                V.tensor_copy(xgT[:, j, :], turn[j][:]).then_inc(xgT_done.sem, 1)

            def step(j, u, i, late):
                b = u % 2
                dve.wait_ge(gate_done.sem, gate_done.value(j, 1))
                dve.wait_ge(h_turned.sem, h_turned.value(j, -1))
                V.scalar_tensor_tensor(h[:, b, :], gate[:, b, :], 1.0, up[b][:, 0:HE], ALU.add, ALU.mult).then_inc(h_steps.sem, 1)
                dve.wait_ge(h_steps.sem, h_steps.value(j, 1))
                V.scalar_tensor_tensor(h[:, b, :], h[:, b, :], 0.5, up[b][:, HE:2 * HE], ALU.mult, ALU.mult).then_inc(h_steps.sem, 1)
                if late == 0:
                    x_turned(j + 2, b)

            loop(dve, step, 2)

        @block.tensor
        def _(pe):
            grant(pe, turned, h_turned, down_done)

            def turn_x(j, u, b, i):
                pe.wait_ge(gathered[u].sem, gathered[u].value(i, 16))
                pe.wait_ge(xgT_done.sem, xgT_done.value(j, -1))
                for k in range(KD):
                    last = nc.tensor.transpose(turn[b][:, k * P:(k + 1) * P], xg[:, u, k * P:(k + 1) * P], ident[:])
                last.then_inc(turned.sem, 1)

            def go_up(j, u, b, i):
                pe.wait_ge(xgT_done.sem, xgT_done.value(j, 1))
                pe.wait_ge(weights_landed[u].sem, weights_landed[u].value(i, 16))
                pe.wait_ge(h_steps.sem, h_steps.value(j, -2))
                for k in range(KD):
                    last = nc.tensor.matmul(up[b][:], xgT[:, b, k * P:(k + 1) * P], weights[:, u, k * 2 * HE:(k + 1) * 2 * HE],
                                            start=k == 0, stop=k == KD - 1)
                last.then_inc(up_done.sem, 1)

            pe.wait_ge(const_landed, 32)
            pe.wait_ge(setup, 1)
            nc.tensor.matmul(up[0][0:E, 0:1], expert_count[:], ones[:], start=True, stop=True).then_inc(table_pe, 1)
            pe.wait_ge(table_steps, 4)
            nc.tensor.matmul(down[0][:, 0:E], blocks_wide[:], before[0:E, 0:E], start=True, stop=True)
            nc.tensor.matmul(up[1][0:E, 0:1], before[0:E, 0:E], blocks[:], start=True, stop=True).then_inc(table_pe, 1)
            pe.wait_ge(table_steps, 11)
            nc.tensor.matmul(up[0][0:1, 0:3 * NBLOCKS], ones[0:E, :], parts[:].rearrange("e a j -> e (a j)"), start=True, stop=True).then_inc(table_pe, 1)
            pe.wait_ge(table_steps, 15)
            pe.wait_ge(place_steps, 1)
            for j in range(2):
                pe.wait_ge(gathered[j].sem, 16)
                for k in range(KD):
                    last = nc.tensor.transpose(turn[j][:, k * P:(k + 1) * P], xg[:, j, k * P:(k + 1) * P], ident[:])
                last.then_inc(turned.sem, 1)
            go_up(0, 0, 0, 0)

            def step(j, u, i, late):
                b = u % 2
                if late < 2:
                    v = (u + 1) % UNROLL
                    go_up(j + 1, v, v % 2, i + (u + 1) // UNROLL)
                if late < 1:
                    v = (u + 2) % UNROLL
                    turn_x(j + 2, v, b, i + (u + 2) // UNROLL)
                pe.wait_ge(h_steps.sem, h_steps.value(j, 2))
                pe.wait_ge(hT_done.sem, hT_done.value(j, -1))
                for k in range(KH):
                    last = nc.tensor.transpose(hturn[b][:, k * P:(k + 1) * P], h[:, b, k * P:(k + 1) * P], ident[:])
                last.then_inc(h_turned.sem, 1)
                pe.wait_ge(hT_done.sem, hT_done.value(j, 1))
                pe.wait_ge(y_done.sem, y_done.value(j, -1))
                for k in range(KH):
                    last = nc.tensor.matmul(down[b][:], hT[:, b, k * P:(k + 1) * P], weights[:, u, W13 + k * D:W13 + (k + 1) * D],
                                            start=k == 0, stop=k == KH - 1)
                last.then_inc(down_done.sem, 1)

            loop(pe, step, 2)


def combine(nc, acc_in, y_rows, gather_rows, pair_weight, out):
    with ExitStack() as stack:
        m = Memory(nc, stack, "co")
        acc = m.sb("acc", [P, 2, D])
        rows = m.sb("rows", [P, 2, TOPK], I32)
        weight = m.sb("weight", [P, 2, TOPK])
        y = m.sb("y", [P, 2, TOPK, D])
        acc_landed = [m.tally(f"acc_landed{s}", 16) for s in range(2)]
        y_landed = [[m.tally(f"y_landed{s}{k}", 16) for k in range(TOPK)] for s in range(2)]
        rows_done = m.tally("rows_done", 2)
        sum_steps = m.tally("sum_steps", TOPK)
        stored = [m.tally(f"stored{s}", 16) for s in range(2)]
        block = stack.enter_context(nc.Block())

        @block.sync
        def _(sp):
            for s in range(2):
                sp.dma_start(acc[:, s, :], acc_in[s]).then_inc(acc_landed[s].sem, 16)

            def step(b, s, i, more):
                sp.wait_ge(sum_steps.sem, sum_steps.value(b, TOPK))
                sp.nop(nofuse=True)
                sp.dma_start(out[b], acc[:, s, :]).then_inc(stored[s].sem, 16)
                if more:
                    sp.wait_ge(stored[s].sem, stored[s].value(i, 16))
                    sp.nop(nofuse=True)
                    sp.dma_start(acc[:, s, :], acc_in[b + 2]).then_inc(acc_landed[s].sem, 16)

            with sp.Fori(0, B // 2 - 1) as i:
                for s in range(2):
                    step(i * 2 + s, s, i, True)
            for s in range(2):
                step(B - 2 + s, s, B // 2 - 1, False)
            for s in range(2):
                sp.wait_ge(stored[s].sem, stored[s].value(B // 2 - 1, 16))
                sp.nop(nofuse=True)

        @block.gpsimd
        def _(pool):
            with pool.Fori(0, B // 2) as i:
                for s in range(2):
                    pool.wait_ge(rows_done.sem, rows_done.value(i * 2 + s, 1))
                    pool.nop(nofuse=True)
                    for k in range(TOPK):
                        pool.indirect_dma_start(y[:, s, k, :], None, y_rows, bass.IndirectOffsetOnAxis(ap=rows[:, s, k:k + 1], axis=0))\
                            .then_inc(y_landed[s][k].sem, 16)

        @block.vector
        def _(dve):
            V = nc.vector

            def numbers(b, s):
                V.tensor_copy(rows[:, s, :], gather_rows[:, bass.ds(b * TOPK, TOPK)]).then_inc(rows_done.sem, 1)
                V.tensor_copy(weight[:, s, :], pair_weight[:, bass.ds(b * TOPK, TOPK)]).then_inc(rows_done.sem, 1)

            for s in range(2):
                numbers(s, s)

            def step(b, s, i, more):
                dve.wait_ge(acc_landed[s].sem, acc_landed[s].value(i, 16))
                dve.wait_ge(rows_done.sem, rows_done.value(b, 2))
                for k in range(TOPK):
                    dve.wait_ge(y_landed[s][k].sem, y_landed[s][k].value(i, 16))
                    if k:
                        dve.wait_ge(sum_steps.sem, sum_steps.value(b, k))
                    V.scalar_tensor_tensor(acc[:, s, :], y[:, s, k, :], weight[:, s, k:k + 1], acc[:, s, :], ALU.mult, ALU.add)\
                        .then_inc(sum_steps.sem, 1)
                if more:
                    dve.wait_ge(sum_steps.sem, sum_steps.value(b, TOPK))
                    numbers(b + 2, s)

            with dve.Fori(0, B // 2 - 1) as i:
                for s in range(2):
                    step(i * 2 + s, s, i, True)
            for s in range(2):
                step(B - 2 + s, s, B // 2 - 1, False)


def build(nc, x, ctx_rows, ctx_cols, w_cq, w_c, w_q, b_cq, b_c, b_q, W_lT, b_l, W_qkT, W_vT, W_g, W_s13, W_s2, W_expert,
          ident, before, out):
    x1 = nc.dram_tensor("x1_rows", (B, P, D), F32).ap()
    normed = nc.dram_tensor("normed_rows", (B, P, D), F32).ap()
    acc = nc.dram_tensor("acc_rows", (B, P, D), F32).ap()
    token_of_slot = nc.dram_tensor("token_of_slot", (ROWS, 1), I32).ap()
    y_rows = nc.dram_tensor("y_rows", (NBLOCKS * P, D), F32).ap()
    cross_attention(nc, x, ctx_rows, ctx_cols, w_cq, w_c, w_q, b_cq, b_c, b_q, W_lT, b_l, ident, x1)
    with ExitStack() as stack:
        def kept(name, shape, dt):
            return stack.enter_context(nc.sbuf_tensor(name, shape, dt))

        pair_rank = kept("pair_rank", [P, B * TOPK], F32)
        pair_expert = kept("pair_expert", [P, B * TOPK], F32)
        pair_weight = kept("pair_weight", [P, B * TOPK], F32)
        gather_rows = kept("gather_rows", [P, B * TOPK], I32)
        expert_count = kept("expert_count", [P, E], F32)
        self_attention_and_routing(nc, x1, W_qkT, W_vT, W_g, W_s13, W_s2, ident, before, normed, acc,
                                   token_of_slot, pair_rank, pair_expert, pair_weight, expert_count)
        experts(nc, normed.rearrange("b p d -> (b p) d"), token_of_slot, W_expert, expert_count, pair_rank, pair_expert,
                gather_rows, ident, before, y_rows)
        combine(nc, acc, y_rows, gather_rows, pair_weight, out)


def kernel(x, ctx_1024, L0_xattn_w_cq, L0_xattn_b_cq, L0_xattn_w_c, L0_xattn_b_c, L0_xattn_w_q, L0_xattn_b_q,
           L0_xattn_W_l, L0_xattn_b_l, L0_attn_Wq, L0_attn_Wk, L0_attn_Wv, L0_ffn_Wg, L0_ffn_W1, L0_ffn_W2, L0_ffn_W3,
           L0_ffn_Ws1, L0_ffn_Ws2, L0_ffn_Ws3):
    import numpy as np
    import concourse.bacc as bacc
    from concourse.bass_utils import run_bass_kernel_spmd

    def blocks(w):
        w = np.asarray(w)
        return np.ascontiguousarray(w.reshape(-1, P, w.shape[1]).transpose(1, 0, 2))

    def expert_blocks(w):
        w = np.asarray(w)
        return w.reshape(E, -1, P, w.shape[2]).transpose(0, 2, 1, 3)

    ctx = np.asarray(ctx_1024)
    w13 = np.concatenate([expert_blocks(L0_ffn_W1), expert_blocks(L0_ffn_W3)], axis=3)
    arrays = {
        "x": np.asarray(x),
        "ctx_rows": np.ascontiguousarray(ctx).reshape(B, 8, P, CTX // 8 // P * D),
        "ctx_cols": np.ascontiguousarray(ctx.reshape(B, CTX // BANK, BANK, KD, P).transpose(0, 1, 4, 3, 2)).reshape(B, CTX // BANK, P, KD * BANK),
        "w_cq": np.ascontiguousarray(np.asarray(L0_xattn_w_cq).reshape(KD, P).T),
        "w_c": np.asarray(L0_xattn_w_c),
        "w_q": np.ascontiguousarray(np.asarray(L0_xattn_w_q).reshape(KD, P).T),
        "b_cq": np.asarray(L0_xattn_b_cq).reshape(1),
        "b_c": np.asarray(L0_xattn_b_c).reshape(1),
        "b_q": np.asarray(L0_xattn_b_q).reshape(1),
        "W_lT": blocks(np.asarray(L0_xattn_W_l).T),
        "b_l": np.asarray(L0_xattn_b_l),
        "W_qkT": blocks(np.concatenate([np.asarray(L0_attn_Wq).T, np.asarray(L0_attn_Wk).T], axis=1)),
        "W_vT": blocks(np.asarray(L0_attn_Wv).T),
        "W_g": blocks(L0_ffn_Wg),
        "W_s13": blocks(np.concatenate([np.asarray(L0_ffn_Ws1), np.asarray(L0_ffn_Ws3)], axis=1)),
        "W_s2": blocks(L0_ffn_Ws2),
        "W_expert": np.concatenate([w13.reshape(E, P, -1), expert_blocks(L0_ffn_W2).reshape(E, P, -1)], axis=2),
        "ident": np.eye(P, dtype=np.float32),
        "before": np.triu(np.ones((P, P), np.float32), 1),
    }
    nc = bacc.Bacc("TRN2", target_bir_lowering=False, num_devices=1)
    ins = [nc.dram_tensor(name, a.shape, F32, kind="ExternalInput").ap() for name, a in arrays.items()]
    out = nc.dram_tensor("out", (B, P, D), F32, kind="ExternalOutput").ap()
    build(nc, *ins, out)
    return run_bass_kernel_spmd(nc, [arrays], core_ids=[0]).results[0]["out"]
```

```python
from contextlib import ExitStack

import concourse.bass as bass
from concourse import mybir

ALU = mybir.AluOpType
ACT = mybir.ActivationFunctionType
AX = mybir.AxisListType
F32 = mybir.dt.float32
F32R = mybir.dt.float32r
I32 = mybir.dt.int32
U32 = mybir.dt.uint32
MAX_OVER_PARTITIONS = bass.bass_isa.ReduceOp.max

P = 128
B = 16
D = 512
KD = D // P
CTX = 2048
BANK = 512
EPS = 1e-5


class Tally:

    def __init__(self, sem, per, credit=0):
        self.sem, self.per, self.credit = sem, per, credit

    def value(self, batch, k):
        return batch * self.per + (self.credit + k)


def grant(eng, *tallies):
    for t in tallies:
        if t.credit:
            eng.sem_inc(t.sem, t.credit)


class Memory:

    def __init__(self, nc, stack, phase):
        self.nc, self.stack, self.phase = nc, stack, phase

    def sb(self, name, shape, dt=F32):
        return self.stack.enter_context(self.nc.sbuf_tensor(f"{self.phase}_{name}", shape, dt))

    def ps(self, name, shape):
        return self.stack.enter_context(self.nc.psum_tensor(f"{self.phase}_{name}", shape, F32))

    def sem(self, name):
        return self.stack.enter_context(self.nc.semaphore(f"{self.phase}_{name}"))

    def tally(self, name, per, credit=0):
        return Tally(self.sem(name), per, credit)


def product(nc, out, stationary, moving, first, last):
    (sh, sl), (mh, ml) = stationary, moving
    nc.tensor.matmul(out, sh, mh, start=first, stop=False)
    nc.tensor.matmul(out, sh, ml, start=False, stop=False)
    return nc.tensor.matmul(out, sl, mh, start=False, stop=last)


def cross_attention(nc, x, ctx_rows, ctx_cols, w_cq, w_c, w_q, b_cq, b_c, b_q, W_lT, b_l, ident_in, x1_out):
    QC = CTX // BANK
    RC = 8
    NJ = CTX // RC // P
    KH = KD // 2
    NU = 2 * QC
    UNIT = KH * BANK
    RAW = 4
    RING = 8
    KZ = 4 * KD

    with ExitStack() as stack:
        m = Memory(nc, stack, "xa")
        wl_hi = m.sb("wl_hi", [P, KZ, D], F32R)
        wl_lo = m.sb("wl_lo", [P, KZ, D], F32R)
        ident = m.sb("ident", [P, P])
        ones = m.sb("ones", [P, P])
        w_c_rows = m.sb("w_c_rows", [P, D])
        b_l_rows = m.sb("b_l_rows", [P, D])
        w_cq_col = m.sb("w_cq_col", [P, KD])
        w_q_col = m.sb("w_q_col", [P, KD])
        biases = m.sb("biases", [P, 3])
        bias_sum = m.sb("bias_sum", [P, 1])
        raw = m.sb("raw", [P, RAW, UNIT])
        ctx_hi = m.sb("ctx_hi", [P, RING, 2, D], F32R)
        ctx_lo = m.sb("ctx_lo", [P, RING, 2, D], F32R)
        x_in = m.sb("x_in", [P, D])
        x_bias = m.sb("x_bias", [P, D])
        c = m.sb("c", [P, D])
        stats = m.sb("stats", [P, 6])
        mean_var = m.sb("mean_var", [P, 2])
        eps_pow = m.sb("eps_pow", [P, 2])
        var_eps = m.sb("var_eps", [P, 1])
        rstd = m.sb("rstd", [P, 1])
        row_dot = m.sb("row_dot", [P, 1])
        cT = m.sb("cT", [P, D])
        cT_held = m.sb("cT_held", [P, D])
        cT_hi = m.sb("cT_hi", [P, D], F32R)
        cT_lo = m.sb("cT_lo", [P, D], F32R)
        cw = m.sb("cw", [P, D])
        cw_hi = m.sb("cw_hi", [P, D], F32R)
        cw_lo = m.sb("cw_lo", [P, D], F32R)
        chunk_max = m.sb("chunk_max", [P, QC])
        neg_max = m.sb("neg_max", [P, 1])
        probs = m.sb("probs", [P, CTX])
        chunk_sum = m.sb("chunk_sum", [P, QC])
        row_sum = m.sb("row_sum", [P, 1])
        row_inv = m.sb("row_inv", [P, 1])
        tok_max = m.sb("tok_max", [P, 1])
        all_max = m.sb("all_max", [P, 1])
        tok_exp = m.sb("tok_exp", [P, 1])
        tok_inv = m.sb("tok_inv", [P, 1])
        q2c = m.sb("q2c", [P, KD])
        probsT_hi = m.sb("probsT_hi", [P, 2, BANK], F32R)
        probsT_lo = m.sb("probsT_lo", [P, 2, BANK], F32R)
        cq2c = m.sb("cq2c", [P, D])
        cq2c_hi = m.sb("cq2c_hi", [P, D], F32R)
        cq2c_lo = m.sb("cq2c_lo", [P, D], F32R)
        c2q = m.sb("c2q", [P, D])
        c2qT_hi = m.sb("c2qT_hi", [P, D], F32R)
        c2qT_lo = m.sb("c2qT_lo", [P, D], F32R)
        cc2q, cc2q_hi, cc2q_lo = cq2c, cq2c_hi, cq2c_lo
        x1 = m.sb("x1", [P, D])

        scores = m.ps("scores", [P, QC, BANK])
        turn = [m.ps("turn0", [P, BANK]), m.ps("turn1", [P, BANK])]
        summed = m.ps("summed", [P, BANK])
        projected = m.ps("projected", [P, BANK])
        tok_sum_ps = scores[:, 0, 8:9]
        q2c_ps = scores[:, 0, 0:KD]

        const_landed = m.sem("const_landed")
        ones_done = m.sem("ones_done")
        bias_done = m.sem("bias_done")
        weight_landed = [m.sem(f"weight_landed{s}") for s in range(RAW)]
        weight_hi = m.sem("weight_hi")
        weight_lo = m.sem("weight_lo")
        x_landed = m.tally("x_landed", 16)
        landed = [m.tally(f"landed{s}", 16 * 2 * NU // RAW) for s in range(RAW)]
        hi_done = m.tally("hi_done", 2 * NU)
        lo_done = m.tally("lo_done", 2 * NU, RAW)
        norm_steps = m.tally("norm_steps", 4)
        rstd_steps = m.tally("rstd_steps", 2)
        c_turned = m.tally("c_turned", 1)
        cT_done = m.tally("cT_done", 1)
        cw_done = m.tally("cw_done", KD)
        cT_hi_done = m.tally("cT_hi_done", 1)
        cT_lo_done = m.tally("cT_lo_done", 1)
        cw_hi_done = m.tally("cw_hi_done", 1)
        cw_lo_done = m.tally("cw_lo_done", 1)
        scored = m.tally("scored", QC, QC)
        max_done = m.tally("max_done", QC + 1)
        tok_max_done = m.tally("tok_max_done", 1)
        all_max_done = m.tally("all_max_done", 1)
        exp_done = m.tally("exp_done", QC)
        tok_exp_done = m.tally("tok_exp_done", 1)
        sum_steps = m.tally("sum_steps", 2, 1)
        probs_turned = m.tally("probs_turned", QC, 1)
        probsT_hi_done = m.tally("probsT_hi_done", QC)
        probsT_lo_done = m.tally("probsT_lo_done", QC, QC)
        q2c_summed = m.tally("q2c_summed", 1, 1)
        q2c_steps = m.tally("q2c_steps", 2 + KD)
        cq2c_hi_done = m.tally("cq2c_hi_done", 1)
        cq2c_lo_done = m.tally("cq2c_lo_done", 1)
        held = m.tally("held", 1)
        gathered = m.tally("gathered", QC, QC)
        c_projected = m.tally("c_projected", 2, 2)
        c2q_done = m.tally("c2q_done", 1, 1)
        c2q_turned = m.tally("c2q_turned", 1)
        c2qT_hi_done = m.tally("c2qT_hi_done", 1)
        c2qT_lo_done = m.tally("c2qT_lo_done", 1, 1)
        cc2q_done = m.tally("cc2q_done", 1, 1)
        cc2q_hi_done = m.tally("cc2q_hi_done", 1)
        cc2q_lo_done = m.tally("cc2q_lo_done", 1)
        z_done = m.tally("z_done", 1, 1)
        x1_done = m.tally("x1_done", 1, 1)
        x_bias_done = m.tally("x_bias_done", 1, 1)
        x1_stored = m.tally("x1_stored", 16, 1)
        block = stack.enter_context(nc.Block())

        @block.sync
        def _(sp):
            grant(sp, x1_stored)
            consts = [(ident[:], ident_in), (w_c_rows[:], w_c[None, :].to_broadcast([P, D])),
                      (b_l_rows[:], b_l[None, :].to_broadcast([P, D])),
                      (biases[:, 0:1], b_cq[None, :].to_broadcast([P, 1])),
                      (biases[:, 1:2], b_c[None, :].to_broadcast([P, 1])),
                      (biases[:, 2:3], b_q[None, :].to_broadcast([P, 1]))]
            sp.dma_start(x_in[:], x[0]).then_inc(x_landed.sem, 16)
            for dst, src in consts:
                sp.dma_start(dst, src).then_inc(const_landed, 16)
            sp.dma_start(w_cq_col[:], w_cq).then_inc(const_landed, 16)
            sp.dma_start(w_q_col[:], w_q).then_inc(const_landed, 16)

            def load_x(b):
                sp.wait_ge(x_bias_done.sem, x_bias_done.value(b, 0))
                sp.nop(nofuse=True)
                sp.dma_start(x_in[:], x[b]).then_inc(x_landed.sem, 16)

            def load_cols(b, u):
                sp.wait_ge(lo_done.sem, lo_done.value(b, u - RAW + 1))
                sp.nop(nofuse=True)
                sp.dma_start(raw[:, u % RAW, :], ctx_cols[b, u // 2, :, (u % 2) * UNIT:(u % 2 + 1) * UNIT]
                             ).then_inc(landed[u % RAW].sem, 16)

            def load_rows(b, h):
                sp.wait_ge(lo_done.sem, lo_done.value(b, NU + h - RAW + 1))
                sp.nop(nofuse=True)
                sp.dma_start(raw[:, h % RAW, :], ctx_rows[b, h]).then_inc(landed[h % RAW].sem, 16)

            for u in range(NU):
                load_cols(0, u)
            for w in range(KZ // NJ):
                if w < RAW:
                    sp.wait_ge(lo_done.sem, lo_done.value(0, NU - RAW + w + 1))
                else:
                    sp.wait_ge(weight_lo, w - RAW + 1)
                sp.dma_start(raw[:, w % RAW, :].rearrange("p (j d) -> p j d", j=NJ),
                             W_lT[:, w * NJ:(w + 1) * NJ, :]).then_inc(weight_landed[w % RAW], 16)
            for h in range(NU):
                if h < RAW:
                    sp.wait_ge(weight_lo, KZ // NJ - RAW + h + 1)
                load_rows(0, h)

            load_cols(1, 0)
            load_cols(1, 1)
            load_x(1)
            load_cols(1, 2)
            load_cols(1, 3)

            def step(b, more):
                if more >= 1:
                    for u in range(RAW, NU):
                        load_cols(b + 1, u)
                    for h in range(NU):
                        load_rows(b + 1, h)
                if more >= 2:
                    load_cols(b + 2, 0)
                    load_cols(b + 2, 1)
                sp.wait_ge(x1_done.sem, x1_done.value(b, 1))
                sp.nop(nofuse=True)
                sp.dma_start(x1_out[b], x1[:]).then_inc(x1_stored.sem, 16)
                if more >= 2:
                    load_x(b + 2)
                    load_cols(b + 2, 2)
                    load_cols(b + 2, 3)

            with sp.Fori(0, B - 2) as i:
                step(i, 2)
            step(B - 2, 1)
            step(B - 1, 0)
            sp.wait_ge(x1_stored.sem, x1_stored.value(B - 1, 16))

        @block.gpsimd
        def _(pool):
            nc.gpsimd.memset(eps_pow[:, 0:1], EPS)
            nc.gpsimd.memset(eps_pow[:, 1:2], -0.5)
            nc.gpsimd.memset(ones[:], 1.0).then_inc(ones_done, 1)
            pool.wait_ge(ones_done, 1)

            def inverse_spread(b):
                pool.wait_ge(norm_steps.sem, norm_steps.value(b, 2))
                pool.nop(nofuse=True)
                nc.gpsimd.tensor_tensor(var_eps[:], mean_var[:, 1:2], eps_pow[:, 0:1], ALU.add).then_inc(rstd_steps.sem, 1)
                pool.wait_ge(rstd_steps.sem, rstd_steps.value(b, 1))
                pool.nop(nofuse=True)
                nc.gpsimd.tensor_tensor(rstd[:], var_eps[:], eps_pow[:, 1:2], ALU.pow).then_inc(rstd_steps.sem, 1)

            def token_maximum(b):
                pool.wait_ge(tok_max_done.sem, tok_max_done.value(b, 1))
                pool.nop(nofuse=True)
                nc.gpsimd.partition_all_reduce(all_max[:], tok_max[:], P, MAX_OVER_PARTITIONS).then_inc(all_max_done.sem, 1)

            def x_plus_bias(b):
                pool.wait_ge(x_landed.sem, x_landed.value(b, 16))
                pool.wait_ge(x1_done.sem, x1_done.value(b, 0))
                pool.nop(nofuse=True)
                nc.gpsimd.tensor_tensor(x_bias[:], x_in[:], b_l_rows[:], ALU.add).then_inc(x_bias_done.sem, 1)

            def hold(b):
                pool.wait_ge(cT_done.sem, cT_done.value(b, 1))
                pool.nop(nofuse=True)
                nc.gpsimd.tensor_copy(cT_held[:], cT[:]).then_inc(held.sem, 1)

            def token_part_low(b):
                pool.wait_ge(cq2c_hi_done.sem, cq2c_hi_done.value(b, 1))
                pool.nop(nofuse=True)
                nc.gpsimd.tensor_tensor(cq2c_lo[:], cq2c[:], cq2c_hi[:].bitcast(F32), ALU.subtract).then_inc(cq2c_lo_done.sem, 1)

            def normed_low(b):
                pool.wait_ge(cT_hi_done.sem, cT_hi_done.value(b, 1))
                pool.nop(nofuse=True)
                nc.gpsimd.tensor_tensor(cT_lo[:], cT[:], cT_hi[:].bitcast(F32), ALU.subtract).then_inc(cT_lo_done.sem, 1)

            grant(pool, x_bias_done)
            inverse_spread(0)
            pool.wait_ge(const_landed, 16 * 8)
            normed_low(0)

            def step(b, more):
                token_maximum(b)
                x_plus_bias(b)
                hold(b)
                if more:
                    inverse_spread(b + 1)
                token_part_low(b)
                if more:
                    normed_low(b + 1)

            with pool.Fori(0, B - 1) as i:
                step(i, True)
            step(B - 1, False)

        @block.scalar
        def _(act):
            def high(out, src):
                return nc.scalar.activation(out, src, ACT.Copy)

            def cols_high(b, u):
                act.wait_ge(landed[u % RAW].sem, landed[u % RAW].value(b, 16 * (u // RAW + 1)))
                act.wait_ge(gathered.sem, gathered.value(b, u // 2 + 1 - QC))
                high(ctx_hi[:, u].rearrange("p j d -> p (j d)"), raw[:, u % RAW, :]).then_inc(hi_done.sem, 1)

            def rows_high(b, h):
                act.wait_ge(landed[h % RAW].sem, landed[h % RAW].value(b, 16 * ((NU + h) // RAW + 1)))
                act.wait_ge(scored.sem, scored.value(b, h // 2 + 1))
                high(ctx_hi[:, h].rearrange("p j d -> p (j d)"), raw[:, h % RAW, :]).then_inc(hi_done.sem, 1)

            def exps(b):
                act.wait_ge(max_done.sem, max_done.value(b, QC + 1))
                act.wait_ge(sum_steps.sem, sum_steps.value(b, 0))
                act.wait_ge(probs_turned.sem, probs_turned.value(b, 0))
                for q in range(QC):
                    nc.scalar.activation(probs[:, q * BANK:(q + 1) * BANK], scores[:, q, :], ACT.Exp,
                                         bias=neg_max[:], accum_out=chunk_sum[:, q:q + 1]).then_inc(exp_done.sem, 1)

            def probsT_high(b, g):
                act.wait_ge(probs_turned.sem, probs_turned.value(b, g + 1))
                act.wait_ge(gathered.sem, gathered.value(b, g - 1))
                high(probsT_hi[:, g % 2, :], turn[g % 2][:] if g < 3 else turn[0][:]).then_inc(probsT_hi_done.sem, 1)

            def token_exp(b):
                act.wait_ge(all_max_done.sem, all_max_done.value(b, 1))
                act.wait_ge(q2c_summed.sem, q2c_summed.value(b, 0))
                nc.scalar.activation(tok_exp[:], all_max[:], ACT.Exp, bias=tok_max[:], scale=-1.0).then_inc(tok_exp_done.sem, 1)

            def normed_turned(b):
                act.wait_ge(c_turned.sem, c_turned.value(b, 1))
                act.wait_ge(held.sem, held.value(b, 0))
                nc.scalar.activation(cT[:], turn[1][:], ACT.Copy).then_inc(cT_done.sem, 1)

            def normed_high(b):
                act.wait_ge(cT_done.sem, cT_done.value(b, 1))
                act.wait_ge(c_projected.sem, c_projected.value(b, -1))
                high(cT_hi[:], cT[:]).then_inc(cT_hi_done.sem, 1)

            def normed_weighted_high(b):
                act.wait_ge(cw_done.sem, cw_done.value(b, KD))
                act.wait_ge(scored.sem, scored.value(b, 0))
                high(cw_hi[:], cw[:]).then_inc(cw_hi_done.sem, 1)

            def weighted_out(b):
                act.wait_ge(gathered.sem, gathered.value(b, QC))
                act.wait_ge(sum_steps.sem, sum_steps.value(b, 2))
                nc.scalar.activation(c2q[:], summed[:], ACT.Copy, scale=row_inv[:]).then_inc(c2q_done.sem, 1)

            def weighted_high(b):
                act.wait_ge(c2q_turned.sem, c2q_turned.value(b, 1))
                act.wait_ge(z_done.sem, z_done.value(b, 0))
                high(c2qT_hi[:], turn[1][:]).then_inc(c2qT_hi_done.sem, 1)

            def weighted_product_high(b):
                act.wait_ge(cc2q_done.sem, cc2q_done.value(b, 1))
                high(cc2q_hi[:], cc2q[:]).then_inc(cc2q_hi_done.sem, 1)

            def weight_high_part(w):
                act.wait_ge(weight_landed[w % RAW], 16 * (w // RAW + 1))
                nc.scalar.activation(wl_hi[:, w * NJ:(w + 1) * NJ, :].rearrange("p j d -> p (j d)"),
                                     raw[:, w % RAW, :], ACT.Copy).then_inc(weight_hi, 1)

            def token_part_high(b):
                act.wait_ge(q2c_steps.sem, q2c_steps.value(b, 2 + KD))
                act.wait_ge(z_done.sem, z_done.value(b, 0))
                high(cq2c_hi[:], cq2c[:]).then_inc(cq2c_hi_done.sem, 1)

            grant(act, c2q_done)
            cols_high(0, 0)
            cols_high(0, 1)
            normed_turned(0)
            normed_high(0)
            normed_weighted_high(0)
            for u in range(2, NU):
                cols_high(0, u)
            for w in range(RAW + 1):
                weight_high_part(w)
            exps(0)
            token_exp(0)
            for w in range(RAW + 1, KZ // NJ):
                weight_high_part(w)
            for h in range(NU - 2):
                rows_high(0, h)

            def step(b, more):
                probsT_high(b, 0)
                probsT_high(b, 1)
                rows_high(b, NU - 2)
                rows_high(b, NU - 1)
                if more:
                    cols_high(b + 1, 0)
                    cols_high(b + 1, 1)
                probsT_high(b, 2)
                token_part_high(b)
                if more:
                    cols_high(b + 1, 2)
                    normed_turned(b + 1)
                    cols_high(b + 1, 3)
                    normed_high(b + 1)
                    normed_weighted_high(b + 1)
                probsT_high(b, 3)
                if more:
                    cols_high(b + 1, 4)
                    cols_high(b + 1, 5)
                weighted_out(b)
                if more:
                    cols_high(b + 1, 6)
                    cols_high(b + 1, 7)
                    rows_high(b + 1, 0)
                    rows_high(b + 1, 1)
                weighted_high(b)
                if more:
                    rows_high(b + 1, 2)
                weighted_product_high(b)
                if more:
                    for h in range(3, NU - 2):
                        rows_high(b + 1, h)
                    exps(b + 1)
                    token_exp(b + 1)

            with act.Fori(0, B - 1) as i:
                step(i, True)
            step(B - 1, False)

        @block.vector
        def _(dve):
            V = nc.vector

            def low(out, raw, hi):
                return V.tensor_tensor(out, raw, hi.bitcast(F32), ALU.subtract)

            def unit_low(slot, done):
                dve.wait_ge(hi_done.sem, done)
                low(ctx_lo[:, slot].rearrange("p j d -> p (j d)"), raw[:, slot % RAW, :],
                    ctx_hi[:, slot].rearrange("p j d -> p (j d)")).then_inc(lo_done.sem, 1)

            def cols_low(b, u):
                unit_low(u, hi_done.value(b, u + 1))

            def rows_low(b, h):
                unit_low(h, hi_done.value(b, NU + h + 1))

            def norm_moments(b):
                dve.wait_ge(x_landed.sem, x_landed.value(b, 16))
                V.bn_stats(stats[:], x_in[:]).then_inc(norm_steps.sem, 1)
                dve.wait_ge(norm_steps.sem, norm_steps.value(b, 1))
                dve.nop(nofuse=True)
                V.bn_aggr(mean_var[:], stats[:]).then_inc(norm_steps.sem, 1)

            def norm(b):
                dve.wait_ge(rstd_steps.sem, rstd_steps.value(b, 2))
                V.tensor_scalar(c[:], x_in[:], mean_var[:, 0:1], rstd[:], ALU.subtract, ALU.mult).then_inc(norm_steps.sem, 1)
                dve.wait_ge(norm_steps.sem, norm_steps.value(b, 3))
                V.tensor_tensor_reduce(out=cw[:], in0=c[:], in1=w_c_rows[:], scale=1.0, scalar=0.0,
                                       op0=ALU.mult, op1=ALU.add, accum_out=row_dot[:]).then_inc(norm_steps.sem, 1)

            def normed_weighted(b):
                dve.wait_ge(cT_done.sem, cT_done.value(b, 1))
                dve.wait_ge(norm_steps.sem, norm_steps.value(b, 4))
                for k in range(KD):
                    V.tensor_scalar(cw[:, k * P:(k + 1) * P], cT[:, k * P:(k + 1) * P], w_cq_col[:, k:k + 1],
                                    w_q_col[:, k:k + 1], ALU.mult, ALU.add).then_inc(cw_done.sem, 1)

            def normed_weighted_low(b):
                dve.wait_ge(cw_hi_done.sem, cw_hi_done.value(b, 1))
                low(cw_lo[:], cw[:], cw_hi[:]).then_inc(cw_lo_done.sem, 1)

            def chunk_maximum(b, q):
                dve.wait_ge(scored.sem, scored.value(b, q + 1))
                V.reduce_max(chunk_max[:, q:q + 1], scores[:, q, :], AX.X).then_inc(max_done.sem, 1)

            def row_maximum(b):
                dve.wait_ge(max_done.sem, max_done.value(b, QC))
                V.tensor_reduce(neg_max[:], chunk_max[:], AX.X, ALU.max, negate=True).then_inc(max_done.sem, 1)
                dve.wait_ge(max_done.sem, max_done.value(b, QC + 1))
                V.tensor_scalar(tok_max[:], row_dot[:], neg_max[:], bias_sum[:], ALU.subtract, ALU.add).then_inc(tok_max_done.sem, 1)

            def probsT_low(b, g):
                dve.wait_ge(probsT_hi_done.sem, probsT_hi_done.value(b, g + 1))
                low(probsT_lo[:, g % 2, :], turn[g % 2][:] if g < 3 else turn[0][:], probsT_hi[:, g % 2, :]).then_inc(probsT_lo_done.sem, 1)

            def sums(b):
                dve.wait_ge(exp_done.sem, exp_done.value(b, QC))
                V.reduce_sum(row_sum[:], chunk_sum[:], AX.X).then_inc(sum_steps.sem, 1)
                dve.wait_ge(sum_steps.sem, sum_steps.value(b, 1))
                dve.wait_ge(c2q_done.sem, c2q_done.value(b, 0))
                V.reciprocal(row_inv[:], row_sum[:]).then_inc(sum_steps.sem, 1)

            def token_part(b):
                dve.wait_ge(q2c_summed.sem, q2c_summed.value(b, 1))
                V.reciprocal(tok_inv[:], tok_sum_ps).then_inc(q2c_steps.sem, 1)
                dve.wait_ge(q2c_steps.sem, q2c_steps.value(b, 1))
                V.tensor_scalar(q2c[:], q2c_ps, tok_inv[:], None, ALU.mult).then_inc(q2c_steps.sem, 1)
                dve.wait_ge(q2c_steps.sem, q2c_steps.value(b, 2))
                for k in range(KD):
                    V.tensor_scalar(cq2c[:, k * P:(k + 1) * P], cT[:, k * P:(k + 1) * P], q2c[:, k:k + 1],
                                    None, ALU.mult).then_inc(q2c_steps.sem, 1)

            grant(dve, sum_steps, c2qT_lo_done, lo_done, probsT_lo_done, cc2q_done, x1_done)
            norm_moments(0)
            dve.wait_ge(const_landed, 16 * 8)
            V.reduce_sum(bias_sum[:], biases[:], AX.X).then_inc(bias_done, 1)
            dve.wait_ge(bias_done, 1)
            norm(0)
            cols_low(0, 0)
            cols_low(0, 1)
            normed_weighted(0)
            normed_weighted_low(0)

            def weight_low_part(w):
                dve.wait_ge(weight_hi, w + 1)
                V.tensor_tensor(wl_lo[:, w * NJ:(w + 1) * NJ, :].rearrange("p j d -> p (j d)"), raw[:, w % RAW, :],
                                wl_hi[:, w * NJ:(w + 1) * NJ, :].rearrange("p j d -> p (j d)").bitcast(F32),
                                ALU.subtract).then_inc(weight_lo, 1)

            for u in range(2, NU):
                cols_low(0, u)
            for q in range(QC):
                chunk_maximum(0, q)
                if q < RAW // 2:
                    weight_low_part(2 * q)
                    weight_low_part(2 * q + 1)
            row_maximum(0)
            for w in range(RAW, KZ // NJ):
                weight_low_part(w)
            for h in range(NU - 2):
                rows_low(0, h)

            def result(b):
                dve.wait_ge(z_done.sem, z_done.value(b, 1))
                dve.wait_ge(x_bias_done.sem, x_bias_done.value(b, 1))
                dve.wait_ge(x1_stored.sem, x1_stored.value(b, 0))
                V.tensor_tensor(x1[:], projected[:], x_bias[:], ALU.add).then_inc(x1_done.sem, 1)

            def step(b, more):
                probsT_low(b, 0)
                probsT_low(b, 1)
                rows_low(b, NU - 2)
                rows_low(b, NU - 1)
                sums(b)
                if more:
                    norm_moments(b + 1)
                token_part(b)
                if more:
                    norm(b + 1)
                probsT_low(b, 2)
                if more:
                    cols_low(b + 1, 0)
                    cols_low(b + 1, 1)
                    cols_low(b + 1, 2)
                    normed_weighted(b + 1)
                    cols_low(b + 1, 3)
                    normed_weighted_low(b + 1)
                probsT_low(b, 3)
                if more:
                    for u in range(4, NU):
                        cols_low(b + 1, u)
                    chunk_maximum(b + 1, 0)
                    rows_low(b + 1, 0)
                    rows_low(b + 1, 1)
                    chunk_maximum(b + 1, 1)
                dve.wait_ge(held.sem, held.value(b, 1))
                dve.wait_ge(c2qT_hi_done.sem, c2qT_hi_done.value(b, 1))
                V.tensor_tensor(cc2q[:], turn[1][:], cT_held[:], ALU.mult).then_inc(cc2q_done.sem, 1)
                low(c2qT_lo[:], turn[1][:], c2qT_hi[:]).then_inc(c2qT_lo_done.sem, 1)
                if more:
                    rows_low(b + 1, 2)
                dve.wait_ge(cc2q_hi_done.sem, cc2q_hi_done.value(b, 1))
                low(cc2q_lo[:], cc2q[:], cc2q_hi[:]).then_inc(cc2q_lo_done.sem, 1)
                if more:
                    rows_low(b + 1, 3)
                    chunk_maximum(b + 1, 2)
                    rows_low(b + 1, 4)
                    chunk_maximum(b + 1, 3)
                    row_maximum(b + 1)
                    rows_low(b + 1, NU - 3)
                result(b)

            with dve.Fori(0, B - 1) as i:
                step(i, True)
            step(B - 1, False)

        @block.tensor
        def _(pe):
            def turn_normed(b):
                pe.wait_ge(norm_steps.sem, norm_steps.value(b, 3))
                pe.wait_ge(probsT_lo_done.sem, probsT_lo_done.value(b, -2))
                for k in range(KD):
                    last = nc.tensor.transpose(turn[1][:, k * P:(k + 1) * P], c[:, k * P:(k + 1) * P], ident[:])
                last.then_inc(c_turned.sem, 1)

            def score(b, q):
                for k in range(KD):
                    u = 2 * q + k // KH
                    if k % KH == 0:
                        pe.wait_ge(lo_done.sem, lo_done.value(b, u + 1))
                    ks = slice(k * P, (k + 1) * P)
                    last = product(nc, scores[:, q, :], (cw_hi[:, ks], cw_lo[:, ks]),
                                   (ctx_hi[:, u, k % KH, :], ctx_lo[:, u, k % KH, :]), k == 0, k == KD - 1)
                last.then_inc(scored.sem, 1)

            def turn_probs(b, g):
                pe.wait_ge(exp_done.sem, exp_done.value(b, g + 1))
                if g == 0:
                    pe.wait_ge(probsT_lo_done.sem, probsT_lo_done.value(b, 0))
                elif g == 1:
                    pe.wait_ge(cc2q_done.sem, cc2q_done.value(b, 0))
                    pe.wait_ge(c2qT_lo_done.sem, c2qT_lo_done.value(b, 0))
                    pe.wait_ge(cT_done.sem, cT_done.value(b, 1))
                else:
                    pe.wait_ge(probsT_lo_done.sem, probsT_lo_done.value(b, g - 1 if g == 2 else 3))
                to = turn[g % 2] if g < 3 else turn[0]
                for t in range(4):
                    h, j = 2 * g + t // NJ, t % NJ
                    last = nc.tensor.transpose(to[:, t * P:(t + 1) * P],
                                               probs[:, h * NJ * P + j:(h + 1) * NJ * P:NJ], ident[:])
                last.then_inc(probs_turned.sem, 1)

            def gather(b, g):
                pe.wait_ge(probsT_lo_done.sem, probsT_lo_done.value(b, g + 1))
                pe.wait_ge(lo_done.sem, lo_done.value(b, NU + 2 * g + 2))
                if g == 0:
                    pe.wait_ge(c2q_done.sem, c2q_done.value(b, 0))
                for t in range(4):
                    h, j = 2 * g + t // NJ, t % NJ
                    last = product(nc, summed[:], (probsT_hi[:, g % 2, t * P:(t + 1) * P], probsT_lo[:, g % 2, t * P:(t + 1) * P]),
                                   (ctx_hi[:, h, j, :], ctx_lo[:, h, j, :]), g == 0 and t == 0, g == QC - 1 and t == 3)
                last.then_inc(gathered.sem, 1)

            def project(part, hi, lo, first, last):
                for k in range(KD):
                    ks = slice(k * P, (k + 1) * P)
                    z = part * KD + k
                    made = product(nc, projected[:], (hi[:, ks], lo[:, ks]), (wl_hi[:, z, :], wl_lo[:, z, :]),
                                   first and k == 0, last and k == KD - 1)
                return made

            def sum_tokens(b):
                pe.wait_ge(tok_exp_done.sem, tok_exp_done.value(b, 1))
                pe.wait_ge(exp_done.sem, exp_done.value(b, QC))
                nc.tensor.matmul(tok_sum_ps, ones[:], tok_exp[:], start=True, stop=True)
                for k in range(KD):
                    last = nc.tensor.matmul(q2c_ps[:, k:k + 1], c[:, k * P:(k + 1) * P], tok_exp[:], start=True, stop=True)
                last.then_inc(q2c_summed.sem, 1)

            grant(pe, probs_turned, q2c_summed, scored, gathered, c_projected, z_done)
            pe.wait_ge(const_landed, 16 * 8)
            pe.wait_ge(ones_done, 1)
            turn_normed(0)
            pe.wait_ge(cw_lo_done.sem, cw_lo_done.value(0, 1))
            for q in range(QC):
                score(0, q)

            def step(b, more):
                turn_probs(b, 0)
                turn_probs(b, 1)
                pe.wait_ge(x1_done.sem, x1_done.value(b, 0))
                pe.wait_ge(cT_lo_done.sem, cT_lo_done.value(b, 1))
                pe.wait_ge(weight_lo, KZ // NJ)
                project(0, cT_hi, cT_lo, True, False).then_inc(c_projected.sem, 1)
                gather(b, 0)
                sum_tokens(b)
                turn_probs(b, 2)
                gather(b, 1)
                if more:
                    turn_normed(b + 1)
                gather(b, 2)
                turn_probs(b, 3)
                pe.wait_ge(cq2c_lo_done.sem, cq2c_lo_done.value(b, 1))
                project(3, cq2c_hi, cq2c_lo, False, False).then_inc(c_projected.sem, 1)
                gather(b, 3)
                if more:
                    pe.wait_ge(cw_lo_done.sem, cw_lo_done.value(b + 1, 1))
                    pe.wait_ge(q2c_steps.sem, q2c_steps.value(b, 2))
                    score(b + 1, 0)
                    score(b + 1, 1)
                pe.wait_ge(c2q_done.sem, c2q_done.value(b, 1))
                if more:
                    pe.wait_ge(cT_done.sem, cT_done.value(b + 1, 1))
                for k in range(KD):
                    last = nc.tensor.transpose(turn[1][:, k * P:(k + 1) * P], c2q[:, k * P:(k + 1) * P], ident[:])
                last.then_inc(c2q_turned.sem, 1)
                if more:
                    score(b + 1, 2)
                    score(b + 1, 3)
                pe.wait_ge(c2qT_lo_done.sem, c2qT_lo_done.value(b, 1))
                project(1, c2qT_hi, c2qT_lo, False, False)
                pe.wait_ge(cc2q_lo_done.sem, cc2q_lo_done.value(b, 1))
                project(2, cc2q_hi, cc2q_lo, False, True).then_inc(z_done.sem, 1)

            with pe.Fori(0, B - 1) as i:
                step(i, True)
            step(B - 1, False)


H = 16
HD = D // H
E = 32
TOPK = 4
CAP = 1024
G = 4
NG = B // G
PAIRS = 2 * P
NBLOCKS = (B * P * TOPK + E * (PAIRS - 1)) // PAIRS
RING = 4
TURNS = -(-NBLOCKS // RING)
ALWAYS = TOPK * CAP // PAIRS
NONE = E * CAP
ROWS = NONE + PAIRS


def self_attention_and_routing(nc, x1_in, W_qkT, W_vT, W_g, W_s13, W_s2, ident_in, before_in, normed_out, acc_out,
                               token_of_slot, y_rows, pair_rank, pair_expert, pair_weight, expert_count):
    CQ = 2 * D // P
    CF = 512 // P
    FILL = 8
    FILLS = (TURNS * RING - ALWAYS) // FILL
    V_ORDER = [(n + G - 1) % G for n in range(G)]
    VW = HD + 1
    with ExitStack() as stack:
        m = Memory(nc, stack, "sa")
        wqk = [m.sb("wqk_hi", [P, KD, 2 * D], F32R), m.sb("wqk_lo", [P, KD, 2 * D], F32R)]
        wv = [m.sb("wv_hi", [P, KD, D], F32R), m.sb("wv_lo", [P, KD, D], F32R)]
        ws13 = [m.sb("ws13_hi", [P, KD, 2 * D], F32R), m.sb("ws13_lo", [P, KD, 2 * D], F32R)]
        ws2 = [m.sb("ws2_hi", [P, CF, D], F32R), m.sb("ws2_lo", [P, CF, D], F32R)]
        wg = [m.sb("wg_hi", [P, KD, E], F32R), m.sb("wg_lo", [P, KD, E], F32R)]
        wg_raw = m.sb("wg_raw", [P, KD, E])
        ident = m.sb("ident", [P, P])
        before = m.sb("before", [P, P])
        ones = m.sb("ones", [P, P])
        eps_pow = m.sb("eps_pow", [P, 2])
        x = m.sb("x", [P, G, D])
        xn = m.sb("xn", [P, 4, D])
        xnT_hi = m.sb("xnT_hi", [P, KD, G * P], F32R)
        xnT_lo = m.sb("xnT_lo", [P, KD, G * P], F32R)
        stats = m.sb("stats", [P, 6])
        mean_var = m.sb("mean_var", [P, 2])
        var_eps = m.sb("var_eps", [P, 1])
        rstd = m.sb("rstd", [P, 1])
        qkT = m.sb("qkT", [P, CQ, G * P])
        v = m.sb("v", [P, G, H, VW])
        probs = m.sb("probs", [P, H, P])
        probsT = m.sb("probsT", [P, H, P])
        head_max = m.sb("head_max", [P, H])
        head_inv = m.sb("head_inv", [P, H])
        mixed = m.sb("mixed", [P, D])
        gate = m.sb("gate", [P, G * P])
        hT = m.sb("hT", [P, G * P])
        hT_hi = m.sb("hT_hi", [P, CF, G * P], F32R)
        hT_lo = m.sb("hT_lo", [P, CF, G * P], F32R)
        acc = m.sb("acc", [P, 2, D])
        logitsT = m.sb("logitsT", [E, G * P])
        logits = m.sb("logits", [P, G, E])
        top = m.sb("top", [P, G, 8])
        top_at = m.sb("top_at", [P, G, 8], U32)
        expert = m.sb("expert", [P, G, TOPK])
        shifted = m.sb("shifted", [P, G, E])
        top_shifted = m.sb("top_shifted", [P, G, TOPK])
        exp_sum = m.sb("exp_sum", [P, G])
        exp_inv = m.sb("exp_inv", [P, G])
        iota_e = m.sb("iota_e", [P, E])
        one_hot = m.sb("one_hot", [P, G, TOPK, E])
        taken = m.sb("taken", [P, G, E])
        counted = expert_count
        group_taken = m.sb("group_taken", [P, E])
        ranked = m.sb("ranked", [P, G, TOPK, E])
        rank = m.sb("rank", [P, G * TOPK])
        kept = m.sb("kept", [P, G * TOPK])
        base = m.sb("base", [P, G * TOPK])
        slot = m.sb("slot", [P, G * TOPK])
        scatter_to = m.sb("scatter_to", [P, G * TOPK], I32)
        tokens_f = m.sb("tokens_f", [P, G])
        tokens = m.sb("tokens", [P, G], I32)
        zeros = acc[:, 0, :]
        q_hi, q_lo = xnT_hi[:, :, (G - 1) * P:G * P], xnT_lo[:, :, (G - 1) * P:G * P]
        k_hi, k_lo = hT_hi, hT_lo

        S = m.ps("scores", [P, 4, BANK])
        turn = [m.ps("turn0", [P, BANK]), m.ps("turn1", [P, BANK])]
        work = [m.ps("work0", [P, BANK]), m.ps("work1", [P, BANK])]

        const_landed = m.sem("const_landed")
        setup = m.sem("setup")
        NW = 6
        w_landed = [m.sem("w_landed0"), m.sem("w_landed1")]
        w_hi = m.sem("w_hi")
        w_lo = m.sem("w_lo")
        x_landed = m.tally("x_landed", 16)
        x_moved = m.tally("x_moved", G, 1)
        norm_steps = m.tally("norm_steps", 3 * 2 * G)
        rstd_steps = m.tally("rstd_steps", 2 * 2 * G)
        turned = m.tally("turned", 2 * G, 1)
        xnT_hi_done = m.tally("xnT_hi_done", 2 * G)
        xnT_lo_done = m.tally("xnT_lo_done", 2 * G, 2 * G)
        normed_stored = [m.tally("normed_stored0", 16 * G // 2, 1), m.tally("normed_stored1", 16 * G // 2, 1)]
        qk_done = m.tally("qk_done", CQ)
        qk_read = m.tally("qk_read", CQ)
        v_done = m.tally("v_done", G)
        v_read = m.tally("v_read", G)
        scored = m.tally("scored", 4 * G, 1)
        k_zeroed = m.tally("k_zeroed", 2)
        qk_hi_done = m.tally("qk_hi_done", 5 * G)
        k_lo_done = m.tally("k_lo_done", 2 * G)
        qk_lo_done = m.tally("qk_lo_done", 3 * G)
        max_done = m.tally("max_done", 4 * G)
        shift_done = m.tally("shift_done", 4 * G)
        exp_done = m.tally("exp_done", 4 * G)
        probs_turned = m.tally("probs_turned", 4 * G, 4)
        probsT_read = m.tally("probsT_read", 4 * G, 4 * G)
        mixed_done = m.tally("mixed_done", G, 1)
        mix_steps = m.tally("mix_steps", 6 * G, 1)
        logitsT_done = m.tally("logitsT_done", 1)
        logitsT_read = m.tally("logitsT_read", 1)
        logits_done = m.tally("logits_done", 1, 1)
        logits_steps = m.tally("logits_steps", 1)
        up_done = m.tally("up_done", CF, 1)
        gate_done = m.tally("gate_done", CF)
        h_steps = m.tally("h_steps", 2 * CF, 2 * CF)
        hT_hi_done = m.tally("hT_hi_done", CF, 1)
        hT_lo_done = m.tally("hT_lo_done", CF, 1)
        down_done = m.tally("down_done", G, 1)
        acc_done = m.tally("acc_done", G, 1)
        acc_stored = [m.tally("acc_stored0", 16 * G // 2, 1), m.tally("acc_stored1", 16 * G // 2, 1)]
        R_SHIFTED, R_TAKEN, R_RANKED, ROUTE_STEPS = 11, 13, 16, 30
        route_steps = m.tally("route_steps", ROUTE_STEPS, 1)
        route_exp_done = m.tally("route_exp_done", 2)
        ranks_done = m.tally("ranks_done", 1)
        scattered = m.tally("scattered", 16 * G * TOPK)
        scatter_over = m.tally("scatter_over", 1, 1)
        zeroed = m.sem("zeroed")
        rows_zeroed = m.sem("rows_zeroed")
        block = stack.enter_context(nc.Block())

        stage = [probs[:].rearrange("p h n -> p (h n)"), probsT[:].rearrange("p h n -> p (h n)")]
        half = KD // 2
        x_next = stage[0].rearrange("p (j d) -> p j d", j=G)

        def k_block(t, r):
            return t[r * HD:(r + 1) * HD, :, r * P:(r + 1) * P]

        def k_raw(j, r):
            return qkT[r * HD:(r + 1) * HD, CQ // 2:CQ, j * P:(j + 1) * P]

        def flat(ap):
            return ap.rearrange("p k n -> p (k n)")

        pieces = [(flat(W_qkT[:, :half, :]), wqk, slice(0, half)), (flat(W_qkT[:, half:, :]), wqk, slice(half, KD)),
                  (flat(W_vT), wv, slice(0, KD)),
                  (flat(W_s13[:, :half, :]), ws13, slice(0, half)), (flat(W_s13[:, half:, :]), ws13, slice(half, KD)),
                  (flat(W_s2), ws2, slice(0, CF))]

        @block.sync
        def _(sp):
            grant(sp, normed_stored[0], normed_stored[1], acc_stored[0], acc_stored[1])
            sp.dma_start(x[:], x1_in[0:G].rearrange("b p d -> p b d")).then_inc(x_landed.sem, 16)
            for dst, src in ((ident[:], ident_in), (before[:], before_in), (wg_raw[:], W_g)):
                sp.dma_start(dst, src).then_inc(const_landed, 16)
            sp.wait_ge(setup, 1)
            sp.dma_start(token_of_slot.rearrange("(p n) one -> p (n one)", p=P), zeros[:, 0:ROWS // P].bitcast(I32)).then_inc(zeroed, 16)
            for n, (src, _, _) in enumerate(pieces):
                if n >= 2:
                    sp.wait_ge(w_lo, n)
                sp.dma_start(stage[n % 2], src).then_inc(w_landed[n % 2], 16)

            for n in range(FILLS):
                rows = slice((ALWAYS + n * FILL) * PAIRS, (ALWAYS + (n + 1) * FILL) * PAIRS)
                sp.dma_start(y_rows[rows].rearrange("(r p) d -> p r d", p=P),
                             zeros.unsqueeze(1).to_broadcast([P, FILL * PAIRS // P, D])).then_inc(rows_zeroed, 16)

            def step(g, more):
                for j in range(G):
                    if more and j == G - 1:
                        sp.wait_ge(probs_turned.sem, probs_turned.value(g, 4 * G))
                        sp.dma_start(x_next, x1_in[bass.ds(g * G + G, G)].rearrange("b p d -> p b d")).then_inc(x_landed.sem, 16)
                    sp.wait_ge(norm_steps.sem, norm_steps.value(g, 3 * (G + j) + 3))
                    sp.dma_start(normed_out[g * G + j], xn[:, 2 + j % 2, :]).then_inc(normed_stored[j % 2].sem, 16)
                for j in range(G):
                    sp.wait_ge(acc_done.sem, acc_done.value(g, j + 1))
                    sp.dma_start(acc_out[g * G + j], acc[:, j % 2, :]).then_inc(acc_stored[j % 2].sem, 16)

            with sp.Fori(0, NG - 1) as i:
                step(i, True)
            step(NG - 1, False)
            for j in range(2):
                sp.wait_ge(normed_stored[j].sem, normed_stored[j].value(NG - 1, 16 * G // 2))
                sp.wait_ge(acc_stored[j].sem, acc_stored[j].value(NG - 1, 16 * G // 2))

        @block.gpsimd
        def _(pool):
            nc.gpsimd.memset(eps_pow[:, 0:1], EPS)
            nc.gpsimd.memset(eps_pow[:, 1:2], -0.5)
            nc.gpsimd.memset(ones[:], 1.0)
            nc.gpsimd.memset(zeros, 0.0)
            nc.gpsimd.memset(counted[:], 0.0)
            for j in range(G):
                nc.gpsimd.memset(v[:, j, :, HD:VW], 1.0)
            nc.gpsimd.iota(iota_e[:], pattern=[[1, E]], base=0, channel_multiplier=0, allow_small_or_imprecise_dtypes=True)
            nc.gpsimd.iota(tokens_f[:], pattern=[[P, G]], base=0, channel_multiplier=1, allow_small_or_imprecise_dtypes=True).then_inc(setup, 1)
            grant(pool, scatter_over)
            pool.wait_ge(setup, 1)

            def inverse_spread(g, n):
                pool.wait_ge(norm_steps.sem, norm_steps.value(g, 3 * n + 2))
                pool.nop(nofuse=True)
                nc.gpsimd.tensor_tensor(var_eps[:], mean_var[:, 1:2], eps_pow[:, 0:1], ALU.add).then_inc(rstd_steps.sem, 1)
                pool.wait_ge(rstd_steps.sem, rstd_steps.value(g, 2 * n + 1))
                pool.nop(nofuse=True)
                nc.gpsimd.tensor_tensor(rstd[:], var_eps[:], eps_pow[:, 1:2], ALU.pow).then_inc(rstd_steps.sem, 1)

            def zero_k(g):
                pool.wait_ge(down_done.sem, down_done.value(g, 0))
                pool.nop(nofuse=True)
                for t in (k_hi, k_lo):
                    nc.gpsimd.memset(t[:].bitcast(F32), 0.0).then_inc(k_zeroed.sem, 1)

            def k_low(g, j):
                for r in range(2):
                    pool.wait_ge(qk_hi_done.sem, qk_hi_done.value(g, 5 * j + r + 1))
                    pool.nop(nofuse=True)
                    nc.gpsimd.tensor_tensor(k_block(k_lo, r), k_raw(j, r), k_block(k_hi, r).bitcast(F32), ALU.subtract).then_inc(k_lo_done.sem, 1)
                    pool.wait_ge(k_lo_done.sem, k_lo_done.value(g, 2 * j + r + 1))
                    pool.nop(nofuse=True)

            zero_k(0)
            for n in range(G):
                inverse_spread(0, n)

            def step(g, more):
                k_low(g, 0)
                k_low(g, 1)
                for j in range(G):
                    if j + 2 < G:
                        k_low(g, j + 2)
                    inverse_spread(g, G + j)
                if more:
                    for n in range(G):
                        inverse_spread(g + 1, n)
                    zero_k(g + 1)
                pool.wait_ge(zeroed, 16)
                pool.wait_ge(route_steps.sem, route_steps.value(g, ROUTE_STEPS))
                pool.nop(nofuse=True)
                for j in range(G):
                    for k in range(TOPK):
                        n = j * TOPK + k
                        pool.indirect_dma_start(token_of_slot, bass.IndirectOffsetOnAxis(ap=scatter_to[:, n:n + 1], axis=0),
                                                tokens[:, j:j + 1], None, bounds_check=NONE - 1, oob_is_err=False)\
                            .then_inc(scattered.sem, 16)
                pool.wait_ge(scattered.sem, scattered.value(g, 16 * G * TOPK))
                pool.nop(nofuse=True)
                pool.sem_inc(scatter_over.sem, 1)

            with pool.Fori(0, NG - 1) as i:
                step(i, True)
            step(NG - 1, False)

        @block.scalar
        def _(act):
            def copy(out, src):
                return nc.scalar.activation(out, src, ACT.Copy)

            grant(act, probsT_read, hT_hi_done, x_moved)

            def normed_high(g, n):
                j = n % G
                act.wait_ge(turned.sem, turned.value(g, n + 1))
                if n < G:
                    act.wait_ge(up_done.sem, up_done.value(g, 0))
                else:
                    act.wait_ge(v_done.sem, v_done.value(g, G))
                copy(xnT_hi[:, :, j * P:(j + 1) * P], turn[n % 2][:].rearrange("p (k t) -> p k t", k=KD)).then_inc(xnT_hi_done.sem, 1)

            def project_out(g, c):
                act.wait_ge(qk_done.sem, qk_done.value(g, c + 1))
                if c == 0:
                    act.wait_ge(scored.sem, scored.value(g, 0))
                copy(qkT[:, c, :], S[:, c % 4, :]).then_inc(qk_read.sem, 1)

            def score_operands_high(g, j):
                act.wait_ge(scored.sem, scored.value(g, 4 * j))
                act.wait_ge(qk_read.sem, qk_read.value(g, CQ))
                if j == 0:
                    act.wait_ge(k_zeroed.sem, k_zeroed.value(g, 2))
                for r in range(4):
                    copy(k_block(k_hi, r), k_raw(j, r)).then_inc(qk_hi_done.sem, 1)
                if j == 0:
                    act.wait_ge(v_done.sem, v_done.value(g, 1))
                copy(q_hi, qkT[:, 0:CQ // 2, j * P:(j + 1) * P]).then_inc(qk_hi_done.sem, 1)

            def attend(g, j):
                for c in range(4):
                    act.wait_ge(shift_done.sem, shift_done.value(g, 4 * j + c + 1))
                    four = probs[:, 4 * c:4 * c + 4, :]
                    nc.scalar.activation(four, four, ACT.Exp, scale=float(D) ** -0.5).then_inc(exp_done.sem, 1)

            def probsT_out(g, j):
                for q in range(4):
                    act.wait_ge(probs_turned.sem, probs_turned.value(g, 4 * j + q + 1))
                    act.wait_ge(mixed_done.sem, mixed_done.value(g, j))
                    copy(probsT[:, q * 4:q * 4 + 4, :], turn[q % 2][:].rearrange("p (h t) -> p h t", h=4)).then_inc(probsT_read.sem, 1)

            act.wait_ge(const_landed, 16 * 3)
            copy(flat(wg[0][:]), flat(wg_raw[:])).then_inc(w_hi, 1)

            def weight_high(n):
                _, (hi, _), ks = pieces[n]
                act.wait_ge(w_landed[n % 2], 16 * (n // 2 + 1))
                copy(flat(hi[:, ks, :]), stage[n % 2]).then_inc(w_hi, 1)

            normed_high(0, 0)
            weight_high(0)
            normed_high(0, 1)
            weight_high(1)
            normed_high(0, 2)
            normed_high(0, 3)
            for n in range(2, NW):
                weight_high(n)

            def move_x(g, j):
                act.wait_ge(x_landed.sem, x_landed.value(g + 1, 16))
                act.wait_ge(acc_done.sem, acc_done.value(g, j + 1))
                copy(x[:, j, :], x_next[:, j, :]).then_inc(x_moved.sem, 1)

            def logits_out(g):
                act.wait_ge(logitsT_done.sem, logitsT_done.value(g, 1))
                act.wait_ge(logits_done.sem, logits_done.value(g, 0))
                copy(logitsT[:], work[1][0:E, :]).then_inc(logitsT_read.sem, 1)

            def shared_gate(g, c):
                act.wait_ge(up_done.sem, up_done.value(g, c + 1))
                act.wait_ge(h_steps.sem, h_steps.value(g, 2 * c - 1))
                nc.scalar.activation(gate[:], S[:, 2 * (c % 2), :], ACT.Tanh, scale=0.5).then_inc(gate_done.sem, 1)
                act.wait_ge(h_steps.sem, h_steps.value(g, 2 * c + 2))
                act.wait_ge(down_done.sem, down_done.value(g, 0))
                copy(hT_hi[:, c, :], hT[:]).then_inc(hT_hi_done.sem, 1)

            def step(g, more):
                for c in range(CQ):
                    project_out(g, c)
                score_operands_high(g, 0)
                score_operands_high(g, 1)
                attend(g, 0)
                act.wait_ge(w_lo, NW + 1)
                for j in range(G):
                    probsT_out(g, j)
                    if j + 2 < G:
                        score_operands_high(g, j + 2)
                    if j + 1 < G:
                        attend(g, j + 1)
                    if j:
                        normed_high(g, G + j - 1)
                normed_high(g, 2 * G - 1)
                logits_out(g)
                shared_gate(g, 0)
                act.wait_ge(route_steps.sem, route_steps.value(g, R_SHIFTED))
                nc.scalar.activation(shifted[:], shifted[:], ACT.Exp).then_inc(route_exp_done.sem, 1)
                nc.scalar.activation(top_shifted[:], top_shifted[:], ACT.Exp).then_inc(route_exp_done.sem, 1)
                for c in range(1, CF):
                    shared_gate(g, c)
                if more:
                    for n in range(G - 1):
                        normed_high(g + 1, n)
                    move_x(g, 0)
                    normed_high(g + 1, G - 1)
                    for j in range(1, G):
                        move_x(g, j)

            with act.Fori(0, NG - 1) as i:
                step(i, True)
            step(NG - 1, False)

        @block.vector
        def _(dve):
            V = nc.vector
            grant(dve, xnT_lo_done, h_steps, route_steps, hT_lo_done, acc_done, mix_steps)

            def low(out, raw, hi):
                return V.tensor_tensor(out, raw, hi.bitcast(F32), ALU.subtract)

            def norm(g, n, x=x):
                j = n % G
                if n == 0:
                    dve.wait_ge(x_landed.sem, x_landed.value(g, 16))
                if n >= G:
                    dve.wait_ge(mix_steps.sem, mix_steps.value(g, 6 * j + 6))
                V.bn_stats(stats[:], x[:, j, :]).then_inc(norm_steps.sem, 1)
                dve.wait_ge(norm_steps.sem, norm_steps.value(g, 3 * n + 1))
                dve.nop(nofuse=True)
                V.bn_aggr(mean_var[:], stats[:]).then_inc(norm_steps.sem, 1)
                dve.wait_ge(rstd_steps.sem, rstd_steps.value(g, 2 * n + 2))
                dve.wait_ge(turned.sem, turned.value(g, n - 1 if j >= 2 else 0))
                if n >= G:
                    dve.wait_ge(normed_stored[j % 2].sem, normed_stored[j % 2].value(g, 16 * (j // 2)))
                V.tensor_scalar(xn[:, 2 * (n // G) + j % 2, :], x[:, j, :], mean_var[:, 0:1], rstd[:], ALU.subtract, ALU.mult)\
                    .then_inc(norm_steps.sem, 1)

            def normed_low(g, n):
                j = n % G
                dve.wait_ge(xnT_hi_done.sem, xnT_hi_done.value(g, n + 1))
                low(xnT_lo[:, :, j * P:(j + 1) * P], turn[n % 2][:].rearrange("p (k t) -> p k t", k=KD),
                    xnT_hi[:, :, j * P:(j + 1) * P]).then_inc(xnT_lo_done.sem, 1)

            def maximum_and_shift(g, j):
                def maximum(c):
                    dve.wait_ge(scored.sem, scored.value(g, 4 * j + c + 1))
                    V.reduce_max(head_max[:, 4 * c:4 * c + 4], S[:, c, :].rearrange("p (r n) -> p r n", n=P), AX.X).then_inc(max_done.sem, 1)

                def shift(c):
                    heads = slice(4 * c, 4 * c + 4)
                    dve.wait_ge(max_done.sem, max_done.value(g, 4 * j + c + 1))
                    if j == 0 and c == 0:
                        dve.wait_ge(x_moved.sem, x_moved.value(g, 0))
                    dve.wait_ge(probs_turned.sem, probs_turned.value(g, 4 * (j - 1) + c + 1))
                    V.tensor_tensor(probs[:, heads, :], S[:, c, :].rearrange("p (r n) -> p r n", n=P),
                                    head_max[:, heads].unsqueeze(2).to_broadcast([P, 4, P]), ALU.subtract).then_inc(shift_done.sem, 1)

                maximum(0)
                for c in range(4):
                    if c < 3:
                        maximum(c + 1)
                    shift(c)

            def score_operands_low(g, j):
                for r in range(2, 4):
                    dve.wait_ge(qk_hi_done.sem, qk_hi_done.value(g, 5 * j + r + 1))
                    low(k_block(k_lo, r), k_raw(j, r), k_block(k_hi, r)).then_inc(qk_lo_done.sem, 1)
                dve.wait_ge(qk_hi_done.sem, qk_hi_done.value(g, 5 * j + 5))
                low(q_lo, qkT[:, 0:CQ // 2, j * P:(j + 1) * P], q_hi).then_inc(qk_lo_done.sem, 1)

            def mix_out(g, j):
                dve.wait_ge(mixed_done.sem, mixed_done.value(g, j + 1))
                k0 = 6 * j
                for w in range(2):
                    hs = slice(w * 8, w * 8 + 8)
                    o = work[w][:, 0:8 * VW].rearrange("p (h n) -> p h n", n=VW)
                    mw = mixed[:, w * 256:(w + 1) * 256].rearrange("p (h n) -> p h n", n=HD)
                    V.reciprocal(head_inv[:, hs], o[:, :, HD:VW].rearrange("p h n -> p (h n)")).then_inc(mix_steps.sem, 1)
                    dve.wait_ge(mix_steps.sem, mix_steps.value(g, k0 + 3 * w + 1))
                    V.tensor_tensor(mw, o[:, :, 0:HD], head_inv[:, hs].unsqueeze(2).to_broadcast([P, 8, HD]), ALU.mult).then_inc(mix_steps.sem, 1)
                    dve.wait_ge(mix_steps.sem, mix_steps.value(g, k0 + 3 * w + 2))
                    xw = x[:, j, w * 256:(w + 1) * 256]
                    V.tensor_tensor(xw, xw, mixed[:, w * 256:(w + 1) * 256], ALU.add).then_inc(mix_steps.sem, 1)

            dve.wait_ge(const_landed, 16 * 3)
            dve.wait_ge(setup, 1)

            def weight_low(n):
                _, (hi, lo), ks = pieces[n]
                dve.wait_ge(w_hi, n + 2)
                low(flat(lo[:, ks, :]), stage[n % 2], flat(hi[:, ks, :])).then_inc(w_lo, 1)

            norm(0, 0)
            dve.wait_ge(w_hi, 1)
            low(flat(wg[1][:]), flat(wg_raw[:]), flat(wg[0][:])).then_inc(w_lo, 1)
            norm(0, 1)
            normed_low(0, 0)
            weight_low(0)
            norm(0, 2)
            normed_low(0, 1)
            weight_low(1)
            norm(0, 3)
            normed_low(0, 2)
            normed_low(0, 3)
            for n in range(2, NW):
                weight_low(n)

            def choose(g):
                dve.wait_ge(logits_done.sem, logits_done.value(g, 1))
                dve.wait_ge(route_steps.sem, route_steps.value(g, 0))
                V.tensor_copy(logits[:], work[0][:, 0:G * E].rearrange("p (j e) -> p j e", e=E)).then_inc(logits_steps.sem, 1)
                dve.wait_ge(logits_steps.sem, logits_steps.value(g, 1))
                dve.nop(nofuse=True)
                for j in range(G):
                    V.max(top[:, j, :], logits[:, j, :]).then_inc(route_steps.sem, 1)
                dve.wait_ge(route_steps.sem, route_steps.value(g, 4))
                dve.nop(nofuse=True)
                for j in range(G):
                    V.max_index(top_at[:, j, :], top[:, j, :], logits[:, j, :]).then_inc(route_steps.sem, 1)
                dve.wait_ge(route_steps.sem, route_steps.value(g, 8))
                V.tensor_copy(expert[:], top_at[:, :, 0:TOPK]).then_inc(route_steps.sem, 1)
                V.tensor_tensor(shifted[:], logits[:], top[:, :, 0:1].to_broadcast([P, G, E]), ALU.subtract).then_inc(route_steps.sem, 1)
                V.tensor_tensor(top_shifted[:], top[:, :, 0:TOPK], top[:, :, 0:1].to_broadcast([P, G, TOPK]), ALU.subtract).then_inc(route_steps.sem, 1)
                dve.wait_ge(route_steps.sem, route_steps.value(g, 11))
                V.tensor_tensor(one_hot[:], iota_e[:].unsqueeze(1).unsqueeze(1).to_broadcast([P, G, TOPK, E]),
                                     expert[:].unsqueeze(3).to_broadcast([P, G, TOPK, E]), ALU.is_equal).then_inc(route_steps.sem, 1)
                dve.wait_ge(route_steps.sem, route_steps.value(g, 12))
                V.tensor_reduce(taken[:], one_hot[:].rearrange("p j k e -> p j e k"), AX.X, ALU.add).then_inc(route_steps.sem, 1)

            def place(g):
                dve.wait_ge(route_exp_done.sem, route_exp_done.value(g, 2))
                V.reduce_sum(exp_sum[:], shifted[:], AX.X).then_inc(route_steps.sem, 1)
                dve.wait_ge(route_steps.sem, route_steps.value(g, 14))
                V.reciprocal(exp_inv[:], exp_sum[:]).then_inc(route_steps.sem, 1)
                dve.wait_ge(ranks_done.sem, ranks_done.value(g, 1))
                V.tensor_tensor(ranked[:], one_hot[:], work[1][:, 0:G * E].rearrange("p (j e) -> p j e", e=E).unsqueeze(2)
                                     .to_broadcast([P, G, TOPK, E]), ALU.mult).then_inc(route_steps.sem, 1)
                V.tensor_reduce(group_taken[:], taken[:].rearrange("p j e -> p e j"), AX.X, ALU.add).then_inc(route_steps.sem, 1)
                dve.wait_ge(route_steps.sem, route_steps.value(g, 17))
                V.tensor_tensor(counted[:], counted[:], group_taken[:], ALU.add).then_inc(route_steps.sem, 1)
                V.reduce_sum(rank[:], ranked[:].rearrange("p j k e -> p (j k) e"), AX.X).then_inc(route_steps.sem, 1)
                dve.wait_ge(route_steps.sem, route_steps.value(g, 19))
                V.tensor_single_scalar(kept[:], rank[:], float(CAP), ALU.is_lt).then_inc(route_steps.sem, 1)
                V.tensor_single_scalar(base[:], expert[:].rearrange("p j k -> p (j k)"), float(CAP), ALU.mult).then_inc(route_steps.sem, 1)
                V.tensor_tensor(top_shifted[:], top_shifted[:], exp_inv[:].unsqueeze(2).to_broadcast([P, G, TOPK]), ALU.mult).then_inc(route_steps.sem, 1)
                dve.wait_ge(route_steps.sem, route_steps.value(g, 22))
                V.tensor_tensor(pair_weight[:, bass.ds(g * (G * TOPK), G * TOPK)], top_shifted[:].rearrange("p j k -> p (j k)"),
                                     kept[:], ALU.mult).then_inc(route_steps.sem, 1)
                V.tensor_single_scalar(pair_rank[:, bass.ds(g * (G * TOPK), G * TOPK)], rank[:], float(CAP - 1), ALU.min).then_inc(route_steps.sem, 1)
                V.tensor_copy(pair_expert[:, bass.ds(g * (G * TOPK), G * TOPK)], expert[:].rearrange("p j k -> p (j k)")).then_inc(route_steps.sem, 1)
                V.tensor_tensor(slot[:], rank[:], base[:], ALU.add).then_inc(route_steps.sem, 1)
                V.tensor_scalar(kept[:], kept[:], -float(NONE), float(NONE), ALU.mult, ALU.add).then_inc(route_steps.sem, 1)
                dve.wait_ge(route_steps.sem, route_steps.value(g, 27))
                dve.wait_ge(scatter_over.sem, scatter_over.value(g, 0))
                V.tensor_tensor(scatter_to[:], slot[:], kept[:], ALU.add).then_inc(route_steps.sem, 1)
                V.tensor_copy(tokens[:], tokens_f[:]).then_inc(route_steps.sem, 1)
                dve.wait_ge(route_steps.sem, route_steps.value(g, 29))
                V.tensor_single_scalar(tokens_f[:], tokens_f[:], float(G * P), ALU.add).then_inc(route_steps.sem, 1)

            def shared_inner(g, c):
                dve.wait_ge(gate_done.sem, gate_done.value(g, c + 1))
                dve.wait_ge(hT_hi_done.sem, hT_hi_done.value(g, c))
                dve.wait_ge(hT_lo_done.sem, hT_lo_done.value(g, c))
                V.scalar_tensor_tensor(hT[:], gate[:], 1.0, S[:, 2 * (c % 2), :], ALU.add, ALU.mult).then_inc(h_steps.sem, 1)
                dve.wait_ge(h_steps.sem, h_steps.value(g, 2 * c + 1))
                V.scalar_tensor_tensor(hT[:], hT[:], 0.5, S[:, 2 * (c % 2) + 1, :], ALU.mult, ALU.mult).then_inc(h_steps.sem, 1)
                dve.wait_ge(hT_hi_done.sem, hT_hi_done.value(g, c + 1))
                low(hT_lo[:, c, :], hT[:], hT_hi[:, c, :]).then_inc(hT_lo_done.sem, 1)

            def shared_out(g, j):
                dve.wait_ge(down_done.sem, down_done.value(g, j + 1))
                if j == 0:
                    dve.wait_ge(zeroed, 16)
                    dve.wait_ge(rows_zeroed, 16 * FILLS)
                dve.wait_ge(acc_stored[j % 2].sem, acc_stored[j % 2].value(g, 16 * (j // 2)))
                V.tensor_tensor(acc[:, j % 2, :], work[j % 2][:], x[:, j, :], ALU.add).then_inc(acc_done.sem, 1)

            def v_out(g, n):
                dve.wait_ge(v_done.sem, v_done.value(g, n + 1))
                dve.wait_ge(mixed_done.sem, mixed_done.value(g, 0))
                V.tensor_copy(v[:, V_ORDER[n], :, 0:HD], work[n % 2][:].rearrange("p (h n) -> p h n", n=HD)).then_inc(v_read.sem, 1)

            def step(g, more):
                score_operands_low(g, 0)
                v_out(g, 0)
                v_out(g, 1)
                maximum_and_shift(g, 0)
                score_operands_low(g, 1)
                v_out(g, 2)
                v_out(g, 3)
                maximum_and_shift(g, 1)
                score_operands_low(g, 2)
                mix_out(g, 0)
                norm(g, G)
                for j in range(1, G):
                    if j + 1 < G:
                        maximum_and_shift(g, j + 1)
                    if j + 2 < G:
                        score_operands_low(g, j + 2)
                    mix_out(g, j)
                    if j + 1 < G:
                        normed_low(g, G + j - 1)
                    norm(g, G + j)
                normed_low(g, 2 * G - 2)
                normed_low(g, 2 * G - 1)
                shared_inner(g, 0)
                choose(g)
                shared_inner(g, 1)
                if more:
                    norm(g + 1, 0, x_next)
                place(g)
                shared_inner(g, 2)
                if more:
                    norm(g + 1, 1, x_next)
                shared_inner(g, 3)
                if more:
                    normed_low(g + 1, 0)
                    norm(g + 1, 2, x_next)
                    normed_low(g + 1, 1)
                shared_out(g, 0)
                if more:
                    norm(g + 1, 3, x_next)
                    normed_low(g + 1, 2)
                shared_out(g, 1)
                if more:
                    normed_low(g + 1, 3)
                shared_out(g, 2)
                shared_out(g, 3)

            with dve.Fori(0, NG - 1) as i:
                step(i, True)
            step(NG - 1, False)

        @block.tensor
        def _(pe):
            grant(pe, up_done, scored, mixed_done, down_done, turned, probs_turned, logits_done)

            def turn_normed(g, n):
                j = n % G
                pe.wait_ge(norm_steps.sem, norm_steps.value(g, 3 * n + 3))
                pe.wait_ge(xnT_lo_done.sem, xnT_lo_done.value(g, n - 1))
                if n >= G:
                    pe.wait_ge(probsT_read.sem, probsT_read.value(g, 4 * (min(j + 1, G - 1) + 1)))
                for k in range(KD):
                    last = nc.tensor.transpose(turn[n % 2][:, k * P:(k + 1) * P], xn[:, 2 * (n // G) + j % 2, k * P:(k + 1) * P], ident[:])
                last.then_inc(turned.sem, 1)

            def tokens_of(j):
                return slice(j * P, (j + 1) * P)

            def project_qk(g, c):
                if c < 4:
                    pe.wait_ge(h_steps.sem, h_steps.value(g, 0))
                else:
                    pe.wait_ge(qk_read.sem, qk_read.value(g, c - 3))
                for k in range(KD):
                    cs = slice(c * P, (c + 1) * P)
                    last = product(nc, S[:, c % 4, :], (wqk[0][:, k, cs], wqk[1][:, k, cs]),
                                   (xnT_hi[:, k, :], xnT_lo[:, k, :]), k == 0, k == KD - 1)
                last.then_inc(qk_done.sem, 1)

            def from_tokens(out, j, a, w, ks, first=True):
                for k in range(ks):
                    last = product(nc, out, (a[0][:, k, tokens_of(j)], a[1][:, k, tokens_of(j)]), (w[0][:, k, :], w[1][:, k, :]), k == 0, k == ks - 1)
                return last

            def project_v(g, n):
                pe.wait_ge(acc_done.sem, acc_done.value(g, 0))
                if n >= 2:
                    pe.wait_ge(v_read.sem, v_read.value(g, n - 1))
                from_tokens(work[n % 2][:], V_ORDER[n], (xnT_hi, xnT_lo), wv, KD).then_inc(v_done.sem, 1)

            def score(g, j):
                pe.wait_ge(k_lo_done.sem, k_lo_done.value(g, 2 * j + 2))
                pe.wait_ge(qk_lo_done.sem, qk_lo_done.value(g, 3 * j + 3))
                pe.wait_ge(qk_read.sem, qk_read.value(g, CQ))
                for c in range(CQ // 2):
                    if j:
                        pe.wait_ge(shift_done.sem, shift_done.value(g, 4 * (j - 1) + c + 1))
                    product(nc, S[:, c, :], (q_hi[:, c, :], q_lo[:, c, :]), (k_hi[:, c, :], k_lo[:, c, :]), True, True)\
                        .then_inc(scored.sem, 1)

            def turn_probs(g, j):
                pe.wait_ge(xnT_lo_done.sem, xnT_lo_done.value(g, G if j == 0 else G + max(0, j - 1)))
                for q in range(4):
                    pe.wait_ge(exp_done.sem, exp_done.value(g, 4 * j + q + 1))
                    pe.wait_ge(probsT_read.sem, probsT_read.value(g, 4 * j + q - 1))
                    for t in range(4):
                        last = nc.tensor.transpose(turn[q % 2][:, t * P:(t + 1) * P], probs[:, 4 * q + t, :], ident[:])
                    last.then_inc(probs_turned.sem, 1)

            def mix(g, j):
                pe.wait_ge(probsT_read.sem, probsT_read.value(g, 4 * j + 4))
                pe.wait_ge(v_read.sem, v_read.value(g, G))
                pe.wait_ge(mix_steps.sem, mix_steps.value(g, 6 * j))
                for h in range(H):
                    last = nc.tensor.matmul(work[h // 8][:, (h % 8) * VW:(h % 8 + 1) * VW], probsT[:, h, :], v[:, j, h, :], start=True, stop=True)
                last.then_inc(mixed_done.sem, 1)

            def gate_logits(g):
                pe.wait_ge(mix_steps.sem, mix_steps.value(g, 6 * G))
                for k in range(KD):
                    last = product(nc, work[1][0:E, :], (wg[0][:, k, :], wg[1][:, k, :]), (xnT_hi[:, k, :], xnT_lo[:, k, :]), k == 0, k == KD - 1)
                last.then_inc(logitsT_done.sem, 1)

            def turn_logits(g):
                pe.wait_ge(logitsT_read.sem, logitsT_read.value(g, 1))
                pe.nop(nofuse=True)
                for j in range(G):
                    last = nc.tensor.transpose(work[0][:, j * E:(j + 1) * E], logitsT[:, tokens_of(j)], ident[0:E, 0:E])
                last.then_inc(logits_done.sem, 1)

            def rank_pairs(g):
                pe.wait_ge(route_steps.sem, route_steps.value(g, R_TAKEN))
                for j in range(G):
                    out = work[1][:, j * E:(j + 1) * E]
                    nc.tensor.matmul(out, before[:], taken[:, j, :], start=True, stop=False)
                    for i in range(j):
                        nc.tensor.matmul(out, ones[:], taken[:, i, :], start=False, stop=False)
                    last = nc.tensor.matmul(out, ones[:], counted[:], start=False, stop=True)
                last.then_inc(ranks_done.sem, 1)

            def shared_up(g, c):
                if c < 2:
                    pe.wait_ge(shift_done.sem, shift_done.value(g, 4 * G))
                else:
                    pe.wait_ge(h_steps.sem, h_steps.value(g, 2 * (c - 1)))
                for part in range(2):
                    cs = slice((part * CF + c) * P, (part * CF + c + 1) * P)
                    for k in range(KD):
                        last = product(nc, S[:, 2 * (c % 2) + part, :], (ws13[0][:, k, cs], ws13[1][:, k, cs]),
                                       (xnT_hi[:, k, :], xnT_lo[:, k, :]), k == 0, k == KD - 1)
                last.then_inc(up_done.sem, 1)

            def shared_down(g, j):
                pe.wait_ge(hT_lo_done.sem, hT_lo_done.value(g, CF))
                if j == 0:
                    pe.wait_ge(logits_steps.sem, logits_steps.value(g, 1))
                elif j == 1:
                    pe.wait_ge(route_steps.sem, route_steps.value(g, R_RANKED))
                else:
                    pe.wait_ge(acc_done.sem, acc_done.value(g, j - 1))
                from_tokens(work[j % 2][:], j, (hT_hi, hT_lo), ws2, CF).then_inc(down_done.sem, 1)

            def step(g, more):
                pe.wait_ge(xnT_lo_done.sem, xnT_lo_done.value(g, G))
                pe.wait_ge(w_lo, 3)
                for c in range(CQ):
                    project_qk(g, c)
                pe.wait_ge(w_lo, 4)
                project_v(g, 0)
                project_v(g, 1)
                score(g, 0)
                project_v(g, 2)
                project_v(g, 3)
                score(g, 1)
                turn_probs(g, 0)
                mix(g, 0)
                for j in range(1, G):
                    if j + 1 < G:
                        score(g, j + 1)
                    turn_probs(g, j)
                    mix(g, j)
                    turn_normed(g, G + j - 1)
                turn_normed(g, 2 * G - 1)
                pe.wait_ge(xnT_lo_done.sem, xnT_lo_done.value(g, 2 * G))
                pe.wait_ge(w_lo, NW + 1)
                gate_logits(g)
                shared_up(g, 0)
                turn_logits(g)
                shared_up(g, 1)
                rank_pairs(g)
                shared_up(g, 2)
                shared_up(g, 3)
                if more:
                    turn_normed(g + 1, 0)
                    turn_normed(g + 1, 1)
                shared_down(g, 0)
                if more:
                    turn_normed(g + 1, 2)
                shared_down(g, 1)
                if more:
                    turn_normed(g + 1, 3)
                shared_down(g, 2)
                shared_down(g, 3)

            pe.wait_ge(const_landed, 16 * 3)
            pe.wait_ge(setup, 1)
            for n in range(G):
                turn_normed(0, n)
            with pe.Fori(0, NG - 1) as i:
                step(i, True)
            step(NG - 1, False)


HE = 256
KH = HE // P


def experts(nc, normed, token_of_slot, W_expert, expert_count, pair_rank, pair_expert, gather_rows,
            ident_in, before_in, y_rows):
    TABLE = (TURNS + 1) * RING
    T = PAIRS // P
    W13 = KD * 2 * HE
    W2 = KH * D
    GROUP = 16
    with ExitStack() as stack:
        m = Memory(nc, stack, "ex")
        w_raw = m.sb("w_raw", [P, RING, W13 + W2])
        w13_hi = m.sb("w13_hi", [P, 2, KD, 2 * HE], F32R)
        w13_lo = m.sb("w13_lo", [P, 2, KD, 2 * HE], F32R)
        w2_hi = m.sb("w2_hi", [P, 2, KH, D], F32R)
        w2_lo = m.sb("w2_lo", [P, 2, KH, D], F32R)
        pair_token = m.sb("pair_token", [P, RING, T], I32)
        xg = m.sb("xg", [P, RING, T, D])
        xT_hi = m.sb("xT_hi", [P, 2, KD, PAIRS], F32R)
        xT_lo = m.sb("xT_lo", [P, 2, KD, PAIRS], F32R)
        gate = m.sb("gate", [P, 2, KH * PAIRS])
        hT = m.sb("hT", [P, 2, KH * PAIRS])
        hT_hi = m.sb("hT_hi", [P, 2, KH * PAIRS], F32R)
        hT_lo = m.sb("hT_lo", [P, 2, KH * PAIRS], F32R)
        y = m.sb("y", [P, RING, T, D])
        ident = m.sb("ident", [P, P])
        before = m.sb("before", [P, P])
        ones = m.sb("ones", [P, 1])
        thresholds = m.sb("thresholds", [E, CAP // PAIRS])
        over = m.sb("over", [E, CAP // PAIRS])
        count = m.sb("count", [E, 1])
        blocks = m.sb("blocks", [E, 1])
        first_block = m.sb("first_block", [E, 1])
        end_block = m.sb("end_block", [E, 1])
        expert_id = m.sb("expert_id", [E, 1])
        expert_row = m.sb("expert_row", [E, 1])
        first_row = m.sb("first_row", [E, 1])
        block_id = m.sb("block_id", [E, TABLE])
        block_row = m.sb("block_row", [E, TABLE])
        started = m.sb("started", [E, TABLE])
        parts = m.sb("parts", [E, 3 * TABLE + 1])
        row_part, expert_part, used_part = (parts[:, a * TABLE:(a + 1) * TABLE] for a in range(3))
        unused = m.sb("unused", [1, TABLE])
        blocks_wide = m.sb("blocks_wide", [E, P])
        first_of = m.sb("first_of", [P, E])
        iota_e = m.sb("iota_e", [P, E])
        one_hot = m.sb("one_hot", [P, GROUP, E])
        pair_first = m.sb("pair_first", [P, GROUP])
        table = m.sb("table", [1, 2 * TABLE + 1], I32)

        turn = [m.ps("turn0", [P, BANK]), m.ps("turn1", [P, BANK])]
        up = [[m.ps(f"up{s}{part}", [P, BANK]) for part in range(2)] for s in range(2)]
        down = [m.ps("down0", [P, BANK]), m.ps("down1", [P, BANK])]

        const_landed = m.sem("const_landed")
        setup = m.sem("setup")
        table_pe = m.sem("table_pe")
        table_steps = m.sem("table_steps")
        place_steps = m.sem("place_steps")
        weights_landed = [m.tally(f"weights_landed{u}", 16) for u in range(RING)]
        pairs_landed = [m.tally(f"pairs_landed{u}", 16) for u in range(RING)]
        gathered = [m.tally(f"gathered{u}", 16 * T) for u in range(RING)]
        stored = [m.tally(f"stored{u}", 16, 1) for u in range(RING)]
        turned = m.tally("turned", T, T * RING)
        xT_hi_done = m.tally("xT_hi_done", T)
        xT_lo_done = m.tally("xT_lo_done", T, T)
        w13_hi_done = m.tally("w13_hi_done", 1)
        w13_lo_done = m.tally("w13_lo_done", 1)
        w2_hi_done = m.tally("w2_hi_done", 1)
        w2_lo_done = m.tally("w2_lo_done", 1, RING)
        up_done = m.tally("up_done", 1, 2)
        gate_done = m.tally("gate_done", 1)
        h_steps = m.tally("h_steps", 2, 4)
        hT_hi_done = m.tally("hT_hi_done", 1)
        hT_lo_done = m.tally("hT_lo_done", 1)
        down_done = m.tally("down_done", T, 2 * T)
        y_done = m.tally("y_done", T, T)
        block = stack.enter_context(nc.Block())

        def loop(eng, step):
            used = eng.value_load(table[0:1, 2 * TABLE:2 * TABLE + 1], min_val=1, max_val=NBLOCKS)
            with eng.Fori(0, TURNS) as i:
                with eng.If(i * RING < used):
                    for u in range(RING):
                        step(i * RING + u, u, i)
            return used

        @block.sync
        def _(sp):
            grant(sp, *stored)
            sp.dma_start(ident[:], ident_in).then_inc(const_landed, 16)
            sp.dma_start(before[:], before_in).then_inc(const_landed, 16)
            sp.wait_ge(table_steps, 16)

            def fetch_pairs(j, u):
                row = sp.value_load(table[0:1, bass.ds(j, 1)], min_val=0, max_val=ROWS - PAIRS)
                sp.wait_ge(turned.sem, turned.value(j, T - T * RING))
                sp.nop(nofuse=True)
                sp.dma_start(pair_token[:, u, :], token_of_slot[bass.ds(row, PAIRS), :].rearrange("(p t) one -> p (t one)", t=T)
                             ).then_inc(pairs_landed[u].sem, 16)

            def fetch_weights(j, u):
                expert = sp.value_load(table[0:1, bass.ds(j + TABLE, 1)], min_val=0, max_val=E - 1)
                sp.wait_ge(w2_lo_done.sem, w2_lo_done.value(j, 1 - RING))
                sp.nop(nofuse=True)
                sp.dma_start(w_raw[:, u, :], W_expert[bass.ds(expert, 1)].rearrange("one p n -> p (one n)")).then_inc(weights_landed[u].sem, 16)

            def store(j, u):
                sp.wait_ge(y_done.sem, y_done.value(j, T))
                sp.nop(nofuse=True)
                sp.dma_start(y_rows[bass.ds(j * PAIRS, PAIRS), :].rearrange("(p t) d -> p t d", t=T), y[:, u]).then_inc(stored[u].sem, 16)

            fetch_pairs(0, 0)
            fetch_pairs(1, 1)
            fetch_weights(0, 0)
            for j in range(2, RING):
                fetch_pairs(j, j)
            for j in range(1, RING - 1):
                fetch_weights(j, j)

            def step(j, u, i):
                fetch_pairs(j + RING, u)
                fetch_weights(j + RING - 1, (u + RING - 1) % RING)
                store(j, u)

            used = loop(sp, step)
            turns = (used + (RING - 1)) // RING
            for u in range(RING):
                sp.wait_ge(stored[u].sem, stored[u].value(turns, 0))
                sp.nop(nofuse=True)
                sp.wait_ge(weights_landed[u].sem, weights_landed[u].value(turns, 16 if u < RING - 1 else 0))
                sp.nop(nofuse=True)
                sp.wait_ge(gathered[u].sem, gathered[u].value(turns, 16 * T))
                sp.nop(nofuse=True)

        @block.gpsimd
        def _(pool):
            nc.gpsimd.memset(ones[:], 1.0)
            nc.gpsimd.iota(thresholds[:], pattern=[[PAIRS, CAP // PAIRS]], base=0, channel_multiplier=0, allow_small_or_imprecise_dtypes=True)
            nc.gpsimd.iota(expert_id[:], pattern=[[0, 1]], base=0, channel_multiplier=1, allow_small_or_imprecise_dtypes=True)
            nc.gpsimd.iota(expert_row[:], pattern=[[0, 1]], base=0, channel_multiplier=CAP, allow_small_or_imprecise_dtypes=True)
            nc.gpsimd.iota(iota_e[:], pattern=[[1, E]], base=0, channel_multiplier=0, allow_small_or_imprecise_dtypes=True)
            nc.gpsimd.iota(block_id[:], pattern=[[1, TABLE]], base=0, channel_multiplier=0, allow_small_or_imprecise_dtypes=True)
            nc.gpsimd.iota(block_row[:], pattern=[[PAIRS, TABLE]], base=0, channel_multiplier=0, allow_small_or_imprecise_dtypes=True).then_inc(setup, 1)

            def gather(u, landed):
                pool.wait_ge(pairs_landed[u].sem, landed)
                pool.nop(nofuse=True)
                for t in range(T):
                    pool.indirect_dma_start(xg[:, u, t, :], None, normed, bass.IndirectOffsetOnAxis(ap=pair_token[:, u, t:t + 1], axis=0))\
                        .then_inc(gathered[u].sem, 16)

            for u in range(RING):
                gather(u, pairs_landed[u].value(0, 16))

            def step(j, u, i):
                pool.wait_ge(turned.sem, turned.value(j, T))
                gather(u, pairs_landed[u].value(i + 1, 16))

            pool.wait_ge(table_steps, 16)
            loop(pool, step)

        @block.scalar
        def _(act):
            grant(act, y_done)

            def high(out, src):
                return nc.scalar.activation(out, src, ACT.Copy)

            def x_high(j, s):
                act.wait_ge(up_done.sem, up_done.value(j, -1))
                for t in range(T):
                    act.wait_ge(turned.sem, turned.value(j, t + 1))
                    high(xT_hi[:, s, :, t * P:(t + 1) * P], turn[t][:].rearrange("p (k n) -> p k n", k=KD)).then_inc(xT_hi_done.sem, 1)

            def w13_high(j, s, u, i):
                act.wait_ge(weights_landed[u].sem, weights_landed[u].value(i, 16))
                act.wait_ge(up_done.sem, up_done.value(j, -1))
                high(w13_hi[:, s].rearrange("p k n -> p (k n)"), w_raw[:, u, 0:W13]).then_inc(w13_hi_done.sem, 1)

            def w2_high(j, s, u):
                act.wait_ge(down_done.sem, down_done.value(j, -T))
                high(w2_hi[:, s].rearrange("p k n -> p (k n)"), w_raw[:, u, W13:W13 + W2]).then_inc(w2_hi_done.sem, 1)

            def inner(j, s):
                act.wait_ge(up_done.sem, up_done.value(j, 1))
                act.wait_ge(h_steps.sem, h_steps.value(j, -2))
                nc.scalar.activation(gate[:, s, :], up[s][0][:], ACT.Tanh, scale=0.5).then_inc(gate_done.sem, 1)
                act.wait_ge(h_steps.sem, h_steps.value(j, 2))
                act.wait_ge(down_done.sem, down_done.value(j, -T))
                high(hT_hi[:, s, :], hT[:, s, :]).then_inc(hT_hi_done.sem, 1)

            def y_out(j, u, i):
                act.wait_ge(stored[u].sem, stored[u].value(i, 0))
                for t in range(T):
                    act.wait_ge(down_done.sem, down_done.value(j, t + 1))
                    nc.scalar.activation(y[:, u, t, :], down[t][:], ACT.Copy).then_inc(y_done.sem, 1)

            act.wait_ge(table_steps, 16)
            x_high(0, 0)
            w13_high(0, 0, 0, 0)
            x_high(1, 1)
            w2_high(0, 0, 0)
            w13_high(1, 1, 1, 0)
            inner(0, 0)

            def step(j, u, i):
                s, near, far = u % 2, (u + 1) % RING, (u + 2) % RING
                w2_high(j + 1, 1 - s, near)
                x_high(j + 2, s)
                w13_high(j + 2, s, far, i + (u + 2) // RING)
                inner(j + 1, 1 - s)
                y_out(j, u, i)

            loop(act, step)

        @block.vector
        def _(dve):
            V = nc.vector
            grant(dve, xT_lo_done, w2_lo_done, h_steps)
            dve.wait_ge(setup, 1)
            dve.wait_ge(table_pe, 1)
            V.tensor_copy(count[:], up[0][0][0:E, 0:1]).then_inc(table_steps, 1)
            dve.wait_ge(table_steps, 1)
            V.tensor_scalar(over[:], thresholds[:], count[:], None, ALU.is_lt).then_inc(table_steps, 1)
            dve.wait_ge(table_steps, 2)
            V.reduce_sum(blocks[:], over[:], AX.X).then_inc(table_steps, 1)
            dve.wait_ge(table_steps, 3)
            V.tensor_copy(blocks_wide[:], blocks[:].to_broadcast([E, P])).then_inc(table_steps, 1)
            dve.wait_ge(table_pe, 2)
            V.tensor_copy(first_block[:], up[1][0][0:E, 0:1]).then_inc(table_steps, 1)
            dve.wait_ge(table_steps, 5)
            V.tensor_tensor(end_block[:], first_block[:], blocks[:], ALU.add).then_inc(table_steps, 1)
            V.scalar_tensor_tensor(first_row[:], first_block[:], -float(PAIRS), expert_row[:], ALU.mult, ALU.add).then_inc(table_steps, 1)
            V.tensor_scalar(started[:], block_id[:], first_block[:], None, ALU.is_ge).then_inc(table_steps, 1)
            dve.wait_ge(table_steps, 8)
            V.scalar_tensor_tensor(used_part, block_id[:], end_block[:], started[:], ALU.is_lt, ALU.mult).then_inc(table_steps, 1)
            V.tensor_copy(parts[:, 3 * TABLE:3 * TABLE + 1], blocks[:]).then_inc(table_steps, 1)
            dve.wait_ge(table_steps, 10)
            V.scalar_tensor_tensor(row_part, block_row[:], first_row[:], used_part, ALU.add, ALU.mult).then_inc(table_steps, 1)
            V.tensor_scalar(expert_part, used_part, expert_id[:], None, ALU.mult).then_inc(table_steps, 1)
            dve.wait_ge(table_pe, 3)
            V.tensor_scalar(unused[:], up[0][0][0:1, 2 * TABLE:3 * TABLE], -float(NONE), float(NONE), ALU.mult, ALU.add).then_inc(table_steps, 1)
            dve.wait_ge(table_steps, 13)
            V.tensor_tensor(table[:, 0:TABLE], unused[:], up[0][0][0:1, 0:TABLE], ALU.add).then_inc(table_steps, 1)
            V.tensor_copy(table[:, TABLE:2 * TABLE], up[0][0][0:1, TABLE:2 * TABLE]).then_inc(table_steps, 1)
            V.tensor_copy(table[:, 2 * TABLE:2 * TABLE + 1], up[0][0][0:1, 3 * TABLE:3 * TABLE + 1]).then_inc(table_steps, 1)
            V.tensor_single_scalar(first_of[:], down[0][:, 0:E], float(PAIRS), ALU.mult).then_inc(place_steps, 1)

            def place(n):
                ps = slice(n * GROUP, (n + 1) * GROUP)
                dve.wait_ge(place_steps, 4 * n + 1)
                V.tensor_tensor(one_hot[:], iota_e[:].unsqueeze(1).to_broadcast([P, GROUP, E]),
                                pair_expert[:, ps].unsqueeze(2).to_broadcast([P, GROUP, E]), ALU.is_equal).then_inc(place_steps, 1)
                dve.wait_ge(place_steps, 4 * n + 2)
                V.tensor_tensor(one_hot[:], one_hot[:], first_of[:].unsqueeze(1).to_broadcast([P, GROUP, E]),
                                ALU.mult).then_inc(place_steps, 1)
                dve.wait_ge(place_steps, 4 * n + 3)
                V.reduce_sum(pair_first[:], one_hot[:], AX.X).then_inc(place_steps, 1)
                dve.wait_ge(place_steps, 4 * n + 4)
                V.tensor_tensor(gather_rows[:, ps], pair_first[:], pair_rank[:, ps], ALU.add).then_inc(place_steps, 1)

            def low(out, raw, hi):
                return V.tensor_tensor(out, raw, hi.bitcast(F32), ALU.subtract)

            def x_low(j, s):
                for t in range(T):
                    dve.wait_ge(xT_hi_done.sem, xT_hi_done.value(j, t + 1))
                    low(xT_lo[:, s, :, t * P:(t + 1) * P], turn[t][:].rearrange("p (k n) -> p k n", k=KD),
                        xT_hi[:, s, :, t * P:(t + 1) * P]).then_inc(xT_lo_done.sem, 1)

            def w13_low(j, s, u):
                dve.wait_ge(w13_hi_done.sem, w13_hi_done.value(j, 1))
                low(w13_lo[:, s].rearrange("p k n -> p (k n)"), w_raw[:, u, 0:W13],
                    w13_hi[:, s].rearrange("p k n -> p (k n)")).then_inc(w13_lo_done.sem, 1)

            def w2_low(j, s, u):
                dve.wait_ge(w2_hi_done.sem, w2_hi_done.value(j, 1))
                low(w2_lo[:, s].rearrange("p k n -> p (k n)"), w_raw[:, u, W13:W13 + W2],
                    w2_hi[:, s].rearrange("p k n -> p (k n)")).then_inc(w2_lo_done.sem, 1)

            def inner(j, s):
                dve.wait_ge(gate_done.sem, gate_done.value(j, 1))
                V.scalar_tensor_tensor(hT[:, s, :], gate[:, s, :], 1.0, up[s][0][:], ALU.add, ALU.mult).then_inc(h_steps.sem, 1)
                dve.wait_ge(h_steps.sem, h_steps.value(j, 1))
                V.scalar_tensor_tensor(hT[:, s, :], hT[:, s, :], 0.5, up[s][1][:], ALU.mult, ALU.mult).then_inc(h_steps.sem, 1)
                dve.wait_ge(hT_hi_done.sem, hT_hi_done.value(j, 1))
                low(hT_lo[:, s, :], hT[:, s, :], hT_hi[:, s, :]).then_inc(hT_lo_done.sem, 1)

            place(0)
            place(1)
            x_low(0, 0)
            w13_low(0, 0, 0)
            x_low(1, 1)
            w2_low(0, 0, 0)
            w13_low(1, 1, 1)
            place(2)
            inner(0, 0)
            for n in range(3, B * TOPK // GROUP):
                place(n)

            def step(j, u, i):
                s, near, far = u % 2, (u + 1) % RING, (u + 2) % RING
                w2_low(j + 1, 1 - s, near)
                x_low(j + 2, s)
                w13_low(j + 2, s, far)
                inner(j + 1, 1 - s)

            dve.wait_ge(table_steps, 16)
            loop(dve, step)

        @block.tensor
        def _(pe):
            grant(pe, turned, up_done, down_done)

            def turn_x(j, u, i):
                pe.wait_ge(gathered[u].sem, gathered[u].value(i, 16 * T))
                for t in range(T):
                    pe.wait_ge(xT_lo_done.sem, xT_lo_done.value(j, t + 1 - T))
                    for k in range(KD):
                        last = nc.tensor.transpose(turn[t][:, k * P:(k + 1) * P], xg[:, u, t, k * P:(k + 1) * P], ident[:])
                    last.then_inc(turned.sem, 1)

            def go_up(j, s):
                pe.wait_ge(xT_lo_done.sem, xT_lo_done.value(j, T))
                pe.wait_ge(w13_lo_done.sem, w13_lo_done.value(j, 1))
                pe.wait_ge(h_steps.sem, h_steps.value(j, -2))
                for part in range(2):
                    for c in range(KH):
                        cs = slice(part * HE + c * P, part * HE + (c + 1) * P)
                        for k in range(KD):
                            last = product(nc, up[s][part][:, c * PAIRS:(c + 1) * PAIRS], (w13_hi[:, s, k, cs], w13_lo[:, s, k, cs]),
                                           (xT_hi[:, s, k, :], xT_lo[:, s, k, :]), k == 0, k == KD - 1)
                last.then_inc(up_done.sem, 1)

            def go_down(j, s):
                pe.wait_ge(hT_lo_done.sem, hT_lo_done.value(j, 1))
                pe.wait_ge(w2_lo_done.sem, w2_lo_done.value(j, 1))
                for t in range(T):
                    pe.wait_ge(y_done.sem, y_done.value(j, t + 1 - T))
                    for k in range(KH):
                        ts = slice(k * PAIRS + t * P, k * PAIRS + (t + 1) * P)
                        last = product(nc, down[t][:], (hT_hi[:, s, ts], hT_lo[:, s, ts]), (w2_hi[:, s, k, :], w2_lo[:, s, k, :]), k == 0, k == KH - 1)
                    last.then_inc(down_done.sem, 1)

            pe.wait_ge(const_landed, 32)
            pe.wait_ge(setup, 1)
            nc.tensor.matmul(up[0][0][0:E, 0:1], expert_count[:], ones[:], start=True, stop=True).then_inc(table_pe, 1)
            pe.wait_ge(table_steps, 4)
            nc.tensor.matmul(down[0][:, 0:E], blocks_wide[:], before[0:E, 0:E], start=True, stop=True)
            nc.tensor.matmul(up[1][0][0:E, 0:1], before[0:E, 0:E], blocks[:], start=True, stop=True).then_inc(table_pe, 1)
            pe.wait_ge(table_steps, 12)
            nc.tensor.matmul(up[0][0][0:1, 0:3 * TABLE + 1], ones[0:E, :], parts[:], start=True, stop=True).then_inc(table_pe, 1)
            pe.wait_ge(table_steps, 16)
            pe.wait_ge(place_steps, 1)
            turn_x(0, 0, 0)
            turn_x(1, 1, 0)
            go_up(0, 0)

            def step(j, u, i):
                s, far = u % 2, (u + 2) % RING
                turn_x(j + 2, far, i + (u + 2) // RING)
                go_up(j + 1, 1 - s)
                go_down(j, s)

            loop(pe, step)


def combine(nc, acc_in, y_rows, gather_rows, pair_weight, out):
    SLOTS = 4
    with ExitStack() as stack:
        m = Memory(nc, stack, "co")
        acc = m.sb("acc", [P, SLOTS, D])
        rows = m.sb("rows", [P, SLOTS, TOPK], I32)
        weight = m.sb("weight", [P, SLOTS, TOPK])
        y = m.sb("y", [P, SLOTS, TOPK, D])
        acc_landed = [m.tally(f"acc_landed{s}", 16) for s in range(SLOTS)]
        y_landed = [m.tally(f"y_landed{s}", 16 * TOPK) for s in range(SLOTS)]
        rows_done = m.tally("rows_done", 2)
        sum_steps = m.tally("sum_steps", TOPK)
        stored = [m.tally(f"stored{s}", 16) for s in range(SLOTS)]
        block = stack.enter_context(nc.Block())

        @block.sync
        def _(sp):
            for s in range(SLOTS):
                sp.dma_start(acc[:, s, :], acc_in[s]).then_inc(acc_landed[s].sem, 16)

            def step(b, s, i, more):
                sp.wait_ge(sum_steps.sem, sum_steps.value(b, TOPK))
                sp.nop(nofuse=True)
                sp.dma_start(out[b], acc[:, s, :]).then_inc(stored[s].sem, 16)
                if more:
                    sp.wait_ge(stored[s].sem, stored[s].value(i, 16))
                    sp.nop(nofuse=True)
                    sp.dma_start(acc[:, s, :], acc_in[b + SLOTS]).then_inc(acc_landed[s].sem, 16)

            with sp.Fori(0, B // SLOTS - 1) as i:
                for s in range(SLOTS):
                    step(i * SLOTS + s, s, i, True)
            for s in range(SLOTS):
                step(B - SLOTS + s, s, B // SLOTS - 1, False)
            for s in range(SLOTS):
                sp.wait_ge(stored[s].sem, stored[s].value(B // SLOTS - 1, 16))
                sp.nop(nofuse=True)

        @block.gpsimd
        def _(pool):
            with pool.Fori(0, B // SLOTS) as i:
                for s in range(SLOTS):
                    pool.wait_ge(rows_done.sem, rows_done.value(i * SLOTS + s, 1))
                    pool.nop(nofuse=True)
                    for k in range(TOPK):
                        pool.indirect_dma_start(y[:, s, k, :], None, y_rows, bass.IndirectOffsetOnAxis(ap=rows[:, s, k:k + 1], axis=0))\
                            .then_inc(y_landed[s].sem, 16)

        @block.vector
        def _(dve):
            V = nc.vector

            def numbers(b, s):
                V.tensor_copy(rows[:, s, :], gather_rows[:, bass.ds(b * TOPK, TOPK)]).then_inc(rows_done.sem, 1)
                V.tensor_copy(weight[:, s, :], pair_weight[:, bass.ds(b * TOPK, TOPK)]).then_inc(rows_done.sem, 1)

            for s in range(SLOTS):
                numbers(s, s)

            def step(b, s, i, more):
                dve.wait_ge(acc_landed[s].sem, acc_landed[s].value(i, 16))
                dve.wait_ge(rows_done.sem, rows_done.value(b, 2))
                dve.wait_ge(y_landed[s].sem, y_landed[s].value(i, 16 * TOPK))
                for k in range(TOPK):
                    if k:
                        dve.wait_ge(sum_steps.sem, sum_steps.value(b, k))
                    V.scalar_tensor_tensor(acc[:, s, :], y[:, s, k, :], weight[:, s, k:k + 1], acc[:, s, :], ALU.mult, ALU.add)\
                        .then_inc(sum_steps.sem, 1)
                if more:
                    dve.wait_ge(sum_steps.sem, sum_steps.value(b, TOPK))
                    numbers(b + SLOTS, s)

            with dve.Fori(0, B // SLOTS - 1) as i:
                for s in range(SLOTS):
                    step(i * SLOTS + s, s, i, True)
            for s in range(SLOTS):
                step(B - SLOTS + s, s, B // SLOTS - 1, False)


def build(nc, x, ctx_rows, ctx_cols, w_cq, w_c, w_q, b_cq, b_c, b_q, W_lT, b_l, W_qkT, W_vT, W_g, W_s13, W_s2, W_expert,
          ident, before, out):
    x1 = nc.dram_tensor("x1_rows", (B, P, D), F32).ap()
    normed = nc.dram_tensor("normed_rows", (B, P, D), F32).ap()
    acc = nc.dram_tensor("acc_rows", (B, P, D), F32).ap()
    token_of_slot = nc.dram_tensor("token_of_slot", (ROWS, 1), I32).ap()
    y_rows = nc.dram_tensor("y_rows", (TURNS * RING * PAIRS, D), F32).ap()
    cross_attention(nc, x, ctx_rows, ctx_cols, w_cq, w_c, w_q, b_cq, b_c, b_q, W_lT, b_l, ident, x1)
    with ExitStack() as stack:
        def kept(name, shape, dt):
            return stack.enter_context(nc.sbuf_tensor(name, shape, dt))

        pair_rank = kept("pair_rank", [P, B * TOPK], F32)
        pair_expert = kept("pair_expert", [P, B * TOPK], F32)
        pair_weight = kept("pair_weight", [P, B * TOPK], F32)
        gather_rows = kept("gather_rows", [P, B * TOPK], I32)
        expert_count = kept("expert_count", [P, E], F32)
        self_attention_and_routing(nc, x1, W_qkT, W_vT, W_g, W_s13, W_s2, ident, before, normed, acc,
                                   token_of_slot, y_rows, pair_rank, pair_expert, pair_weight, expert_count)
        experts(nc, normed.rearrange("b p d -> (b p) d"), token_of_slot, W_expert, expert_count, pair_rank, pair_expert,
                gather_rows, ident, before, y_rows)
        combine(nc, acc, y_rows, gather_rows, pair_weight, out)


def kernel(x, ctx_1024, L0_xattn_w_cq, L0_xattn_b_cq, L0_xattn_w_c, L0_xattn_b_c, L0_xattn_w_q, L0_xattn_b_q,
           L0_xattn_W_l, L0_xattn_b_l, L0_attn_Wq, L0_attn_Wk, L0_attn_Wv, L0_ffn_Wg, L0_ffn_W1, L0_ffn_W2, L0_ffn_W3,
           L0_ffn_Ws1, L0_ffn_Ws2, L0_ffn_Ws3):
    import numpy as np
    import concourse.bacc as bacc
    from concourse.bass_utils import run_bass_kernel_spmd

    def blocks(w):
        w = np.asarray(w)
        return np.ascontiguousarray(w.reshape(-1, P, w.shape[1]).transpose(1, 0, 2))

    def expert_blocks(w):
        w = np.asarray(w)
        return w.reshape(E, -1, P, w.shape[2]).transpose(0, 2, 1, 3)

    ctx = np.asarray(ctx_1024)
    w13 = np.concatenate([expert_blocks(L0_ffn_W1), expert_blocks(L0_ffn_W3)], axis=3)
    arrays = {
        "x": np.asarray(x),
        "ctx_rows": np.ascontiguousarray(ctx).reshape(B, 8, P, CTX // 8 // P * D),
        "ctx_cols": np.ascontiguousarray(ctx.reshape(B, CTX // BANK, BANK, KD, P).transpose(0, 1, 4, 3, 2)).reshape(B, CTX // BANK, P, KD * BANK),
        "w_cq": np.ascontiguousarray(np.asarray(L0_xattn_w_cq).reshape(KD, P).T),
        "w_c": np.asarray(L0_xattn_w_c),
        "w_q": np.ascontiguousarray(np.asarray(L0_xattn_w_q).reshape(KD, P).T),
        "b_cq": np.asarray(L0_xattn_b_cq).reshape(1),
        "b_c": np.asarray(L0_xattn_b_c).reshape(1),
        "b_q": np.asarray(L0_xattn_b_q).reshape(1),
        "W_lT": blocks(np.asarray(L0_xattn_W_l).T),
        "b_l": np.asarray(L0_xattn_b_l),
        "W_qkT": blocks(np.concatenate([np.asarray(L0_attn_Wq).T, np.asarray(L0_attn_Wk).T], axis=1)),
        "W_vT": blocks(np.asarray(L0_attn_Wv).T),
        "W_g": blocks(L0_ffn_Wg),
        "W_s13": blocks(np.concatenate([np.asarray(L0_ffn_Ws1), np.asarray(L0_ffn_Ws3)], axis=1)),
        "W_s2": blocks(L0_ffn_Ws2),
        "W_expert": np.concatenate([w13.reshape(E, P, -1), expert_blocks(L0_ffn_W2).reshape(E, P, -1)], axis=2),
        "ident": np.eye(P, dtype=np.float32),
        "before": np.triu(np.ones((P, P), np.float32), 1),
    }
    nc = bacc.Bacc("TRN2", target_bir_lowering=False, num_devices=1)
    ins = [nc.dram_tensor(name, a.shape, F32, kind="ExternalInput").ap() for name, a in arrays.items()]
    out = nc.dram_tensor("out", (B, P, D), F32, kind="ExternalOutput").ap()
    build(nc, *ins, out)
    return run_bass_kernel_spmd(nc, [arrays], core_ids=[0]).results[0]["out"]
```
